# Optimizing a Trainium2 kernel written in Bass

```python
import numpy as np
import jax
import jax.numpy as jnp

def _softmax(x, axis=-1):
    return jax.nn.softmax(x, axis=axis)

def _gelu(x):
    return jax.nn.gelu(x, approximate=True)

def _silu(x):
    return jax.nn.silu(x)

def _sigmoid(x):
    return jax.nn.sigmoid(x)

def _layernorm(x, axis=-1, eps=1e-05):
    m = jnp.mean(x, axis=axis, keepdims=True)
    v = jnp.var(x, axis=axis, keepdims=True)
    return (x - m) / jnp.sqrt(v + eps)

def _scatter_add(tgt, idx, src, axis=0):
    return tgt.at[idx].add(src)

def _segment_sum(src, seg, n):
    return jax.ops.segment_sum(src, seg, n)
kernel_name = 'mk_sandwich_d2_jaxref_r8_0dda1b'

def setup_inputs(seed: int=0):
    np.random.seed(seed)
    _w = jnp.asarray

    def _L0_attn_setup():
        import jax, jax.numpy as jnp
        import numpy as np
        B, N, E, H, DEPTH = (2, 256, 128, 8, 12)
        D = E // H // 2
        LN_EPS = 1e-05
        key = jax.random.key(seed)
        ks = jax.random.split(key, 10)
        w = lambda k: jax.random.normal(k, (E, E), jnp.float32) * E ** (-0.5)
        lp = lambda k: jax.random.normal(k, (D,), jnp.float32) * 0.1
        return {'x': jax.random.normal(ks[0], (B, N, E), jnp.float32), 'Wq': w(ks[1]), 'Wk': w(ks[2]), 'Wv': w(ks[3]), 'Wo': w(ks[4]), 'lq1': lp(ks[5]), 'lk1': lp(ks[6]), 'lq2': lp(ks[7]), 'lk2': lp(ks[8]), 'ln_g': jnp.ones((2 * D,), jnp.float32), 'ln_b': jnp.zeros((2 * D,), jnp.float32)}
    _L0_attn_in = _L0_attn_setup()

    def _L0_ffn_setup():
        import jax, jax.numpy as jnp
        import numpy as np
        EPS = 1e-08

        def _ternary_linear(x, w):
            alpha = jnp.mean(jnp.abs(w))
            w_t = jnp.sign(w) * (jnp.abs(w) > 0.5 * alpha).astype(w.dtype)
            w_q = w + jax.lax.stop_gradient(w_t - w)
            d = x.shape[-1]
            rms = jnp.sqrt(jnp.sum(x * x, axis=-1, keepdims=True)) / jnp.sqrt(jnp.asarray(d, x.dtype))
            x_norm = x / (rms + EPS)
            return jnp.einsum('bsd,fd->bsf', x_norm, w_q)
        key = jax.random.key(seed)
        k1, k2, k3 = jax.random.split(key, 3)
        d_model, d_ff = (128, 512)
        B, S = (4, 512)
        x = jax.random.normal(k1, (B, S, d_model), dtype=jnp.float32)
        w_up = jax.random.normal(k2, (d_ff, d_model), dtype=jnp.float32) * 0.02
        w_down = jax.random.normal(k3, (d_model, d_ff), dtype=jnp.float32) * 0.02
        return {'x': x, 'w_up': w_up, 'w_down': w_down}
    _L0_ffn_in = _L0_ffn_setup()

    def _L1_attn_setup():
        import jax, jax.numpy as jnp
        import numpy as np
        H = 128
        I = 512
        TAU = 9
        LN_EPS = 1e-12

        def _l2_normalize(x):
            n = jnp.sqrt(jnp.sum(x * x, axis=-1, keepdims=True))
            return x / jnp.maximum(n, 1e-12)
        key = jax.random.key(seed)
        k1, k2, k3, k4 = jax.random.split(key, 4)
        return {'hidden_states': jax.random.normal(k1, (4, 256, H), jnp.float32), 'ln_weight': jnp.ones((H,), jnp.float32), 'ln_bias': jnp.zeros((H,), jnp.float32), 'k_weight': 0.02 * jax.random.normal(k2, (I, H), jnp.float32), 'q_weight': 0.02 * jax.random.normal(k3, (I, H), jnp.float32), 'bias': 0.001 * jax.random.normal(k4, (H,), jnp.float32)}
    _L1_attn_in = _L1_attn_setup()

    def _L1_ffn_setup():
        import jax, jax.numpy as jnp
        import numpy as np
        N_EXPERTS = 32
        TOP_K = 8
        N_GROUP = 4
        TOPK_GROUP = 2
        ROUTED_SCALING = 2.5

        def _gate(x, gate_w, gate_bias):
            T, E = (x.shape[0], gate_w.shape[0])
            logits = jnp.einsum('th,eh->te', x, gate_w)
            scores = jax.nn.sigmoid(logits)
            scores_choice = scores + gate_bias[None, :]
            grp = scores_choice.reshape(T, N_GROUP, E // N_GROUP)
            top2, _ = jax.lax.top_k(grp, 2)
            group_scores = top2.sum(-1)
            _, grp_idx = jax.lax.top_k(group_scores, TOPK_GROUP)
            group_mask = jax.nn.one_hot(grp_idx, N_GROUP, dtype=scores.dtype).sum(1)
            expert_mask = jnp.repeat(group_mask, E // N_GROUP, axis=1)
            masked = jnp.where(expert_mask > 0, scores_choice, 0.0)
            _, topk_idx = jax.lax.top_k(masked, TOP_K)
            topk_w = jnp.take_along_axis(scores, topk_idx, axis=1)
            topk_w = topk_w / (topk_w.sum(-1, keepdims=True) + 1e-20)
            topk_w = topk_w * ROUTED_SCALING
            return (topk_idx, topk_w)

        def _mlp(x, wg, wu, wd):
            return jnp.einsum('...i,hi->...h', jax.nn.silu(jnp.einsum('...h,ih->...i', x, wg)) * jnp.einsum('...h,ih->...i', x, wu), wd)
        key = jax.random.key(seed)
        ks = jax.random.split(key, 9)
        B, S, H, I = (2, 64, 128, 64)
        w = 0.02
        return {'hidden_states': jax.random.normal(ks[0], (B, S, H), jnp.float32), 'gate_w': jax.random.normal(ks[1], (N_EXPERTS, H), jnp.float32) * w, 'gate_bias': jax.random.normal(ks[2], (N_EXPERTS,), jnp.float32) * w, 'expert_gate': jax.random.normal(ks[3], (N_EXPERTS, I, H), jnp.float32) * w, 'expert_up': jax.random.normal(ks[4], (N_EXPERTS, I, H), jnp.float32) * w, 'expert_down': jax.random.normal(ks[5], (N_EXPERTS, H, I), jnp.float32) * w, 'shared_gate': jax.random.normal(ks[6], (2 * I, H), jnp.float32) * w, 'shared_up': jax.random.normal(ks[7], (2 * I, H), jnp.float32) * w, 'shared_down': jax.random.normal(ks[8], (H, 2 * I), jnp.float32) * w}
    _L1_ffn_in = _L1_ffn_setup()
    _d = {'L0_attn_x': _L0_attn_in['x'], 'L0_attn_Wq': _L0_attn_in['Wq'], 'L0_attn_Wk': _L0_attn_in['Wk'], 'L0_attn_Wv': _L0_attn_in['Wv'], 'L0_attn_Wo': _L0_attn_in['Wo'], 'L0_attn_lq1': _L0_attn_in['lq1'], 'L0_attn_lk1': _L0_attn_in['lk1'], 'L0_attn_lq2': _L0_attn_in['lq2'], 'L0_attn_lk2': _L0_attn_in['lk2'], 'L0_attn_ln_g': _L0_attn_in['ln_g'], 'L0_attn_ln_b': _L0_attn_in['ln_b'], 'L0_ffn_w_up': _L0_ffn_in['w_up'], 'L0_ffn_w_down': _L0_ffn_in['w_down'], 'L1_attn_ln_weight': _L1_attn_in['ln_weight'], 'L1_attn_ln_bias': _L1_attn_in['ln_bias'], 'L1_attn_k_weight': _L1_attn_in['k_weight'], 'L1_attn_q_weight': _L1_attn_in['q_weight'], 'L1_attn_bias': _L1_attn_in['bias'], 'L1_ffn_gate_w': _L1_ffn_in['gate_w'], 'L1_ffn_gate_bias': _L1_ffn_in['gate_bias'], 'L1_ffn_expert_gate': _L1_ffn_in['expert_gate'], 'L1_ffn_expert_up': _L1_ffn_in['expert_up'], 'L1_ffn_expert_down': _L1_ffn_in['expert_down'], 'L1_ffn_shared_gate': _L1_ffn_in['shared_gate'], 'L1_ffn_shared_up': _L1_ffn_in['shared_up'], 'L1_ffn_shared_down': _L1_ffn_in['shared_down']}
    _x0 = _d['L0_attn_x']
    _d['L0_attn_x'] = jax.random.normal(jax.random.fold_in(jax.random.key(seed), 1), (2, 2048, 128), dtype=_x0.dtype)
    del _x0
    return _d

def reference(L0_attn_x, L0_attn_Wq, L0_attn_Wk, L0_attn_Wv, L0_attn_Wo, L0_attn_lq1, L0_attn_lk1, L0_attn_lq2, L0_attn_lk2, L0_attn_ln_g, L0_attn_ln_b, L0_ffn_w_up, L0_ffn_w_down, L1_attn_ln_weight, L1_attn_ln_bias, L1_attn_k_weight, L1_attn_q_weight, L1_attn_bias, L1_ffn_gate_w, L1_ffn_gate_bias, L1_ffn_expert_gate, L1_ffn_expert_up, L1_ffn_expert_down, L1_ffn_shared_gate, L1_ffn_shared_up, L1_ffn_shared_down):

    def _L0_attn_ref(x, Wq, Wk, Wv, Wo, lq1, lk1, lq2, lk2, ln_g, ln_b):
        import jax, jax.numpy as jnp
        import numpy as np
        B, N, E, H, DEPTH = (2, 256, 128, 8, 12)
        D = E // H // 2
        LN_EPS = 1e-05
        b, n, e = x.shape
        lam_init = 0.8 - 0.6 * np.exp(-0.3 * DEPTH)
        q = (x @ Wq).reshape(b, n, 2 * H, D).transpose(0, 2, 1, 3) * D ** (-0.5)
        k = (x @ Wk).reshape(b, n, 2 * H, D).transpose(0, 2, 1, 3)
        v = (x @ Wv).reshape(b, n, H, 2 * D).transpose(0, 2, 1, 3)
        scores = jnp.einsum('bhqd,bhkd->bhqk', q, k)
        attn = jax.nn.softmax(scores, axis=-1).reshape(b, H, 2, n, n)
        lam = jnp.exp(jnp.sum(lq1 * lk1)) - jnp.exp(jnp.sum(lq2 * lk2)) + lam_init
        w_diff = attn[:, :, 0] - lam * attn[:, :, 1]
        o = jnp.einsum('bhqk,bhkd->bhqd', w_diff, v)
        mu = o.mean(-1, keepdims=True)
        var = ((o - mu) ** 2).mean(-1, keepdims=True)
        o = (o - mu) * jax.lax.rsqrt(var + LN_EPS) * ln_g + ln_b
        o = o.transpose(0, 2, 1, 3).reshape(b, n, e)
        return o @ Wo

    def _L0_ffn_ref(x, w_up, w_down):
        import jax, jax.numpy as jnp
        import numpy as np
        EPS = 1e-08

        def _ternary_linear(x, w):
            alpha = jnp.mean(jnp.abs(w))
            w_t = jnp.sign(w) * (jnp.abs(w) > 0.5 * alpha).astype(w.dtype)
            w_q = w + jax.lax.stop_gradient(w_t - w)
            d = x.shape[-1]
            rms = jnp.sqrt(jnp.sum(x * x, axis=-1, keepdims=True)) / jnp.sqrt(jnp.asarray(d, x.dtype))
            x_norm = x / (rms + EPS)
            return jnp.einsum('bsd,fd->bsf', x_norm, w_q)
        h = jax.nn.gelu(_ternary_linear(x, w_up), approximate=False)
        return _ternary_linear(h, w_down)

    def _L1_attn_ref(hidden_states, ln_weight, ln_bias, k_weight, q_weight, bias):
        import jax, jax.numpy as jnp
        import numpy as np
        H = 128
        I = 512
        TAU = 9
        LN_EPS = 1e-12

        def _l2_normalize(x):
            n = jnp.sqrt(jnp.sum(x * x, axis=-1, keepdims=True))
            return x / jnp.maximum(n, 1e-12)
        lead_shape = hidden_states.shape[:-1]
        x = hidden_states.reshape(-1, H)
        mu = jnp.mean(x, axis=-1, keepdims=True)
        var = jnp.mean(jnp.square(x - mu), axis=-1, keepdims=True)
        x = (x - mu) * jax.lax.rsqrt(var + LN_EPS) * ln_weight + ln_bias
        Q = _l2_normalize(x)
        K = _l2_normalize(k_weight)
        s = jnp.clip(jnp.einsum('nh,ih->ni', Q, K), -1.0 + 1e-06, 1.0 - 1e-06)
        B = jnp.power(1.0 - jnp.arccos(s) / jnp.pi, TAU)
        X = jnp.einsum('ni,ih->nh', B, q_weight)
        X = _l2_normalize(X) + bias
        return X.reshape(*lead_shape, H)

    def _L1_ffn_ref(hidden_states, gate_w, gate_bias, expert_gate, expert_up, expert_down, shared_gate, shared_up, shared_down):
        import jax, jax.numpy as jnp
        import numpy as np
        N_EXPERTS = 32
        TOP_K = 8
        N_GROUP = 4
        TOPK_GROUP = 2
        ROUTED_SCALING = 2.5

        def _gate(x, gate_w, gate_bias):
            T, E = (x.shape[0], gate_w.shape[0])
            logits = jnp.einsum('th,eh->te', x, gate_w)
            scores = jax.nn.sigmoid(logits)
            scores_choice = scores + gate_bias[None, :]
            grp = scores_choice.reshape(T, N_GROUP, E // N_GROUP)
            top2, _ = jax.lax.top_k(grp, 2)
            group_scores = top2.sum(-1)
            _, grp_idx = jax.lax.top_k(group_scores, TOPK_GROUP)
            group_mask = jax.nn.one_hot(grp_idx, N_GROUP, dtype=scores.dtype).sum(1)
            expert_mask = jnp.repeat(group_mask, E // N_GROUP, axis=1)
            masked = jnp.where(expert_mask > 0, scores_choice, 0.0)
            _, topk_idx = jax.lax.top_k(masked, TOP_K)
            topk_w = jnp.take_along_axis(scores, topk_idx, axis=1)
            topk_w = topk_w / (topk_w.sum(-1, keepdims=True) + 1e-20)
            topk_w = topk_w * ROUTED_SCALING
            return (topk_idx, topk_w)

        def _mlp(x, wg, wu, wd):
            return jnp.einsum('...i,hi->...h', jax.nn.silu(jnp.einsum('...h,ih->...i', x, wg)) * jnp.einsum('...h,ih->...i', x, wu), wd)
        orig_shape = hidden_states.shape
        H = orig_shape[-1]
        residuals = hidden_states
        x = hidden_states.reshape(-1, H)
        topk_idx, topk_w = _gate(x, gate_w, gate_bias)
        g = jnp.einsum('th,eih->eti', x, expert_gate)
        u = jnp.einsum('th,eih->eti', x, expert_up)
        outs = jnp.einsum('eti,ehi->eth', jax.nn.silu(g) * u, expert_down)
        outs_t = jnp.transpose(outs, (1, 0, 2))
        gathered = jnp.take_along_axis(outs_t, topk_idx[:, :, None], axis=1)
        final = (gathered * topk_w[:, :, None]).sum(1)
        shared = _mlp(residuals, shared_gate, shared_up, shared_down)
        return final.reshape(orig_shape) + shared
    x = L0_attn_x
    x = x + _layernorm(_L0_attn_ref(_layernorm(x, axis=-1), L0_attn_Wq, L0_attn_Wk, L0_attn_Wv, L0_attn_Wo, L0_attn_lq1, L0_attn_lk1, L0_attn_lq2, L0_attn_lk2, L0_attn_ln_g, L0_attn_ln_b), axis=-1)
    x = x + _layernorm(_L0_ffn_ref(_layernorm(x, axis=-1), L0_ffn_w_up, L0_ffn_w_down), axis=-1)
    x = x + _layernorm(_L1_attn_ref(_layernorm(x, axis=-1), L1_attn_ln_weight, L1_attn_ln_bias, L1_attn_k_weight, L1_attn_q_weight, L1_attn_bias), axis=-1)
    x = x + _layernorm(_L1_ffn_ref(_layernorm(x, axis=-1), L1_ffn_gate_w, L1_ffn_gate_bias, L1_ffn_expert_gate, L1_ffn_expert_up, L1_ffn_expert_down, L1_ffn_shared_gate, L1_ffn_shared_up, L1_ffn_shared_down), axis=-1)
    return x

_drawn_inputs = setup_inputs


def setup_inputs(seed=0):
    import zlib

    import numpy as np

    out = dict(_drawn_inputs(seed))
    spreads = {'L0_attn_ln_g': (1.0, 0.2),
     'L0_attn_ln_b': (0.0, 0.1),
     'L1_attn_ln_weight': (1.0, 0.2),
     'L1_attn_ln_bias': (0.0, 0.1)}
    factors = {'L0_attn_lq1': 3.121, 'L1_attn_bias': 2.965}
    for name, (base, spread) in spreads.items():
        noise = np.random.default_rng([zlib.crc32(name.encode()), seed]).standard_normal(out[name].shape)
        drawn = base * np.exp(spread * noise) if base else spread * noise
        out[name] = jnp.asarray(drawn.astype(out[name].dtype))
    for name, factor in factors.items():
        out[name] = (out[name] * factor).astype(out[name].dtype)
    return out
```

```python
import concourse.bass as bass
from concourse import mybir
from contextlib import ExitStack

F32 = mybir.dt.float32
BF16 = mybir.dt.bfloat16
I32 = mybir.dt.int32
ALU = mybir.AluOpType
ACT = mybir.ActivationFunctionType
AX = mybir.AxisListType
RMAX = bass.bass_isa.ReduceOp.max
RADD = bass.bass_isa.ReduceOp.add

P = 128
B = 2
N = 2048
NT = B * N // P
TB = NT // B
H = 8
S2 = 16
D = 8
DV = 16
ROW = 64
NSPLIT = 6
SH = NSPLIT * D
VC = 64
NQC = 4
KT = 16
RING = 4
SAFE = 40.0
LAM_INIT = 0.8 - 0.6 * 2.718281828459045 ** (-0.3 * 12)


class Chain:

    def __init__(self, eng, sem, base=0):
        self.eng, self.sem, self.base, self.n = eng, sem, base, 0

    def __call__(self, ins):
        self.n += 1
        ins.then_inc(self.sem, 1)
        self.eng.wait_ge(self.sem, self.base + self.n)


class Semaphores:

    def __init__(self, nc):
        self.nc = nc

    def __enter__(self):
        self.handles = []
        return self

    def __call__(self, name):
        self.handles.append(self.nc.alloc_semaphore(name=name))
        return self.handles[-1]

    def __exit__(self, *_):
        with self.nc.Block() as block:
            @block.gpsimd
            def _(pool):
                for handle in self.handles:
                    pool.sem_clear(handle)
        for handle in self.handles:
            self.nc.release_semaphore(handle)


def pipelined(eng, front, back, n, base):
    half = n // 2
    front(0, 0, base)
    with eng.Fori(0, half - 1) as k:
        front(2 * k + 1, 1, base + k)
        back(2 * k, 0, base + k)
        front(2 * k + 2, 0, base + k + 1)
        back(2 * k + 1, 1, base + k)
    front(n - 1, 1, base + half - 1)
    back(n - 2, 0, base + half - 1)
    back(n - 1, 1, base + half - 1)


def mean_rstd(dve, pool_pow, ch, st, mean, var, tmp):
    ch(dve.tensor_tensor(mean, st[:, :, 1], st[:, :, 4], ALU.add))
    ch(dve.tensor_scalar(mean, mean, 0.5, None, ALU.mult))
    ch(dve.tensor_tensor(tmp, st[:, :, 1], mean, ALU.subtract))
    ch(dve.tensor_tensor(tmp, tmp, tmp, ALU.mult))
    ch(dve.tensor_tensor(var, st[:, :, 2], st[:, :, 5], ALU.add))
    ch(dve.tensor_scalar(var, var, 1.0 / P, None, ALU.mult))
    ch(dve.tensor_tensor(var, var, tmp, ALU.add))


def attention_layer(nc, a, sb, pb, sem, xs, o_all, ident, identb, DEBUG=None):
    with ExitStack() as ctx:
        def sbt(name, shape, dt):
            return ctx.enter_context(nc.sbuf_tensor(name, shape, dt))

        xn = sbt("xn", [P, NT, P], F32)
        wqkv = sbt("wqkv_sb", [P, 3 * P], F32)
        sel = sbt("sel_sb", [P, DV + 1], F32)
        lqk = sbt("lqk_sb", [P, 4, D], F32)
        lam = sbt("lam", [P, 1], F32)
        lam4 = sbt("lam4", [P, 6], F32)
        st = sbt("st", [P, NT, 6], F32)
        mean = sbt("mean", [P, NT], F32)
        var = sbt("var", [P, NT], F32)
        vtmp = sbt("vtmp", [P, NT], F32)
        mhalf = sbt("mhalf", [P, NT], F32)
        rstd = sbt("rstd", [P, NT], F32)
        xslot = sbt("xslot", [P, 2, P], F32)
        xnT = sbt("xnT", [P, 2, P], F32)
        qkv = sbt("qkv", [P, 2, 3 * P], F32)
        rest = sbt("rest", [P, 2, 3 * P], F32)
        parts = sbt("parts", [P, 2, 3, 3 * P], BF16)
        q_rows = sbt("q_rows", [P, 2, S2, ROW], BF16)
        k_rows = sbt("k_rows", [P, 2, S2, ROW], BF16)
        sq = sbt("sq", [P, 2, 2 * P], F32)
        norms = sbt("norms", [P, TB, 2 * S2], F32)
        nmax = sbt("nmax", [P, 2 * S2], F32)
        nall = sbt("nall", [P, 2 * S2], F32)
        bound = sbt("bound", [P, 2], F32)
        state = sbt("state", [P, 2], F32)
        state_i = sbt("state_i", [P, 2], I32)
        QT = sbt("QT", [P, H, N], BF16)
        KTa = sbt("KTa", [P, H, N], BF16)
        V = sbt("V", [P, TB, H, VC], BF16)
        kts = sbt("kts", [P, N], BF16)
        qts = sbt("qts", [P, 2, 2, 512], BF16)
        vts = sbt("vts", [P, KT, VC], BF16)
        prob = sbt("prob", [P, RING, 1024], F32)
        low = sbt("low", [P, RING, 1024], BF16)
        stack = sbt("stack", [P, 1024], F32)
        rec = sbt("rec", [P, 8], F32)
        onrm = sbt("onrm", [P, 8, DV], F32)
        ot = sbt("ot", [P, 4, DV], F32)
        shift = sbt("shift", [P, TB, S2], F32)
        shparts = sbt("shparts", [P, TB, 3, S2], BF16)

        loaded = sem("attn_loaded")
        dve_done = sem("a_dve")
        preset = sem("a_preset")
        mv_ready = sem("a_mv_ready")
        lam_sum = sem("lam_sum")
        lam_exp = sem("lam_exp")
        rstd_done = sem("a_rstd")
        pool_done = sem("a_pool")

        with nc.Block() as block:
            @block.sync
            def _(sp):
                for c in range(4):
                    sp.dma_start(xs[:, 8 * c:8 * c + 8, :], a["x"][:, 8 * c:8 * c + 8, :]).then_inc(loaded, 16)
                sp.dma_start(wqkv[:], a["wqkv"]).then_inc(loaded, 16)
                sp.dma_start(sel[:], a["sel"]).then_inc(loaded, 16)
                sp.dma_start(ident[:], a["ident"]).then_inc(loaded, 16)
                sp.dma_start(lqk[:], a["lqk"].partition_broadcast(P)).then_inc(loaded, 16)

            @block.gpsimd
            def _(pool):
                pool.memset(mhalf[:], -0.5).then_inc(preset, 1)
                pool.memset(q_rows[:], 0.0).then_inc(preset, 1)
                pool.memset(k_rows[:], 0.0).then_inc(preset, 1)
                pool.memset(V[:], 0.0).then_inc(preset, 1)
                pool.memset(qts[:], 0.0).then_inc(preset, 1)
                pool.wait_ge(preset, 5)
                pool.memset(k_rows[:, :, :, SH:SH + 3], 1.0).then_inc(preset, 1)
                pool.memset(V[:, :, :, 3 * DV:3 * DV + 1], 1.0).then_inc(preset, 1)
                pool.wait_ge(preset, 7)
                pool.wait_ge(mv_ready, 1)
                pool.tensor_tensor(rstd[:], var[:], mhalf[:], ALU.pow).then_inc(rstd_done, 1)

            @block.scalar
            def _(act):
                act.wait_ge(lam_sum, 1)
                act.activation(lam4[:, 2:4], lam4[:, 0:2], ACT.Exp).then_inc(lam_exp, 1)

            @block.vector
            def _(dve):
                ch = Chain(dve, dve_done)
                dve.wait_ge(loaded, 16 * 8)
                ch(dve.tensor_copy(identb[:], ident[:]))
                ch(dve.memset(state[:], 0.0))
                ch(dve.tensor_tensor(lqk[:, 0::2, :], lqk[:, 0::2, :], lqk[:, 1::2, :], ALU.mult))
                dve.tensor_reduce(lam4[:, 0:2], lqk[:, 0::2, :], AX.X, ALU.add).then_inc(lam_sum, 1)
                with dve.Fori(0, NT) as t:
                    dve.bn_stats(st[:, bass.ds(t, 1), :], xs[:, bass.ds(t, 1), :]).then_inc(dve_done, 1)
                ch.n += NT
                dve.wait_ge(dve_done, ch.n)
                mean_rstd(dve, None, ch, st, mean[:], var[:], vtmp[:])
                dve.tensor_scalar(var[:], var[:], 1e-5, None, ALU.add).then_inc(mv_ready, 1)
                dve.wait_ge(lam_exp, 1)
                ch(dve.tensor_tensor(lam4[:, 4:5], lam4[:, 2:3], lam4[:, 3:4], ALU.subtract))
                ch(dve.tensor_scalar(lam[:], lam4[:, 4:5], LAM_INIT, None, ALU.add))
                dve.wait_ge(rstd_done, 1)
                with dve.Fori(0, NT) as t:
                    dve.tensor_scalar(xn[:, bass.ds(t, 1), :], xs[:, bass.ds(t, 1), :], mean[:, bass.ds(t, 1)],
                                      rstd[:, bass.ds(t, 1)], ALU.subtract, ALU.mult).then_inc(dve_done, 1)
                ch.n += NT
                dve.wait_ge(dve_done, ch.n)

        x_in = [sem(f"x_in{s}") for s in range(2)]
        xT_ready = [sem(f"xT_ready{s}") for s in range(2)]
        xT_copied = [sem(f"xT_copied{s}") for s in range(2)]
        qkv_ready = [sem(f"qkv_ready{s}") for s in range(2)]
        qkv_copied = [sem(f"qkv_copied{s}") for s in range(2)]
        squared = [sem(f"squared{s}") for s in range(2)]
        split_done = [sem(f"split_done{s}") for s in range(2)]
        build_chain = sem("build_chain")
        norms_done = [sem(f"norms_done{s}") for s in range(2)]
        q_rows_done = [sem(f"q_rows_done{s}") for s in range(2)]
        k_rows_done = [sem(f"k_rows_done{s}") for s in range(2)]
        v_done = [sem(f"v_done{s}") for s in range(2)]
        qT_ready = [sem(f"qT_ready{s}") for s in range(2)]
        kT_ready = [sem(f"kT_ready{s}") for s in range(2)]
        qT_copied = [sem(f"qT_copied{s}") for s in range(2)]
        kT_copied = [sem(f"kT_copied{s}") for s in range(2)]
        nmax_ready = sem("nmax_ready")
        carried = sem("carried")
        nall_ready = sem("nall_ready")
        bound_chain = sem("bound_chain")

        keys_masked = sem("keys_masked")
        all_scores = [sem(f"all_scores{s}") for s in range(2)]
        max_taken = [sem(f"max_taken{s}") for s in range(2)]
        shift_chain = sem("shift_chain")
        shift_split = sem("shift_split")
        shift_T = sem("shift_T")
        shift_copied = sem("shift_copied")
        shift_rows = sem("shift_rows")

        q_in = [sem(f"q_in{r}") for r in range(2)]
        k_in = [sem(f"k_in{c}") for c in range(4)]
        v_in = [sem(f"v_in{c}") for c in range(4)]
        q_free = [sem(f"q_free{r}") for r in range(2)]
        k_free = [sem(f"k_free{c}") for c in range(4)]
        v_free = [sem(f"v_free{c}") for c in range(4)]
        scores_ready = [sem(f"scores_ready{s}") for s in range(2)]
        exp_done = [sem(f"exp_done{s}") for s in range(RING)]
        low_done = [sem(f"low_done{s}") for s in range(RING)]
        pv_done = [sem(f"pv_done{s}") for s in range(RING)]
        evac0 = sem("evac0")
        evac1 = sem("evac1")
        t_ready = sem("t_ready")
        norm_chain = sem("norm_chain")

        with nc.Fori(0, B) as b:
            with ExitStack() as pctx, nc.Block() as block:
                def pt(name, shape, dt):
                    return pctx.enter_context(nc.psum_tensor(name, shape, dt))
                ps_x = [pt(f"ps_x{s}", [P, 512], F32) for s in range(2)]
                ps_qkv = [pt(f"ps_qkv{s}", [P, 512], F32) for s in range(2)]
                ps_q = [pt(f"ps_q{s}", [P, 1024], BF16) for s in range(2)]
                ps_k = [pt(f"ps_k{s}", [P, 1024], BF16) for s in range(2)]
                HB = TB // 2

                def row_groups(rows, s, lo, hi, step):
                    return rows[:, s, :, :].rearrange("p n (g d) -> p n g d", d=D)[:, :, lo:hi:step, :]

                def part_groups(s, j, o, n):
                    return parts[:, s, j, o * P:(o + 1) * P].rearrange("p (n a d) -> p n a d", a=1, d=D) \
                        .to_broadcast([P, S2, n, D])

                @block.sync
                def _(sp):
                    with sp.Fori(0, HB) as k:
                        for s in range(2):
                            sp.wait_ge(xT_ready[s], b * HB + k)
                            sp.dma_start(xslot[:, s, :], xn[:, bass.ds(b * TB + 2 * k + s, 1), :]
                                         .rearrange("p a d -> p (a d)")).then_inc(x_in[s], 16)

                @block.tensor
                def _(pe):
                    def front(t, s, used):
                        pe.wait_ge(x_in[s], 16 * (used + 1))
                        pe.wait_ge(xT_copied[s], used)
                        pe.transpose(ps_x[s][:, 0:P], xslot[:, s, :], ident[:]).then_inc(xT_ready[s], 1)
                        pe.wait_ge(xT_copied[s], used + 1)
                        pe.wait_ge(squared[s], used)
                        pe.matmul(ps_qkv[s][:, 0:3 * P], xnT[:, s, :], wqkv[:], start=True, stop=True) \
                            .then_inc(qkv_ready[s], 1)

                    def back(t, s, used):
                        pe.wait_ge(q_rows_done[s], used + 1)
                        pe.wait_ge(qT_copied[s], used)
                        for h in range(H):
                            last = pe.transpose(ps_q[s][:, h * P:(h + 1) * P],
                                                q_rows[:, s, 2 * h:2 * h + 2, :].rearrange("p a r -> p (a r)"),
                                                identb[:])
                        last.then_inc(qT_ready[s], 1)
                        pe.wait_ge(k_rows_done[s], used + 1)
                        pe.wait_ge(kT_copied[s], used)
                        for h in range(H):
                            last = pe.transpose(ps_k[s][:, h * P:(h + 1) * P],
                                                k_rows[:, s, 2 * h:2 * h + 2, :].rearrange("p a r -> p (a r)"),
                                                identb[:])
                        last.then_inc(kT_ready[s], 1)

                    pipelined(pe, front, back, TB, b * HB)

                @block.scalar
                def _(act):
                    def front(t, s, used):
                        act.wait_ge(xT_ready[s], used + 1)
                        act.copy(xnT[:, s, :], ps_x[s][:, 0:P]).then_inc(xT_copied[s], 1)
                        act.wait_ge(qkv_ready[s], used + 1)
                        act.wait_ge(split_done[s], used)
                        act.wait_ge(norms_done[s], used)
                        act.mul(qkv[:, s, 0:P], ps_qkv[s][:, 0:P], D ** -0.5).then_inc(qkv_copied[s], 1)
                        act.copy(qkv[:, s, P:3 * P], ps_qkv[s][:, P:3 * P]).then_inc(qkv_copied[s], 1)
                        act.wait_ge(qkv_copied[s], 2 * (used + 1))
                        act.activation(sq[:, s, :], qkv[:, s, 0:2 * P], ACT.Square).then_inc(squared[s], 1)

                    def back(t, s, used):
                        act.wait_ge(split_done[s], used + 1)
                        act.wait_ge(kT_ready[s], used)
                        for n, (j, lo, hi, step) in enumerate(((0, 0, 4, 3), (0, 5, 6, 1), (1, 1, 5, 3), (2, 2, 3, 1))):
                            last = act.copy(row_groups(k_rows, s, lo, hi, step), part_groups(s, j, 1, (hi - lo + step - 1) // step))
                        last.then_inc(k_rows_done[s], 1)

                    pipelined(act, front, back, TB, b * HB)

                @block.vector
                def _(dve):
                    def front(t, s, used):
                        c = (b * TB + t) * 3
                        dve.wait_ge(qkv_copied[s], 2 * (used + 1))
                        dve.wait_ge(q_rows_done[s], used)
                        dve.wait_ge(k_rows_done[s], used)
                        dve.wait_ge(v_done[s], used)
                        hi, mid, lo = (parts[:, s, k, :] for k in range(3))
                        dve.tensor_copy(hi, qkv[:, s, :]).then_inc(build_chain, 1)
                        dve.wait_ge(build_chain, c + 1)
                        dve.tensor_tensor(rest[:, s, :], qkv[:, s, :], hi, ALU.subtract).then_inc(build_chain, 1)
                        dve.wait_ge(build_chain, c + 2)
                        dve.tensor_copy(mid, rest[:, s, :]).then_inc(build_chain, 1)
                        dve.wait_ge(build_chain, c + 3)
                        dve.tensor_tensor(lo, rest[:, s, :], mid, ALU.subtract).then_inc(split_done[s], 1)
                        dve.wait_ge(squared[s], used + 1)
                        dve.tensor_reduce(norms[:, bass.ds(t, 1), :].rearrange("p a n -> p (a n)"),
                                          sq[:, s, :].rearrange("p (n d) -> p n d", d=D), AX.X, ALU.add) \
                            .then_inc(norms_done[s], 1)

                    def back(t, s, used):
                        dve.wait_ge(qT_ready[s], used + 1)
                        dve.tensor_copy(QT[:, :, bass.ds(t * P, P)],
                                        ps_q[s][:].rearrange("p (h t) -> p h t", h=H)).then_inc(qT_copied[s], 1)
                        dve.wait_ge(kT_ready[s], used + 1)
                        dve.tensor_copy(KTa[:, :, bass.ds(t * P, P)],
                                        ps_k[s][:].rearrange("p (h t) -> p h t", h=H)).then_inc(kT_copied[s], 1)

                    pipelined(dve, front, back, TB, b * HB)
                    dve.wait_ge(norms_done[0], (b + 1) * HB)
                    dve.wait_ge(norms_done[1], (b + 1) * HB)
                    dve.tensor_reduce(nmax[:], norms[:].rearrange("p t n -> p n t"), AX.X, ALU.max) \
                        .then_inc(nmax_ready, 1)
                    dve.wait_ge(nall_ready, b + 1)
                    c = b * 8
                    dve.tensor_tensor(nall[:, 0:S2], nall[:, 0:S2], nall[:, S2:2 * S2], ALU.mult) \
                        .then_inc(bound_chain, 1)
                    dve.wait_ge(bound_chain, c + 1)
                    dve.tensor_reduce(bound[:, 0:1], nall[:, 0:S2], AX.X, ALU.max).then_inc(bound_chain, 1)
                    dve.wait_ge(bound_chain, c + 2)
                    dve.tensor_tensor(state[:, 0:1], state[:, 0:1], state[:, 1:2], ALU.add).then_inc(bound_chain, 1)
                    dve.wait_ge(bound_chain, c + 3)
                    dve.tensor_scalar(bound[:, 1:2], bound[:, 0:1], SAFE * SAFE, None, ALU.is_le) \
                        .then_inc(bound_chain, 1)
                    dve.wait_ge(bound_chain, c + 4)
                    dve.tensor_scalar(state[:, 1:2], bound[:, 1:2], -1.0, 1.0, ALU.mult, ALU.add) \
                        .then_inc(bound_chain, 1)
                    dve.wait_ge(bound_chain, c + 5)
                    dve.tensor_copy(state_i[:], state[:]).then_inc(bound_chain, 3)

                @block.gpsimd
                def _(pool):
                    with pool.Fori(0, HB) as k:
                        for s in range(2):
                            used = b * HB + k
                            t = 2 * k + s
                            pool.wait_ge(split_done[s], used + 1)
                            pool.wait_ge(qT_ready[s], used)
                            pool.sem_inc(carried, 1)
                            for j, lo, hi in ((0, 0, 3), (1, 3, 5), (2, 5, 6)):
                                last = pool.tensor_copy(row_groups(q_rows, s, lo, hi, 1), part_groups(s, j, 0, hi - lo))
                            last.then_inc(q_rows_done[s], 1)
                            pool.tensor_copy(
                                V[:, bass.ds(t, 1), :, 0:3 * DV].rearrange("p a h (j d) -> p (a h) j d", j=3),
                                parts[:, s, :, 2 * P:3 * P].rearrange("p j (h d) -> p h j d", d=DV)) \
                                .then_inc(v_done[s], 1)
                    pool.wait_ge(nmax_ready, b + 1)
                    pool.sem_inc(carried, 1)
                    pool.partition_all_reduce(nall[:], nmax[:], P, RMAX).then_inc(nall_ready, 1)

            with ExitStack() as pctx, nc.Block() as block:
                ps_m = [pctx.enter_context(nc.psum_tensor(f"ps_m{s}", [P, N], F32)) for s in range(2)]
                HEADS = 2 * H
                PAIRS = TB // 2

                @block.tensor
                def _(pe):
                    m = pe.value_load(state_i[0:1, 0:1], min_val=0, max_val=1)
                    with pe.If(pe.value_load(state_i[0:1, 1:2], min_val=0, max_val=1) > 0):
                        for i in range(2):
                            with pe.Fori(0, H) as h:
                                head = m * HEADS + i * H + h
                                pe.wait_ge(keys_masked, head + 1)
                                pe.sem_inc(carried, 1)
                                with pe.Fori(0, PAIRS) as k:
                                    for s in range(2):
                                        pe.wait_ge(max_taken[s], head * PAIRS + k)
                                        for c in range(4):
                                            last = pe.matmul(ps_m[s][:, 512 * c:512 * (c + 1)],
                                                             QT[:, bass.ds(h, 1), bass.ds((2 * k + s) * P, P)]
                                                             .rearrange("p a n -> p (a n)"),
                                                             kts[:, 512 * c:512 * (c + 1)], start=True, stop=True)
                                        last.then_inc(all_scores[s], 1)
                        pe.wait_ge(shift_split, m + 1)
                        pe.sem_inc(carried, 1)
                        for t in range(TB):
                            last = pe.transpose(ps_m[0][0:3 * S2, t * P // 2:(t + 1) * P // 2].bitcast(BF16),
                                                shparts[:, t, :, :].rearrange("p j n -> p (j n)"), identb[:])
                        last.then_inc(shift_T, 1)

                @block.vector
                def _(dve):
                    m = dve.value_load(state_i[0:1, 0:1], min_val=0, max_val=1)
                    with dve.If(dve.value_load(state_i[0:1, 1:2], min_val=0, max_val=1) > 0):
                        for i in range(2):
                            dve.memset(kts[:], 0.0).then_inc(shift_chain, 1)
                            dve.wait_ge(shift_chain, m * 6 + i + 1)
                            dve.sem_inc(carried, 1)
                            with dve.Fori(0, H) as h:
                                head = m * HEADS + i * H + h
                                rows = slice(ROW * i, ROW * (i + 1))
                                dve.tensor_copy(kts[rows, :], KTa[rows, bass.ds(h, 1), :]
                                                .rearrange("p a n -> p (a n)")).then_inc(keys_masked, 1)
                                with dve.Fori(0, PAIRS) as k:
                                    for s in range(2):
                                        dve.wait_ge(all_scores[s], head * PAIRS + k + 1)
                                        dve.tensor_reduce(shift[:, bass.ds(2 * k + s, 1), bass.ds(i * H + h, 1)]
                                                          .rearrange("p a n -> p (a n)"),
                                                          ps_m[s][:], AX.X, ALU.max, negate=True) \
                                            .then_inc(max_taken[s], 1)
                            for s in range(2):
                                dve.wait_ge(max_taken[s], (m * HEADS + (i + 1) * H) * PAIRS)
                        dve.tensor_copy(shparts[:, :, 0, :], shift[:]).then_inc(shift_chain, 1)
                        dve.wait_ge(shift_chain, m * 6 + 3)
                        dve.tensor_tensor(shift[:], shift[:], shparts[:, :, 0, :], ALU.subtract) \
                            .then_inc(shift_chain, 1)
                        dve.wait_ge(shift_chain, m * 6 + 4)
                        dve.tensor_copy(shparts[:, :, 1, :], shift[:]).then_inc(shift_chain, 1)
                        dve.wait_ge(shift_chain, m * 6 + 5)
                        dve.tensor_tensor(shift[:], shift[:], shparts[:, :, 1, :], ALU.subtract) \
                            .then_inc(shift_chain, 1)
                        dve.wait_ge(shift_chain, m * 6 + 6)
                        dve.tensor_copy(shparts[:, :, 2, :], shift[:]).then_inc(shift_split, 1)

                @block.scalar
                def _(act):
                    m = act.value_load(state_i[0:1, 0:1], min_val=0, max_val=1)
                    with act.If(act.value_load(state_i[0:1, 1:2], min_val=0, max_val=1) > 0):
                        act.wait_ge(shift_T, m + 1)
                        act.copy(low[0:3 * S2, 0:2, :].rearrange("p r n -> p (r n)"),
                                 ps_m[0][0:3 * S2, 0:N // 2].bitcast(BF16)).then_inc(shift_copied, 1)

                @block.sync
                def _(sp):
                    m = sp.value_load(state_i[0:1, 0:1], min_val=0, max_val=1)
                    with sp.If(sp.value_load(state_i[0:1, 1:2], min_val=0, max_val=1) > 0):
                        sp.wait_ge(shift_copied, m + 1)
                        for j in range(3):
                            for i in range(2):
                                row = j * S2 + i * H
                                sp.dma_start(QT[ROW * i + SH + j:ROW * i + SH + j + 1, :, :],
                                             low[row:row + H, 0:2, :]).then_inc(shift_rows, 16)
                        sp.wait_ge(shift_rows, (m + 1) * 6 * 16)
                        sp.sem_inc(carried, 1)

            with ExitStack() as pctx, nc.Block() as block:
                def pt(name, shape, dt):
                    return pctx.enter_context(nc.psum_tensor(name, shape, dt))
                ps_s = pt("ps_s", [P, 4, 512], F32)
                ps_o = pt("ps_o", [P, 2, 512], F32)
                ps_t = pt("ps_t", [P, 512], F32)
                NU = 2 * H
                G = 32

                @block.sync
                def _(sp):
                    with sp.Fori(0, H) as h:
                        with sp.Fori(0, 2) as qp:
                            U = b * NU + h * 2 + qp

                            def load_q(r):
                                sp.wait_ge(q_free[r], U)
                                for i in range(2):
                                    rows = slice(ROW * i, ROW * (i + 1))
                                    sp.dma_start(qts[rows, r, i, :],
                                                 QT[rows, bass.ds(h, 1), bass.ds(qp * 1024 + r * 512, 512)]
                                                 .rearrange("p a n -> p (a n)")).then_inc(q_in[r], 16)
                            load_q(0)
                            for c in range(4):
                                sp.wait_ge(k_free[c], U)
                                sp.dma_start(kts[:, c * 512:(c + 1) * 512],
                                             KTa[:, bass.ds(h, 1), c * 512:(c + 1) * 512]
                                             .rearrange("p a n -> p (a n)")).then_inc(k_in[c], 16)
                                sp.wait_ge(v_free[c], U)
                                sp.dma_start(vts[:, 4 * c:4 * c + 4, :],
                                             V[:, 4 * c:4 * c + 4, bass.ds(h, 1), :]
                                             .rearrange("p t a n -> p t (a n)")).then_inc(v_in[c], 16)
                            load_q(1)

                @block.tensor
                def _(pe):
                    def scores(u, x):
                        U, x = b * NU + u + x // G, x % G
                        r, kt = x // KT, x % KT
                        if kt == 0:
                            pe.wait_ge(q_in[r], 32 * (U + 1))
                        if r == 0 and kt % 4 == 0:
                            pe.wait_ge(k_in[kt // 4], 16 * (U + 1))
                        y = x - 2
                        pe.wait_ge(exp_done[y % RING], U * (G // RING) + y // RING + 1)
                        for i in range(2):
                            last = pe.matmul(ps_s[:, 2 * (x % 2) + i, :], kts[:, kt * P:(kt + 1) * P], qts[:, r, i, :],
                                             start=True, stop=True)
                        last.then_inc(scores_ready[x % 2], 1)

                    def values(u, x):
                        U, x = b * NU + u + x // G, x % G
                        r, kt, slot = x // KT, x % KT, x % RING
                        if r == 0 and kt % 4 == 0:
                            pe.wait_ge(v_in[kt // 4], 16 * (U + 1))
                        if kt == 0:
                            pe.wait_ge(evac0, U * 2 + r)
                            pe.wait_ge(evac1, U * 2 + r)
                        pe.wait_ge(exp_done[slot], U * (G // RING) + x // RING + 1)
                        pe.wait_ge(low_done[slot], U * (G // RING) + x // RING + 1)
                        for i in range(2):
                            high = prob[:, slot, 512 * i:512 * (i + 1)].bitcast(BF16)[:, 1::2]
                            mm = pe.matmul(ps_o[0:64, i, :], vts[:, kt, :], high, start=(kt == 0),
                                           stop=(kt == KT - 1))
                            if i == 0 and r == 1 and kt % 4 == 3:
                                mm.then_inc(k_free[kt // 4], 1)
                            if i == 0 and r == 1 and kt % 4 == 0 and kt:
                                mm.then_inc(v_free[kt // 4 - 1], 1)
                            if i == 1 and kt == KT - 1:
                                mm.then_inc(q_free[r], 1)
                            last = pe.matmul(ps_o[64:128, i, :], vts[:, kt, :], low[:, slot, 512 * i:512 * (i + 1)],
                                             start=(kt == 0), stop=(kt == KT - 1))
                        last.then_inc(pv_done[slot], 1)

                    def totals(u, r):
                        n = (b * NU + u) * 2 + r
                        pe.wait_ge(evac0, n + 1)
                        pe.wait_ge(evac1, n + 1)
                        pe.wait_ge(norm_chain, 4 * n)
                        for i in range(8):
                            last = pe.matmul(ps_t[:, i * (DV + 1):(i + 1) * (DV + 1)], stack[:, i * P:(i + 1) * P],
                                             sel[:], start=True, stop=True)
                            if r == 1 and i == 0:
                                last.then_inc(v_free[3], 1)
                        last.then_inc(t_ready, 1)

                    AHEAD, T = 3, 4

                    def step(u, x, more=True):
                        values(u, x)
                        if more or x + AHEAD < G:
                            scores(u, x + AHEAD)
                        if x == KT + T - 1:
                            totals(u, 0)
                        if x == G + T - 1:
                            totals(u, 1)

                    for x in range(AHEAD):
                        scores(0, x)
                    for x in range(T):
                        step(0, x)
                    with pe.Fori(0, NU - 1) as u:
                        for x in range(T, G + T):
                            step(u, x)
                    for x in range(T, G):
                        step(NU - 1, x, more=False)
                    totals(NU - 1, 1)

                @block.scalar
                def _(act):
                    def exps(u, x):
                        U, x = b * NU + u + x // G, x % G
                        slot = x % RING
                        act.wait_ge(scores_ready[x % 2], U * (G // 2) + x // 2 + 1)
                        act.wait_ge(pv_done[slot], U * (G // RING) + x // RING)
                        act.activation(prob[:, slot, :],
                                       ps_s[:, 2 * (x % 2):2 * (x % 2) + 2, :].rearrange("p a n -> p (a n)"),
                                       ACT.Exp).then_inc(exp_done[slot], 1)

                    def evacuate(u, r):
                        U = b * NU + u
                        x = KT * r + KT - 1
                        act.wait_ge(pv_done[x % RING], U * (G // RING) + x // RING + 1)
                        act.wait_ge(t_ready, U * 2 + r)
                        act.copy(stack[:, 0:512], ps_o[:, 0, :]).then_inc(evac0, 1)

                    def step(u, x):
                        exps(u, x)
                        if x == KT + 1:
                            evacuate(u, 0)
                        if x == G + 1:
                            evacuate(u, 1)

                    for x in range(2):
                        exps(0, x)
                    with act.Fori(0, NU - 1) as u:
                        for x in range(2, G + 2):
                            step(u, x)
                    for x in range(2, G):
                        step(NU - 1, x)
                    evacuate(NU - 1, 1)

                @block.vector
                def _(dve):
                    def lows(u, x):
                        U, x = b * NU + u + x // G, x % G
                        slot = x % RING
                        dve.wait_ge(exp_done[slot], U * (G // RING) + x // RING + 1)
                        dve.tensor_tensor(low[:, slot, :], prob[:, slot, :], prob[:, slot, :].bitcast(BF16)[:, 1::2],
                                          ALU.subtract).then_inc(low_done[slot], 1)

                    def evacuate(u, r):
                        U = b * NU + u
                        x = KT * r + KT - 1
                        dve.wait_ge(pv_done[x % RING], U * (G // RING) + x // RING + 1)
                        dve.wait_ge(t_ready, U * 2 + r)
                        dve.tensor_copy(stack[:, 512:1024], ps_o[:, 1, :]).then_inc(evac1, 1)

                    def normalise(u, r):
                        U = b * NU + u
                        c = (U * 2 + r) * 4
                        tot = ps_t[:, 0:8 * (DV + 1)].rearrange("p (i n) -> p i n", n=DV + 1)
                        dve.wait_ge(t_ready, U * 2 + r + 1)
                        dve.reciprocal(rec[:], tot[:, :, DV]).then_inc(norm_chain, 1)
                        dve.wait_ge(norm_chain, c + 1)
                        dve.tensor_tensor(onrm[:], tot[:, :, 0:DV],
                                          rec[:].rearrange("p (i a) -> p i a", a=1).to_broadcast([P, 8, DV]),
                                          ALU.mult).then_inc(norm_chain, 1)
                        dve.wait_ge(norm_chain, c + 2)
                        dve.tensor_scalar(ot[:], onrm[:, 4:8, :], lam[:], None, ALU.mult).then_inc(norm_chain, 1)
                        dve.wait_ge(norm_chain, c + 3)
                        dve.tensor_tensor(o_all[:, bass.ds(U * 8 + r * 4, 4), :], onrm[:, 0:4, :], ot[:],
                                          ALU.subtract).then_inc(norm_chain, 1)

                    E, NRM = KT, 22

                    def step(u, x):
                        lows(u, x)
                        if x == KT:
                            evacuate(u, 0)
                        if x == NRM:
                            normalise(u, 0)
                        if x == KT + KT:
                            evacuate(u, 1)
                        if x == KT + NRM:
                            normalise(u, 1)

                    for x in range(7):
                        lows(0, x)
                    with dve.Fori(0, NU - 1) as u:
                        for x in range(7, G + 7):
                            step(u, x)
                    for x in range(7, G):
                        step(NU - 1, x)
                    evacuate(NU - 1, 1)
                    normalise(NU - 1, 1)



FF = 512
NK3 = 512
KF = FF // P
CH = 512
CT = CH // P
NC = B * N // CH
E = 32
EP = E // 2
EALL = EP + 1
TWO_OVER_PI = 0.6366197723675814


def add_normalised(nc, sem, name, xs, y, st, scalars, mhalf, scale_of=None, last=False):
    mean, var, tmp, rstd = scalars
    chain = sem(name + "_dve")
    var_ready = sem(name + "_var_ready")
    rstd_done = sem(name + "_rstd_done")
    with nc.Block() as block:
        @block.vector
        def _(dve):
            ch = Chain(dve, chain)
            mean_rstd(dve, None, ch, st, mean, var, tmp)
            dve.tensor_scalar(var, var, 1e-5, None, ALU.add).then_inc(var_ready, 1)
            dve.wait_ge(rstd_done, 1)
            with dve.Fori(0, NT) as t:
                dve.tensor_scalar(y[:, bass.ds(t, 1), :], y[:, bass.ds(t, 1), :], mean[:, bass.ds(t, 1)],
                                  rstd[:, bass.ds(t, 1)], ALU.subtract, ALU.mult).then_inc(chain, 1)
            ch.n += NT
            dve.wait_ge(chain, ch.n)
            ch(dve.tensor_tensor(xs[:], xs[:], y[:], ALU.add))
            if not last:
                with dve.Fori(0, NT) as t:
                    dve.bn_stats(st[:, bass.ds(t, 1), :], xs[:, bass.ds(t, 1), :]).then_inc(chain, 1)
                ch.n += NT
                dve.wait_ge(chain, ch.n)

        @block.gpsimd
        def _(pool):
            pool.wait_ge(var_ready, 1)
            pool.tensor_tensor(rstd, var, mhalf, ALU.pow).then_inc(rstd_done, 1)


def later_layers(nc, a, sem, xs, o_all, ident, identb, out):
    with ExitStack() as ctx:
        def sbt(name, shape, dt=F32, c=ctx):
            return c.enter_context(nc.sbuf_tensor(name, shape, dt))

        y = sbt("y", [P, NT, P])
        st = sbt("stats", [P, NT, 6])
        mean = sbt("mean2", [P, NT])[:]
        var = sbt("var2", [P, NT])[:]
        tmp = sbt("tmp2", [P, NT])[:]
        rstd = sbt("rstd2", [P, NT])[:]
        scale = sbt("scale2", [P, NT])[:]
        mhalf = sbt("mhalf2", [P, 2 * P])
        scalars = (mean, var, tmp, rstd)
        slot = sbt("slot", [P, 2, CT, P])
        xT = sbt("xT", [P, 2, CH])
        wo = sbt("wo_sb", [P, P])
        lng = sbt("lng", [P, 1])
        lnb = sbt("lnb", [P, 1])
        wg = sbt("wg", [P, EALL * P])
        wu = sbt("wu", [P, EALL * P])
        wd = sbt("wd", [P, EALL, P])
        gw = sbt("gw", [P, E])
        gbias = sbt("gbias", [P, E])
        esel = sbt("esel", [3 * E, EP * P], BF16)
        w_in = sem("wo_in")
        moe_in = sem("moe_in")
        constants_set = sem("constants_set")
        carried = sem("carried_later")

        n_g = NT * H
        grstd = sbt("grstd", [P, n_g])
        esel_f = sbt("esel_f", [3 * E, EP * P])
        group = ExitStack()
        gsum = sbt("gsum", [P, n_g], F32, group)
        gvar = sbt("gvar", [P, n_g], F32, group)
        gsq = sbt("gsq", [P, n_g, DV], F32, group)
        g_chain, g_sq, g_var, g_rstd = sem("g_chain"), sem("g_sq"), sem("g_var"), sem("g_rstd")
        

        def bc(v, n, d):
            return v.rearrange("p (n a) -> p n a", a=1).to_broadcast([P, n, d])

        with nc.Block() as block:
            @block.sync
            def _(sp):
                sp.dma_start(wo[:], a["wo"]).then_inc(w_in, 16)
                sp.dma_start(lng[:], a["lng"]).then_inc(w_in, 16)
                sp.dma_start(lnb[:], a["lnb"]).then_inc(w_in, 16)
                sp.dma_start(wg[:], a["wg"]).then_inc(moe_in, 16)
                sp.dma_start(wu[:], a["wu"]).then_inc(moe_in, 16)
                sp.dma_start(wd[:], a["wd"]).then_inc(moe_in, 16)
                sp.dma_start(gw[:], a["gw"]).then_inc(moe_in, 16)
                sp.dma_start(gbias[:], a["gb"].partition_broadcast(P)).then_inc(moe_in, 16)
                sp.dma_start(esel_f[:], a["esel"]).then_inc(moe_in, 16)

            @block.vector
            def _(dve):
                ch = Chain(dve, g_chain)
                ch(dve.tensor_reduce(gsum[:], o_all[:], AX.X, ALU.add))
                ch(dve.tensor_scalar(gsum[:], gsum[:], 1.0 / DV, None, ALU.mult))
                ch(dve.tensor_tensor(o_all[:], o_all[:], bc(gsum[:], n_g, DV), ALU.subtract))
                dve.wait_ge(g_sq, 1)
                ch(dve.tensor_reduce(gvar[:], gsq[:], AX.X, ALU.add))
                dve.tensor_scalar(gvar[:], gvar[:], 1.0 / DV, 1e-5, ALU.mult, ALU.add).then_inc(g_var, 1)
                dve.wait_ge(g_rstd, 1)

            @block.scalar
            def _(act):
                act.wait_ge(g_chain, 3)
                act.activation(gsq[:], o_all[:], ACT.Square).then_inc(g_sq, 1)

            @block.gpsimd
            def _(pool):
                pool.memset(mhalf[:], -0.5).then_inc(constants_set, 1)
                pool.wait_ge(constants_set, 1)
                pool.wait_ge(g_var, 1)
                pool.tensor_tensor(grstd[:], gvar[:], mhalf[:], ALU.pow).then_inc(g_rstd, 1)

        group.close()

        def slots(name):
            return [sem(f"{name}{s}") for s in range(2)]

        with ExitStack() as pctx, nc.Block() as block:
            ps_t = [pctx.enter_context(nc.psum_tensor(f"p1_t{s}", [P, CH], F32)) for s in range(2)]
            ps_y = [pctx.enter_context(nc.psum_tensor(f"p1_y{s}", [P, CH], F32)) for s in range(2)]
            on_ready, t_ready, t_copied = slots("p1_on"), slots("p1_t"), slots("p1_tc")
            y_ready, y_copied, stat = slots("p1_y"), slots("p1_yc"), sem("p1_stat")
            o_v = o_all[:].rearrange("p (b h q t) d -> p b h q t d", b=B, h=H, q=NQC)
            r_v = grstd[:].rearrange("p (b h q t a) -> p b h q t a", b=B, h=H, q=NQC, a=1)

            @block.vector
            def _(dve):
                def front(c, s, used):
                    b, q = c // NQC, c % NQC
                    dve.wait_ge(t_ready[s], used)
                    for t in range(CT):
                        last = dve.tensor_tensor(
                            slot[:, s, t, :].rearrange("p (h d) -> p h d", h=H),
                            o_v[:, b, :, q, t, :], r_v[:, b, :, q, t, :].to_broadcast([P, H, DV]), ALU.mult)
                    last.then_inc(on_ready[s], 1)

                def back(c, s, used):
                    dve.wait_ge(y_copied[s], used + 1)
                    for t in range(CT):
                        dve.bn_stats(st[:, CT * c + t:CT * c + t + 1, :], y[:, CT * c + t:CT * c + t + 1, :]) \
                            .then_inc(stat, 1)

                for c in range(NC):
                    front(c, c % 2, c // 2)
                    if c:
                        back(c - 1, (c - 1) % 2, (c - 1) // 2)
                back(NC - 1, 1, (NC - 1) // 2)
                dve.wait_ge(stat, NT)

            @block.tensor
            def _(pe):
                pe.wait_ge(w_in, 48)

                def front(c, s, used):
                    pe.wait_ge(on_ready[s], used + 1)
                    pe.wait_ge(t_copied[s], used)
                    for t in range(CT):
                        last = pe.transpose(ps_t[s][:, t * P:(t + 1) * P], slot[:, s, t, :], ident[:])
                    last.then_inc(t_ready[s], 1)

                def back(c, s, used):
                    pe.wait_ge(t_copied[s], used + 1)
                    pe.wait_ge(y_copied[s], used)
                    for t in range(CT):
                        last = pe.matmul(ps_y[s][:, t * P:(t + 1) * P], xT[:, s, t * P:(t + 1) * P], wo[:],
                                         start=True, stop=True)
                    last.then_inc(y_ready[s], 1)

                pipelined(pe, front, back, NC, 0)

            @block.scalar
            def _(act):
                act.wait_ge(w_in, 48)

                def front(c, s, used):
                    act.wait_ge(t_ready[s], used + 1)
                    act.wait_ge(y_ready[s], used)
                    act.activation(xT[:, s, :], ps_t[s][:], ACT.Identity, bias=lnb[:], scale=lng[:]) \
                        .then_inc(t_copied[s], 1)

                def back(c, s, used):
                    act.wait_ge(y_ready[s], used + 1)
                    act.sem_inc(carried, 1)
                    act.copy(y[:, bass.ds(CT * c, CT), :].rearrange("p t d -> p (t d)"), ps_y[s][:]) \
                        .then_inc(y_copied[s], 1)

                pipelined(act, front, back, NC, 0)

        add_normalised(nc, sem, "res1", xs, y, st, scalars, mhalf[:, 0:NT])

        small = sem("l2_small")
        with ExitStack() as l2:
            def sb2(name, shape, dt=F32):
                return l2.enter_context(nc.sbuf_tensor(name, shape, dt))
            up = sb2("up", [P, FF])
            down = sb2("down", [P, KF, P])
            tern = sb2("tern", [P, FF])
            sgn = sb2("sgn", [P, FF])
            asum = sb2("asum", [P, 2])
            aall = sb2("aall", [P, 2])
            ones = sb2("ones", [P, 1])
            hid = sb2("hid", [P, 2, KF, CH])
            hsq = sb2("hsq", [P, KF, CH])
            hsum = sb2("hsum", [P, 2, CH])
            rms = sb2("rms", [P, NT])
            loaded, chain, asum_ready, aall_ready, sqrt_in, sqrt_out = (sem("l2_" + n) for n in (
                "loaded", "chain", "asum", "aall", "sqrt_in", "sqrt_out"))
            with nc.Block() as block:
                @block.sync
                def _(sp):
                    sp.dma_start(up[:], a["up"]).then_inc(loaded, 16)
                    sp.dma_start(down[:], a["down"]).then_inc(loaded, 16)

                @block.gpsimd
                def _(pool):
                    pool.memset(ones[:], 1.0)
                    pool.wait_ge(asum_ready, 1)
                    pool.partition_all_reduce(aall[:], asum[:], P, RADD).then_inc(aall_ready, 1)
                    pool.wait_ge(sqrt_in, 1)
                    pool.tensor_tensor(rstd, scale, mhalf[:, 0:NT], ALU.pow).then_inc(sqrt_out, 1)

                @block.vector
                def _(dve):
                    ch = Chain(dve, chain)
                    mean_rstd(dve, None, ch, st, mean, var, tmp)
                    dve.tensor_scalar(scale, var, 1e-5, None, ALU.add).then_inc(sqrt_in, 1)
                    dve.wait_ge(loaded, 32)
                    flat_down = down[:].rearrange("p k n -> p (k n)")
                    for i, w in enumerate((up[:], flat_down)):
                        ch(dve.tensor_reduce(asum[:, i:i + 1], w, AX.X, ALU.add, apply_absolute_value=True))
                    dve.tensor_scalar(asum[:], asum[:], 0.5 / (P * FF), None, ALU.mult).then_inc(asum_ready, 1)
                    dve.wait_ge(aall_ready, 1)
                    ch(dve.tensor_scalar(asum[:], aall[:], -1.0, None, ALU.mult))
                    for i, w in enumerate((up[:], flat_down)):
                        ch(dve.tensor_scalar(tern[:], w, aall[:, i:i + 1], None, ALU.is_gt))
                        ch(dve.tensor_scalar(sgn[:], w, asum[:, i:i + 1], None, ALU.is_lt))
                        ch(dve.tensor_tensor(tern[:], tern[:], sgn[:], ALU.subtract))
                        ch(dve.tensor_tensor(tern[:], tern[:], w, ALU.subtract))
                        ch(dve.tensor_tensor(w, w, tern[:], ALU.add))
                    dve.wait_ge(sqrt_out, 1)
                    ch(dve.tensor_tensor(tmp, rstd, rstd, ALU.mult))
                    dve.tensor_tensor(tmp, tmp, var, ALU.mult).then_inc(small, 1)
            with nc.Block() as block:
                @block.gpsimd
                def _(pool):
                    pool.tensor_scalar(mhalf[:, P:P + NT], mhalf[:, P:P + NT], -1.0, None, ALU.mult).then_inc(small, 1)
                    pool.wait_ge(small, 2)
                    pool.tensor_tensor(scale, tmp, mhalf[:, P:P + NT], ALU.pow).then_inc(small, 1)

                @block.vector
                def _(dve):
                    dve.wait_ge(small, 3)
                    dve.tensor_scalar(scale, scale, 1e-8, None, ALU.add).then_inc(small, 1)
                    dve.wait_ge(small, 4)
                    dve.reciprocal(scale, scale).then_inc(small, 1)
                    dve.wait_ge(small, 5)
                    dve.tensor_tensor(scale, scale, rstd, ALU.mult).then_inc(small, 1)

            with ExitStack() as pctx, nc.Block() as block:
                ps_t = pctx.enter_context(nc.psum_tensor("p2_t", [P, CH], F32))
                ps_h = pctx.enter_context(nc.psum_tensor("p2_h", [P, KF, CH], F32))
                ps_y = pctx.enter_context(nc.psum_tensor("p2_y", [P, CH], F32))
                ps_r = pctx.enter_context(nc.psum_tensor("p2_r", [P, CH], F32))
                xn_ready, t_ready, t_copied, h_ready, h_done, sq_done, sum_done, y_ready = (
                    slots("p2_" + n) for n in ("xn", "t", "tc", "h", "hd", "sq", "sum", "y"))
                y_copied, stat, r_copied = sem("p2_yc"), sem("p2_stat"), sem("p2_rc")
                t_free = sem("p2_t_free")

                @block.vector
                def _(dve):
                    def front(c, s, used):
                        dve.wait_ge(t_ready[s], used)
                        for t in range(CT):
                            i = CT * c + t
                            last = dve.tensor_scalar(slot[:, s, t, :], xs[:, bass.ds(i, 1), :].rearrange("p a d -> p (a d)"),
                                                     mean[:, bass.ds(i, 1)], scale[:, bass.ds(i, 1)],
                                                     ALU.subtract, ALU.mult)
                        last.then_inc(xn_ready[s], 1)

                    def back(c, s, used):
                        dve.wait_ge(sq_done[s], used + 1)
                        dve.wait_ge(y_ready[s], used)
                        dve.tensor_reduce(hsum[:, s, :], hsq[:].rearrange("p k n -> p n k"), AX.X, ALU.add) \
                            .then_inc(sum_done[s], 1)
                        dve.wait_ge(y_copied, c + 1)
                        dve.tensor_copy(rms[:, bass.ds(CT * c, CT)], ps_r[:, 0:CT]).then_inc(r_copied, 1)
                        for t in range(CT):
                            dve.bn_stats(st[:, bass.ds(CT * c + t, 1), :], y[:, bass.ds(CT * c + t, 1), :]) \
                                .then_inc(stat, 1)

                    pipelined(dve, front, back, NC, 0)
                    dve.wait_ge(stat, NT)

                @block.tensor
                def _(pe):
                    def front(c, s, used):
                        pe.wait_ge(xn_ready[s], used + 1)
                        pe.wait_ge(t_copied[1 - s], used + s)
                        for t in range(CT):
                            last = pe.transpose(ps_t[:, t * P:(t + 1) * P], slot[:, s, t, :], ident[:])
                        last.then_inc(t_ready[s], 1)
                        pe.wait_ge(t_copied[s], used + 1)
                        for k in range(KF):
                            pe.wait_ge(h_done[1 - s], (used + s) * KF)
                            pe.matmul(ps_h[:, k, :], up[:, k * P:(k + 1) * P], xT[:, s, :], start=True, stop=True) \
                                .then_inc(h_ready[s], 1)

                    def back(c, s, used):
                        pe.wait_ge(h_done[s], (used + 1) * KF)
                        pe.wait_ge(y_copied, c)
                        pe.wait_ge(r_copied, c)
                        for t in range(CT):
                            for k in range(KF):
                                pe.matmul(ps_y[:, t * P:(t + 1) * P], hid[:, s, k, t * P:(t + 1) * P], down[:, k, :],
                                          start=(k == 0), stop=(k == KF - 1))
                        pe.wait_ge(sum_done[s], used + 1)
                        for t in range(CT):
                            last = pe.matmul(ps_r[:, t:t + 1], hsum[:, s, t * P:(t + 1) * P], ones[:],
                                             start=True, stop=True)
                        last.then_inc(y_ready[s], 1)

                    pipelined(pe, front, back, NC, 0)

                @block.scalar
                def _(act):
                    def front(c, s, used):
                        act.wait_ge(t_ready[s], used + 1)
                        act.copy(xT[:, s, :], ps_t[:]).then_inc(t_copied[s], 1)
                        act.wait_ge(y_ready[s], used)
                        for k in range(KF):
                            act.wait_ge(h_ready[s], used * KF + k + 1)
                            act.activation(hid[:, s, k, :], ps_h[:, k, :], ACT.Gelu).then_inc(h_done[s], 1)
                        act.wait_ge(h_done[s], (used + 1) * KF)
                        act.wait_ge(sum_done[1 - s], used + s)
                        act.activation(hsq[:], hid[:, s, :, :], ACT.Square).then_inc(sq_done[s], 1)

                    def back(c, s, used):
                        act.wait_ge(y_ready[s], used + 1)
                        act.sem_inc(carried, 1)
                        act.copy(y[:, bass.ds(CT * c, CT), :].rearrange("p t d -> p (t d)"), ps_y[:]) \
                            .then_inc(y_copied, 1)

                    pipelined(act, front, back, NC, 0)

            q = sem("l2_q")
            with nc.Block() as block:
                @block.gpsimd
                def _(pool):
                    pool.wait_ge(q, 1)
                    pool.tensor_tensor(rms[:], rms[:], mhalf[:, P:P + NT], ALU.pow).then_inc(q, 1)

                @block.vector
                def _(dve):
                    dve.tensor_scalar(rms[:], rms[:], 1.0 / FF, None, ALU.mult).then_inc(q, 1)
                    dve.wait_ge(q, 2)
                    ch = Chain(dve, q, 2)
                    ch(dve.tensor_scalar(rms[:], rms[:], 1e-8, None, ALU.add))
                    ch(dve.reciprocal(rms[:], rms[:]))
                    with dve.Fori(0, NT) as t:
                        dve.tensor_scalar(y[:, bass.ds(t, 1), :], y[:, bass.ds(t, 1), :], rms[:, bass.ds(t, 1)],
                                          None, ALU.mult).then_inc(q, 1)
                    ch.n += NT
                    dve.wait_ge(q, 2 + ch.n)
                    with dve.Fori(0, NT) as t:
                        dve.bn_stats(st[:, bass.ds(t, 1), :], y[:, bass.ds(t, 1), :]).then_inc(q, 1)
                    ch.n += NT
                    dve.wait_ge(q, 2 + ch.n)
        add_normalised(nc, sem, "res2", xs, y, st, scalars, mhalf[:, 0:NT])
        third_layer(nc, a, sem, xs, y, o_all, st, scalars, scale, mhalf, slot, xT, ident, slots, carried)
        add_normalised(nc, sem, "res3", xs, y, st, scalars, mhalf[:, 0:NT])
        experts(nc, a, sem, xs, y, st, scalars, scale, mhalf, slot, xT, ident, identb, slots,
                wg, wu, wd, gw, gbias, esel_f, esel, moe_in, carried)
        add_normalised(nc, sem, "res4", xs, y, st, scalars, mhalf[:, 0:NT], last=True)
        stored = sem("stored")
        with nc.Block() as block:
            @block.sync
            def _(sp):
                for c in range(4):
                    sp.dma_start(out[:, 8 * c:8 * c + 8, :], xs[:, 8 * c:8 * c + 8, :]).then_inc(stored, 16)
                sp.wait_ge(stored, 64)


def third_layer(nc, a, sem, xs, y, o_all, st, scalars, scale, mhalf, slot, xT, ident, slots, carried):
    mean, var, tmp, rstd = scalars
    with ExitStack() as l3:
        def sb3(name, shape, dt=F32):
            return l3.enter_context(nc.sbuf_tensor(name, shape, dt))
        kw = sb3("kw", [P, KF, P])
        kT = sb3("kT", [P, NK3])
        qw = sb3("qw", [P, KF, P])
        bias3 = sb3("bias3", [P, P])
        w3 = sb3("w3", [P, P])
        b3 = sb3("b3", [P, P])
        kn = sb3("kn", [P, KF])
        ksq = sb3("ksq", [P, KF, P])
        zsq = o_all[:].rearrange("p g d -> p (g d)").rearrange("p (t n) -> p t n", n=P)
        zn = sb3("zn", [P, NT])
        loaded, kc, pc, kt_ready, zs = (sem("l3_" + n) for n in ("loaded", "kc", "pc", "kt", "zs"))

        def rows(v):
            return v[:].rearrange("p (a d) -> p a d", a=1).to_broadcast([P, NT, P])

        with ExitStack() as pctx, nc.Block() as block:
            ps_k = pctx.enter_context(nc.psum_tensor("p3_k", [P, NK3], F32))

            @block.sync
            def _(sp):
                sp.dma_start(kw[:], a["kw"]).then_inc(loaded, 16)
                sp.dma_start(qw[:], a["qw"]).then_inc(loaded, 16)
                for dst, n in ((bias3, "bias3"), (w3, "w3"), (b3, "b3")):
                    sp.dma_start(dst[:], a[n].partition_broadcast(P)).then_inc(loaded, 16)

            @block.gpsimd
            def _(pool):
                pool.wait_ge(pc, 1)
                pool.tensor_tensor(kn[:], kn[:], mhalf[:, 0:KF], ALU.pow).then_inc(pc, 1)
                pool.wait_ge(pc, 3)
                pool.tensor_tensor(rstd, scale, mhalf[:, 0:NT], ALU.pow).then_inc(pc, 1)
                pool.wait_ge(pc, 5)
                pool.tensor_tensor(tmp, tmp, mhalf[:, 0:NT], ALU.pow).then_inc(pc, 1)
                pool.wait_ge(pc, 7)
                pool.tensor_tensor(zn[:], zn[:], mhalf[:, 0:NT], ALU.pow).then_inc(pc, 1)

            @block.vector
            def _(dve):
                ch = Chain(dve, kc)
                dve.wait_ge(loaded, 80)
                ch(dve.tensor_tensor(ksq[:], kw[:], kw[:], ALU.mult))
                ch(dve.tensor_reduce(kn[:], ksq[:], AX.X, ALU.add))
                dve.tensor_scalar(kn[:], kn[:], 1e-24, None, ALU.max).then_inc(pc, 1)
                dve.wait_ge(pc, 2)
                ch(dve.tensor_tensor(kw[:], kw[:], kn[:].rearrange("p (k a) -> p k a", a=1).to_broadcast([P, KF, P]),
                                     ALU.mult))
                mean_rstd(dve, None, ch, st, mean, var, tmp)
                dve.tensor_scalar(scale, var, 1e-5, None, ALU.add).then_inc(pc, 1)
                dve.wait_ge(pc, 4)
                ch(dve.tensor_tensor(tmp, rstd, rstd, ALU.mult))
                ch(dve.tensor_tensor(tmp, tmp, var, ALU.mult))
                dve.tensor_scalar(tmp, tmp, 1e-12, None, ALU.add).then_inc(pc, 1)
                dve.wait_ge(pc, 6)
                ch(dve.tensor_tensor(scale, rstd, tmp, ALU.mult))
                with dve.Fori(0, NT) as t:
                    dve.tensor_scalar(y[:, bass.ds(t, 1), :], xs[:, bass.ds(t, 1), :], mean[:, bass.ds(t, 1)],
                                      scale[:, bass.ds(t, 1)], ALU.subtract, ALU.mult).then_inc(kc, 1)
                ch.n += NT
                dve.wait_ge(kc, ch.n)
                ch(dve.tensor_tensor(y[:], y[:], rows(w3), ALU.mult))
                dve.tensor_tensor(y[:], y[:], rows(b3), ALU.add).then_inc(zs, 1)
                dve.wait_ge(zs, 2)
                ch(dve.tensor_reduce(zn[:], zsq, AX.X, ALU.add))
                dve.tensor_scalar(zn[:], zn[:], 1e-24, None, ALU.max).then_inc(pc, 1)
                dve.wait_ge(pc, 8)

            @block.scalar
            def _(act):
                act.wait_ge(kt_ready, 1)
                act.copy(kT[:], ps_k[:]).then_inc(kt_ready, 1)
                act.wait_ge(zs, 1)
                act.activation(zsq, y[:], ACT.Square).then_inc(zs, 1)

            @block.tensor
            def _(pe):
                pe.wait_ge(kc, 3)
                for k in range(KF):
                    last = pe.transpose(ps_k[:, k * P:(k + 1) * P], kw[:, k, :], ident[:])
                last.then_inc(kt_ready, 1)

        d_all = sb3("d_all", [P, NC, KF * CH])
        s_sb = sb3("s_sb", [P, KF * CH])
        ln_p = sb3("ln_p", [P, KF * CH])
        ln_m = s_sb
        pw = sb3("pw", [P, KF, CH])
        with ExitStack() as pctx, nc.Block() as block:
            ps_t = pctx.enter_context(nc.psum_tensor("p3_t", [P, CH], F32))
            ps_s = pctx.enter_context(nc.psum_tensor("p3_s", [P, KF, CH], F32))
            q_ready, t_ready, t_copied = slots("p3_q"), slots("p3_t"), slots("p3_tc")
            s_ready, clipped, lns, d_done = sem("p3_s"), sem("p3_clip"), sem("p3_ln"), sem("p3_d")

            @block.vector
            def _(dve):
                def front(c, s, used):
                    dve.wait_ge(t_ready[s], used)
                    for t in range(CT):
                        i = CT * c + t
                        last = dve.tensor_scalar(slot[:, s, t, :], y[:, bass.ds(i, 1), :].rearrange("p a d -> p (a d)"),
                                                 zn[:, bass.ds(i, 1)], None, ALU.mult)
                    last.then_inc(q_ready[s], 1)

                def back(c, s, used):
                    dve.wait_ge(d_done, c)
                    for k in range(KF):
                        dve.wait_ge(s_ready, KF * c + k + 1)
                        dve.tensor_scalar(s_sb[:, k * CH:(k + 1) * CH], ps_s[:, k, :], 1.0 - 1e-6, -1.0 + 1e-6,
                                          ALU.min, ALU.max).then_inc(clipped, 1)
                    dve.wait_ge(lns, 2 * c + 2)
                    dve.tensor_tensor(d_all[:, bass.ds(c, 1), :].rearrange("p a n -> p (a n)"), ln_p[:], ln_m[:],
                                      ALU.subtract).then_inc(d_done, 1)

                pipelined(dve, front, back, NC, 0)

            @block.tensor
            def _(pe):
                def front(c, s, used):
                    pe.wait_ge(q_ready[s], used + 1)
                    pe.wait_ge(t_copied[1 - s], used + s)
                    for t in range(CT):
                        last = pe.transpose(ps_t[:, t * P:(t + 1) * P], slot[:, s, t, :], ident[:])
                    last.then_inc(t_ready[s], 1)

                def back(c, s, used):
                    pe.wait_ge(t_copied[s], used + 1)
                    for k in range(KF):
                        pe.wait_ge(clipped, KF * c)
                        pe.matmul(ps_s[:, k, :], kT[:, k * P:(k + 1) * P], xT[:, s, :], start=True, stop=True) \
                            .then_inc(s_ready, 1)

                pipelined(pe, front, back, NC, 0)

            @block.scalar
            def _(act):
                def front(c, s, used):
                    act.wait_ge(t_ready[s], used + 1)
                    act.copy(xT[:, s, :], ps_t[:]).then_inc(t_copied[s], 1)

                def back(c, s, used):
                    act.wait_ge(clipped, KF * c + KF)
                    act.wait_ge(d_done, c)
                    act.activation(ln_p[:], s_sb[:], ACT.Ln, bias=1.0, scale=1.0).then_inc(lns, 1)
                    act.wait_ge(lns, 2 * c + 1)
                    act.activation(ln_m[:], s_sb[:], ACT.Ln, bias=1.0, scale=-1.0).then_inc(lns, 1)

                pipelined(act, front, back, NC, 0)

        at, w_2 = s_sb, ln_p
        with ExitStack() as pctx, nc.Block() as block:
            ps_x = [pctx.enter_context(nc.psum_tensor(f"p3_x{s}", [P, CH], F32)) for s in range(2)]
            ac, w4_done, w8_done, pw_done, x_ready, x_copied = (sem("p3c_" + n) for n in (
                "ac", "w4", "w8", "pw", "x", "xc"))
            half_b = sb3("half_b", [P, 1])
            hb = sem("p3_half")

            @block.gpsimd
            def _(pool):
                pool.memset(half_b[:], 0.5).then_inc(hb, 1)

            @block.scalar
            def _(act):
                act.wait_ge(hb, 1)
                with act.Fori(0, NC) as c:
                    d_c = d_all[:, bass.ds(c, 1), :].rearrange("p a n -> p (a n)")
                    act.activation(d_c, d_c, ACT.Tanh, scale=0.25).then_inc(ac, 1)
                    act.wait_ge(pw_done, c)
                    act.wait_ge(ac, 3 * c + 1)
                    act.sem_inc(carried, 1)
                    act.activation(at[:], d_c, ACT.Arctan).then_inc(ac, 1)
                    act.wait_ge(ac, 3 * c + 2)
                    act.activation(w_2[:], at[:], ACT.Square, bias=half_b[:], scale=TWO_OVER_PI).then_inc(ac, 1)
                    act.wait_ge(w4_done, c + 1)
                    act.activation(w_2[:], w_2[:], ACT.Square, scale=TWO_OVER_PI ** 0.5).then_inc(w8_done, 1)
                    act.wait_ge(x_ready, c + 1)
                    act.sem_inc(carried, 1)
                    act.copy(y[:, bass.ds(CT * c, CT), :].rearrange("p t d -> p (t d)"), ps_x[0][:]) \
                        .then_inc(x_copied, 1)

            @block.vector
            def _(dve):
                with dve.Fori(0, NC) as c:
                    dve.wait_ge(ac, 3 * c + 3)
                    dve.tensor_tensor(w_2[:], w_2[:], w_2[:], ALU.mult).then_inc(w4_done, 1)
                    dve.wait_ge(w8_done, c + 1)
                    dve.wait_ge(x_ready, c)
                    dve.scalar_tensor_tensor(pw[:].rearrange("p k n -> p (k n)"), at[:], 0.7853981633974483, w_2[:],
                                             ALU.add, ALU.mult).then_inc(pw_done, 1)

            @block.tensor
            def _(pe):
                with pe.Fori(0, NC) as c:
                    pe.wait_ge(pw_done, c + 1)
                    pe.wait_ge(x_copied, c)
                    for t in range(CT):
                        for k in range(KF):
                            last = pe.matmul(ps_x[0][:, t * P:(t + 1) * P], pw[:, k, t * P:(t + 1) * P], qw[:, k, :],
                                             start=(k == 0), stop=(k == KF - 1))
                    last.then_inc(x_ready, 1)

        xc, xp = sem("l3_xc"), sem("l3_xp")
        with nc.Block() as block:
            @block.scalar
            def _(act):
                act.activation(zsq, y[:], ACT.Square).then_inc(xp, 1)

            @block.gpsimd
            def _(pool):
                pool.wait_ge(xp, 2)
                pool.tensor_tensor(zn[:], zn[:], mhalf[:, 0:NT], ALU.pow).then_inc(xp, 1)

            @block.vector
            def _(dve):
                ch = Chain(dve, xc)
                dve.wait_ge(xp, 1)
                ch(dve.tensor_reduce(zn[:], zsq, AX.X, ALU.add))
                dve.tensor_scalar(zn[:], zn[:], 1e-24, None, ALU.max).then_inc(xp, 1)
                dve.wait_ge(xp, 3)
                with dve.Fori(0, NT) as t:
                    dve.tensor_scalar(y[:, bass.ds(t, 1), :], y[:, bass.ds(t, 1), :], zn[:, bass.ds(t, 1)],
                                      None, ALU.mult).then_inc(xc, 1)
                ch.n += NT
                dve.wait_ge(xc, ch.n)
                ch(dve.tensor_tensor(y[:], y[:], rows(bias3), ALU.add))
                with dve.Fori(0, NT) as t:
                    dve.bn_stats(st[:, bass.ds(t, 1), :], y[:, bass.ds(t, 1), :]).then_inc(xc, 1)
                ch.n += NT
                dve.wait_ge(xc, ch.n)


def experts(nc, a, sem, xs, y, st, scalars, scale, mhalf, slot, xT, ident, identb, slots,
            wg, wu, wd, gw, gbias, esel_f, esel, moe_in, carried):
    mean, var, tmp, rstd = scalars
    NG, TOPK, BIG = 4, 8, 3.0e38
    EG = E // NG
    with ExitStack() as l4:
        def sb4(name, shape, dt=F32):
            return l4.enter_context(nc.sbuf_tensor(name, shape, dt))
        xnT = sb4("xnT_all", [P, B * N])
        sc = sb4("sc", [P, NT, E])
        cho = sb4("cho", [P, NT, E])
        work = sb4("work", [P, NT, E])
        eq = sb4("eq", [P, NT, E])
        m1 = sb4("m1", [P, NT * NG])
        m2 = sb4("m2", [P, NT * NG])
        cnt = sb4("cnt", [P, NT * NG])
        rank = sb4("rank", [P, NT, NG])
        cmp = sb4("cmp", [P, NT, NG])
        top8 = sb4("top8", [P, NT, TOPK])
        wsum = sb4("wsum", [P, NT])
        wparts = sb4("wparts", [P, NT, 3, E], BF16)
        wT = sb4("wT", [3 * E, B * N], BF16)
        silu = sb4("silu", [P, 2, CH])
        prod = sb4("prod", [P, 2, CH])
        hT = sb4("hT", [P, 2, CH])
        fT = sb4("fT", [P, CH])
        pc, chain = sem("l4_pc"), sem("l4_chain")
        with nc.Block() as block:
            @block.gpsimd
            def _(pool):
                pool.wait_ge(pc, 1)
                pool.tensor_tensor(rstd, scale, mhalf[:, 0:NT], ALU.pow).then_inc(pc, 1)

            @block.vector
            def _(dve):
                ch = Chain(dve, chain)
                mean_rstd(dve, None, ch, st, mean, var, tmp)
                dve.tensor_scalar(scale, var, 1e-5, None, ALU.add).then_inc(pc, 1)
                dve.wait_ge(moe_in, 16 * 6)
                ch(dve.tensor_copy(esel[:], esel_f[:]))
                dve.wait_ge(pc, 2)

        with ExitStack() as pctx, nc.Block() as block:
            ps_t = [pctx.enter_context(nc.psum_tensor(f"p4_t{s}", [P, CH], F32)) for s in range(2)]
            ps_l = [pctx.enter_context(nc.psum_tensor(f"p4_l{s}", [P, CH], F32)) for s in range(2)]
            xn_ready, t_ready, t_copied, l_ready, all_copied = (
                slots("p4_" + n) for n in ("xn", "t", "tc", "l", "all"))
            sig_done = sem("p4_sig")

            @block.vector
            def _(dve):
                with dve.Fori(0, NC // 2) as k:
                    for s in range(2):
                        dve.wait_ge(t_ready[s], k)
                        for t in range(CT):
                            i = CT * (2 * k + s) + t
                            last = dve.tensor_scalar(slot[:, s, t, :], xs[:, bass.ds(i, 1), :].rearrange("p a d -> p (a d)"),
                                                     mean[:, bass.ds(i, 1)], rstd[:, bass.ds(i, 1)],
                                                     ALU.subtract, ALU.mult)
                        last.then_inc(xn_ready[s], 1)

            @block.tensor
            def _(pe):
                def front(c, s, used):
                    pe.wait_ge(xn_ready[s], used + 1)
                    pe.wait_ge(t_copied[s], used)
                    for t in range(CT):
                        last = pe.transpose(ps_t[s][:, t * P:(t + 1) * P], slot[:, s, t, :], ident[:])
                    last.then_inc(t_ready[s], 1)

                def back(c, s, used):
                    pe.wait_ge(t_copied[s], used + 1)
                    for t in range(CT):
                        last = pe.matmul(ps_l[s][:, t * E:(t + 1) * E], xT[:, s, t * P:(t + 1) * P], gw[:],
                                         start=True, stop=True)
                    last.then_inc(l_ready[s], 1)

                pipelined(pe, front, back, NC, 0)

            @block.scalar
            def _(act):
                def front(c, s, used):
                    act.wait_ge(t_ready[s], used + 1)
                    act.wait_ge(l_ready[s], used)
                    act.wait_ge(all_copied[s], used)
                    act.copy(xT[:, s, :], ps_t[s][:]).then_inc(t_copied[s], 1)

                def back(c, s, used):
                    act.wait_ge(l_ready[s], used + 1)
                    act.sem_inc(carried, 1)
                    act.activation(sc[:, bass.ds(CT * c, CT), :].rearrange("p t e -> p (t e)"),
                                   ps_l[s][:, 0:CT * E], ACT.Sigmoid).then_inc(sig_done, 1)

                pipelined(act, front, back, NC, 0)

            @block.gpsimd
            def _(pool):
                with pool.Fori(0, NC // 2) as k:
                    for s in range(2):
                        pool.wait_ge(t_copied[s], k + 1)
                        pool.sem_inc(carried, 1)
                        pool.tensor_copy(xnT[:, bass.ds((2 * k + s) * CH, CH)], xT[:, s, :]).then_inc(all_copied[s], 1)

        with ExitStack() as pctx, nc.Block() as block:
            ps_w = [pctx.enter_context(nc.psum_tensor(f"p4_w{s}", [P, 1024], BF16)) for s in range(2)]
            wp_ready, w_ready, w_copied = sem("p4_wp"), sem("p4_w"), sem("p4_wc")
            rc = sem("p4_rc")

            @block.vector
            def _(dve):
                ch = Chain(dve, rc)

                def g3(v):
                    return v[:].rearrange("p t (g e) -> p (t g) e", g=NG)

                def gb3(v):
                    return v[:].rearrange("p (n a) -> p n a", a=1).to_broadcast([P, NT * NG, EG])

                ch(dve.tensor_tensor(cho[:], sc[:],
                                     gbias[:].rearrange("p (a e) -> p a e", a=1).to_broadcast([P, NT, E]), ALU.add))
                ch(dve.tensor_reduce(m1[:], g3(cho), AX.X, ALU.max))
                ch(dve.tensor_tensor(g3(eq), g3(cho), gb3(m1), ALU.is_equal))
                ch(dve.tensor_reduce(cnt[:], g3(eq), AX.X, ALU.add))
                ch(dve.scalar_tensor_tensor(work[:], eq[:], -BIG, cho[:], ALU.mult, ALU.add))
                ch(dve.tensor_reduce(m2[:], g3(work), AX.X, ALU.max))
                ch(dve.tensor_scalar(cnt[:], cnt[:], 1.5, None, ALU.is_gt))
                ch(dve.copy_predicated(m2[:], cnt[:].bitcast(I32), m1[:]))
                ch(dve.tensor_tensor(m1[:], m1[:], m2[:], ALU.add))
                gs = m1[:].rearrange("p (t g) -> p t g", g=NG)
                ch(dve.memset(rank[:], 0.0))
                for j in range(NG):
                    other = gs[:, :, j:j + 1]
                    if j + 1 < NG:
                        ch(dve.tensor_tensor(cmp[:, :, j + 1:NG], other.to_broadcast([P, NT, NG - j - 1]),
                                             gs[:, :, j + 1:NG], ALU.is_ge))
                    if j:
                        ch(dve.tensor_tensor(cmp[:, :, 0:j], other.to_broadcast([P, NT, j]), gs[:, :, 0:j], ALU.is_gt))
                    ch(dve.memset(cmp[:, :, j:j + 1], 0.0))
                    ch(dve.tensor_tensor(rank[:], rank[:], cmp[:], ALU.add))
                ch(dve.tensor_scalar(rank[:], rank[:], 1.5, None, ALU.is_lt))
                ch(dve.tensor_tensor(g3(work), g3(cho),
                                     rank[:].rearrange("p t (g a) -> p (t g) a", a=1).to_broadcast([P, NT * NG, EG]),
                                     ALU.mult))
                for t in range(NT):
                    dve.max(top8[:, t, :], work[:, t, :]).then_inc(rc, 1)
                ch.n += NT
                dve.wait_ge(rc, ch.n)
                for t in range(NT):
                    dve.match_replace(eq[:, t, :], top8[:, t, :], work[:, t, :], BIG).then_inc(rc, 1)
                ch.n += NT
                dve.wait_ge(rc, ch.n)
                ch(dve.tensor_scalar(eq[:], eq[:], BIG, None, ALU.is_ge))
                ch(dve.tensor_tensor(sc[:], sc[:], eq[:], ALU.mult))
                ch(dve.tensor_reduce(wsum[:], sc[:], AX.X, ALU.add))
                ch(dve.tensor_scalar(wsum[:], wsum[:], 1e-20, None, ALU.add))
                ch(dve.reciprocal(wsum[:], wsum[:]))
                ch(dve.tensor_scalar(wsum[:], wsum[:], 2.5, None, ALU.mult))
                ch(dve.tensor_tensor(sc[:], sc[:], wsum[:].rearrange("p (t a) -> p t a", a=1)
                                     .to_broadcast([P, NT, E]), ALU.mult))
                ch(dve.tensor_copy(wparts[:, :, 0, :], sc[:]))
                ch(dve.tensor_tensor(sc[:], sc[:], wparts[:, :, 0, :], ALU.subtract))
                ch(dve.tensor_copy(wparts[:, :, 1, :], sc[:]))
                dve.tensor_tensor(wparts[:, :, 2, :], sc[:], wparts[:, :, 1, :], ALU.subtract).then_inc(wp_ready, 1)

            @block.tensor
            def _(pe):
                pe.wait_ge(wp_ready, 1)
                for t in range(NT):
                    g = t // 8
                    if t % 8 == 0 and g >= 2:
                        pe.wait_ge(w_copied, g - 1)
                    pe.transpose(ps_w[g % 2][0:3 * E, (t % 8) * P:(t % 8 + 1) * P],
                                 wparts[:, t, :, :].rearrange("p j e -> p (j e)"), identb[:]).then_inc(w_ready, 1)

            @block.scalar
            def _(act):
                for g in range(NT // 8):
                    act.wait_ge(w_ready, 8 * (g + 1))
                    act.copy(wT[:, g * 1024:(g + 1) * 1024], ps_w[g % 2][0:3 * E, :]).then_inc(w_copied, 1)

        with ExitStack() as pctx, nc.Block() as block:
            def pt(name):
                return [pctx.enter_context(nc.psum_tensor(f"{name}{s}", [P, CH], F32)) for s in range(2)]
            ps_g, ps_u, ps_w = pt("p5_g"), pt("p5_u"), pt("p5_w")
            ps_f = pctx.enter_context(nc.psum_tensor("p5_f", [P, CH], F32))
            ps_t = pctx.enter_context(nc.psum_tensor("p5_t", [P, CH], F32))
            g_ready, u_ready, w_ready, silu_done, prod_done, h_done, down_done = (
                slots("p5_" + n) for n in ("g", "u", "w", "silu", "prod", "h", "down"))
            f_copied, ft_ready, ft_copied, stat = sem("p5_fc"), sem("p5_ft"), sem("p5_ftc"), sem("p5_stat")
            USES = (EALL - EALL // 2, EALL // 2)

            def uses(c, e):
                return e % 2, c * USES[e % 2] + e // 2

            def w_uses(c, e):
                return c * (EP // 2) + e // 2

            @block.tensor
            def _(pe):
                def down(c, e):
                    s, n = uses(c, e)
                    pe.wait_ge(h_done[s], n + 1)
                    pe.matmul(ps_f[:], wd[:, e, :], hT[:, s, :], start=(e == 0), stop=(e == EP)) \
                        .then_inc(down_done[s], 1)

                with pe.Fori(0, NC) as c:
                    x_c = xnT[:, bass.ds(c * CH, CH)]
                    for e in range(EALL):
                        s, n = uses(c, e)
                        pe.wait_ge(silu_done[s], n)
                        pe.matmul(ps_g[s][:], wg[:, e * P:(e + 1) * P], x_c, start=True, stop=True) \
                            .then_inc(g_ready[s], 1)
                        pe.wait_ge(prod_done[s], n)
                        pe.matmul(ps_u[s][:], wu[:, e * P:(e + 1) * P], x_c, start=True, stop=True) \
                            .then_inc(u_ready[s], 1)
                        if e < EP:
                            pe.wait_ge(h_done[s], n)
                            pe.matmul(ps_w[s][:], esel[:, e * P:(e + 1) * P], wT[:, bass.ds(c * CH, CH)],
                                      start=True, stop=True).then_inc(w_ready[s], 1)
                        if e == 1:
                            pe.wait_ge(f_copied, c)
                        if e >= 1:
                            down(c, e - 1)
                    down(c, EP)
                    pe.wait_ge(f_copied, c + 1)
                    pe.wait_ge(ft_copied, c)
                    for t in range(CT):
                        last = pe.transpose(ps_t[:, t * P:(t + 1) * P], fT[:, t * P:(t + 1) * P], ident[:])
                    last.then_inc(ft_ready, 1)

            @block.scalar
            def _(act):
                with act.Fori(0, NC) as c:
                    for e in range(EALL):
                        s, n = uses(c, e)
                        act.wait_ge(g_ready[s], n + 1)
                        act.wait_ge(prod_done[s], n)
                        act.activation(silu[:, s, :], ps_g[s][:], ACT.Silu).then_inc(silu_done[s], 1)
                    s, n = uses(c, EP)
                    act.wait_ge(down_done[s], n + 1)
                    act.wait_ge(ft_ready, c)
                    act.copy(fT[:], ps_f[:]).then_inc(f_copied, 1)
                    act.wait_ge(ft_ready, c + 1)
                    act.sem_inc(carried, 1)
                    act.copy(y[:, bass.ds(CT * c, CT), :].rearrange("p t d -> p (t d)"), ps_t[:]) \
                        .then_inc(ft_copied, 1)

            @block.vector
            def _(dve):
                with dve.Fori(0, NC) as c:
                    for e in range(EALL):
                        s, n = uses(c, e)
                        dve.wait_ge(silu_done[s], n + 1)
                        dve.wait_ge(u_ready[s], n + 1)
                        if e < EP:
                            dve.tensor_tensor(prod[:, s, :], ps_u[s][:], silu[:, s, :], ALU.mult) \
                                .then_inc(prod_done[s], 1)
                            dve.wait_ge(prod_done[s], n + 1)
                            dve.wait_ge(w_ready[s], w_uses(c, e) + 1)
                            dve.wait_ge(down_done[s], n)
                            dve.tensor_tensor(hT[:, s, :], ps_w[s][:], prod[:, s, :], ALU.mult) \
                                .then_inc(h_done[s], 1)
                        else:
                            dve.wait_ge(down_done[s], n)
                            dve.tensor_tensor(prod[:, s, :], ps_u[s][:], silu[:, s, :], ALU.mult) \
                                .then_inc(prod_done[s], 1)
                            dve.wait_ge(prod_done[s], n + 1)
                            dve.tensor_copy(hT[:, s, :], prod[:, s, :]).then_inc(h_done[s], 1)
                    dve.wait_ge(ft_copied, c + 1)
                    for t in range(CT):
                        dve.bn_stats(st[:, bass.ds(CT * c + t, 1), :], y[:, bass.ds(CT * c + t, 1), :]) \
                            .then_inc(stat, 1)
                dve.wait_ge(stat, NT)


def program(nc, a, out):
    with ExitStack() as ctx:
        def sb(name, shape, dt):
            return ctx.enter_context(nc.sbuf_tensor(name, shape, dt))

        xs = sb("xs", [P, NT, P], F32)
        o_all = sb("o_all", [P, B * H * NQC * CT, DV], F32)
        ident = sb("ident_sb", [P, P], F32)
        identb = sb("identb", [P, P], BF16)
        with Semaphores(nc) as sem:
            attention_layer(nc, a, sb, None, sem, xs, o_all, ident, identb)
        with Semaphores(nc) as sem:
            later_layers(nc, a, sem, xs, o_all, ident, identb, out)


def kernel(**inputs):
    import numpy as np
    import concourse.bacc as bacc
    from concourse.bass_utils import run_bass_kernel_spmd

    f = {k: np.asarray(v) for k, v in inputs.items()}
    sel = np.zeros((P, DV + 1), np.float32)
    for base in (0, VC):
        for r in range(3 * DV):
            sel[base + r, r % DV] = 1
        sel[base + 3 * DV, DV] = 1
    esel = np.zeros((3 * E, EP * P), np.float32)
    for r in range(3 * E):
        esel[r, (r % E) * (P // 2):(r % E + 1) * (P // 2)] = 1
    tiles = lambda w: np.ascontiguousarray(w.reshape(-1, P, w.shape[-1]).transpose(1, 0, 2))
    arrays = {
        "x": f["L0_attn_x"].reshape(B * N, P),
        "wqkv": np.concatenate([f["L0_attn_Wq"], f["L0_attn_Wk"], f["L0_attn_Wv"]], 1),
        "sel": sel, "ident": np.eye(P, dtype=np.float32),
        "lqk": np.stack([f["L0_attn_" + k] for k in ("lq1", "lk1", "lq2", "lk2")]),
        "wo": f["L0_attn_Wo"],
        "lng": np.tile(f["L0_attn_ln_g"], H)[:, None], "lnb": np.tile(f["L0_attn_ln_b"], H)[:, None],
        "up": f["L0_ffn_w_up"].T, "down": tiles(f["L0_ffn_w_down"].T),
        "kw": tiles(f["L1_attn_k_weight"]), "qw": tiles(f["L1_attn_q_weight"]),
        "bias3": f["L1_attn_bias"], "w3": f["L1_attn_ln_weight"], "b3": f["L1_attn_ln_bias"],
        "gw": f["L1_ffn_gate_w"].T, "gb": f["L1_ffn_gate_bias"], "esel": esel,
        "wg": np.concatenate([f["L1_ffn_expert_gate"].reshape(-1, P), f["L1_ffn_shared_gate"]]).T,
        "wu": np.concatenate([f["L1_ffn_expert_up"].reshape(-1, P), f["L1_ffn_shared_up"]]).T,
        "wd": tiles(np.concatenate([f["L1_ffn_expert_down"].transpose(0, 2, 1).reshape(-1, P),
                                    f["L1_ffn_shared_down"].T])),
    }
    arrays = {k: np.ascontiguousarray(v) for k, v in arrays.items()}
    nc = bacc.Bacc("TRN2", target_bir_lowering=False, num_devices=1)
    a = {k: nc.dram_tensor("in_" + k, v.shape, F32, kind="ExternalInput").ap() for k, v in arrays.items()}
    a["x"] = a["x"].rearrange("(t p) d -> p t d", p=P)
    out = nc.dram_tensor("out", (B * N, P), F32, kind="ExternalOutput").ap()
    program(nc, a, out.rearrange("(t p) d -> p t d", p=P))
    r = run_bass_kernel_spmd(nc, [{"in_" + k: v for k, v in arrays.items()}], core_ids=[0])
    return r.results[0]["out"].reshape(B, N, P)
```

```python
import concourse.bass as bass
from concourse import mybir
from contextlib import ExitStack

F32 = mybir.dt.float32
BF16 = mybir.dt.bfloat16
I32 = mybir.dt.int32
ALU = mybir.AluOpType
ACT = mybir.ActivationFunctionType
AX = mybir.AxisListType
RMAX = bass.bass_isa.ReduceOp.max
RADD = bass.bass_isa.ReduceOp.add

P = 128
B = 2
N = 2048
NT = B * N // P
TB = NT // B
H = 8
S2 = 16
D = 8
DV = 16
ROW = 64
NSPLIT = 6
SH = NSPLIT * D
VC = 64
NQC = 4
KT = 16
RING = 4
SAFE = 40.0
ONE = 1
LAM_INIT = 0.8 - 0.6 * 2.718281828459045 ** (-0.3 * 12)


class Chain:

    def __init__(self, eng, sem, base=0):
        self.eng, self.sem, self.base, self.n = eng, sem, base, 0

    def __call__(self, ins):
        self.n += 1
        ins.then_inc(self.sem, 1)
        self.eng.wait_ge(self.sem, self.base + self.n)


class Semaphores:

    def __init__(self, nc):
        self.nc = nc

    def __enter__(self):
        self.handles, self.from_one = [], []
        return self

    def __call__(self, name, start=0):
        self.handles.append(self.nc.alloc_semaphore(name=name))
        if start == ONE:
            self.from_one.append(self.handles[-1])
        return self.handles[-1]

    def start(self, eng):
        for handle in self.from_one:
            eng.sem_inc(handle, ONE)
        self.from_one = []

    def __exit__(self, *_):
        with self.nc.Block() as block:
            @block.gpsimd
            def _(pool):
                for handle in self.handles:
                    pool.sem_clear(handle)
        for handle in self.handles:
            self.nc.release_semaphore(handle)


def pipelined(eng, front, back, n, base):
    half = n // 2
    front(0, 0, base)
    with eng.Fori(0, half - 1) as k:
        front(2 * k + 1, 1, base + k)
        back(2 * k, 0, base + k)
        front(2 * k + 2, 0, base + k + 1)
        back(2 * k + 1, 1, base + k)
    front(n - 1, 1, base + half - 1)
    back(n - 2, 0, base + half - 1)
    back(n - 1, 1, base + half - 1)


def pipelined3(eng, first, second, third, n):
    half = n // 2
    first(0, 0, 0)
    first(1, 1, 0)
    second(0, 0, 0)
    with eng.Fori(0, half - 1) as k:
        first(2 * k + 2, 0, k + 1)
        second(2 * k + 1, 1, k)
        third(2 * k, 0, k)
        first(2 * k + 3, 1, k + 1)
        second(2 * k + 2, 0, k + 1)
        third(2 * k + 1, 1, k)
    second(n - 1, 1, half - 1)
    third(n - 2, 0, half - 1)
    third(n - 1, 1, half - 1)


def tiles(eng):
    with eng.Fori(0, NT // 8) as k:
        for j in range(8):
            yield lambda v: v[:, bass.ds(8 * k, 8)][:, j:j + 1]


def mean_rstd(dve, pool_pow, ch, st, mean, var, tmp):
    ch(dve.tensor_tensor(mean, st[:, :, 1], st[:, :, 4], ALU.add))
    ch(dve.tensor_scalar(mean, mean, 0.5, None, ALU.mult))
    ch(dve.tensor_tensor(tmp, st[:, :, 1], mean, ALU.subtract))
    ch(dve.tensor_tensor(tmp, tmp, tmp, ALU.mult))
    ch(dve.tensor_tensor(var, st[:, :, 2], st[:, :, 5], ALU.add))
    ch(dve.tensor_scalar(var, var, 1.0 / P, None, ALU.mult))
    ch(dve.tensor_tensor(var, var, tmp, ALU.add))


def attention_layer(nc, a, sb, pb, sem, xs, o_all, ident, identb, DEBUG=None):
    with ExitStack() as ctx:
        def sbt(name, shape, dt):
            return ctx.enter_context(nc.sbuf_tensor(name, shape, dt))

        xn = sbt("xn", [P, NT, P], F32)
        wqkv = sbt("wqkv_sb", [P, 3 * P], F32)
        sel = sbt("sel_sb", [P, DV + 1], F32)
        lqk = sbt("lqk_sb", [P, 4, D], F32)
        lam = sbt("lam", [P, 1], F32)
        lam4 = sbt("lam4", [P, 6], F32)
        st = sbt("st", [P, NT, 6], F32)
        mean = sbt("mean", [P, NT], F32)
        var = sbt("var", [P, NT], F32)
        vtmp = sbt("vtmp", [P, NT], F32)
        rstd = sbt("rstd", [P, NT], F32)
        xslot = sbt("xslot", [P, 2, P], F32)
        xnT = sbt("xnT", [P, 2, P], F32)
        qkv = sbt("qkv", [P, 2, 3 * P], F32)
        rest = sbt("rest", [P, 2, 3 * P], F32)
        parts = sbt("parts", [P, 2, 3, 3 * P], BF16)
        q_rows = sbt("q_rows", [P, 2, S2, ROW], BF16)
        k_rows = sbt("k_rows", [P, 2, S2, ROW], BF16)
        sq = sbt("sq", [P, 2, 2 * P], F32)
        norms = sbt("norms", [P, TB, 2 * S2], F32)
        nmax = sbt("nmax", [P, 2 * S2], F32)
        nall = sbt("nall", [P, 2 * S2], F32)
        bound = sbt("bound", [P, 2], F32)
        state = sbt("state", [P, 2], F32)
        state_i = sbt("state_i", [P, 2], I32)
        QT = sbt("QT", [P, H, N], BF16)
        KTa = sbt("KTa", [P, H, N], BF16)
        V = sbt("V", [P, TB, H, VC], BF16)
        kts = sbt("kts", [P, N], BF16)
        qts = sbt("qts", [P, 2, 2, 512], BF16)
        vts = sbt("vts", [P, KT, VC], BF16)
        V32 = sbt("V32", [P, TB // 2, P], F32)
        vts32 = sbt("vts32", [P, KT // RING, VC], F32)
        prob = sbt("prob", [P, RING, 1024], F32)
        low = sbt("low", [P, RING - 1, 1024], BF16)
        stack = sbt("stack", [P, 1024], F32)
        rec = sbt("rec", [P, 8], F32)
        onrm = sbt("onrm", [P, 8, DV], F32)
        ot = sbt("ot", [P, 4, DV], F32)
        shift = sbt("shift", [P, TB, S2], F32)
        shparts = sbt("shparts", [P, TB, 3, S2], BF16)

        loaded = sem("attn_loaded")
        dve_done = sem("a_dve")
        preset = sem("a_preset")
        mv_ready = sem("a_mv_ready")
        lam_sum = sem("lam_sum")
        lam_exp = sem("lam_exp")
        rstd_done = sem("a_rstd")
        pool_done = sem("a_pool")

        x_in = [sem(f"x_in{s}") for s in range(2)]
        xT_ready = [sem(f"xT_ready{s}", ONE) for s in range(2)]
        xT_copied = [sem(f"xT_copied{s}", ONE) for s in range(2)]
        qkv_ready = [sem(f"qkv_ready{s}") for s in range(2)]
        qkv_copied = [sem(f"qkv_copied{s}") for s in range(2)]
        squared = [sem(f"squared{s}", ONE) for s in range(2)]
        split_done = [sem(f"split_done{s}", ONE) for s in range(2)]
        build_chain = sem("build_chain")
        norms_done = [sem(f"norms_done{s}", ONE) for s in range(2)]
        q_rows_done = [sem(f"q_rows_done{s}", ONE) for s in range(2)]
        k_rows_done = [sem(f"k_rows_done{s}", ONE) for s in range(2)]
        v_done = [sem(f"v_done{s}", ONE) for s in range(2)]
        qT_ready = [sem(f"qT_ready{s}", ONE) for s in range(2)]
        kT_ready = [sem(f"kT_ready{s}", ONE) for s in range(2)]
        qT_copied = [sem(f"qT_copied{s}", ONE) for s in range(2)]
        kT_copied = [sem(f"kT_copied{s}", ONE) for s in range(2)]
        nmax_ready = sem("nmax_ready")
        carried = sem("carried")
        nall_ready = sem("nall_ready")
        bound_chain = sem("bound_chain")

        keys_masked = sem("keys_masked")
        all_scores = [sem(f"all_scores{s}") for s in range(2)]
        max_taken = [sem(f"max_taken{s}", ONE) for s in range(2)]
        shift_chain = sem("shift_chain")
        shift_split = sem("shift_split")
        shift_T = sem("shift_T")
        shift_copied = sem("shift_copied")
        shift_rows = sem("shift_rows")

        q_in = [sem(f"q_in{r}") for r in range(2)]
        k_in = [sem(f"k_in{c}") for c in range(4)]
        v_in = [sem(f"v_in{c}") for c in range(4)]
        q_free = [sem(f"q_free{r}", ONE) for r in range(2)]
        k_free = [sem(f"k_free{c}", ONE) for c in range(4)]
        v_free = [sem(f"v_free{c}", ONE) for c in range(4)]
        scores_ready = [sem(f"scores_ready{s}") for s in range(2)]
        exp_done = [sem(f"exp_done{s}", ONE) for s in range(RING)]
        low_done = [sem(f"low_done{s}") for s in range(RING - 1)]
        pv_done = [sem(f"pv_done{s}", ONE) for s in range(RING)]
        evac0 = sem("evac0", ONE)
        evac1 = sem("evac1", ONE)
        t_ready = sem("t_ready", ONE)
        norm_chain = sem("norm_chain", ONE)

        with nc.Block() as block:
            @block.sync
            def _(sp):
                for c in range(4):
                    sp.dma_start(xs[:, 8 * c:8 * c + 8, :], a["x"][:, 8 * c:8 * c + 8, :]).then_inc(loaded, 16)
                sp.dma_start(wqkv[:], a["wqkv"]).then_inc(loaded, 16)
                sp.dma_start(sel[:], a["sel"]).then_inc(loaded, 16)
                sp.dma_start(ident[:], a["ident"]).then_inc(loaded, 16)
                sp.dma_start(lqk[:], a["lqk"].partition_broadcast(P)).then_inc(loaded, 16)

            @block.gpsimd
            def _(pool):
                pool.memset(q_rows[:], 0.0).then_inc(preset, 1)
                pool.memset(k_rows[:], 0.0).then_inc(preset, 1)
                pool.memset(V[:], 0.0).then_inc(preset, 1)
                pool.memset(qts[:], 0.0).then_inc(preset, 1)
                pool.memset(vts32[:], 0.0).then_inc(preset, 1)
                pool.wait_ge(preset, 5)
                pool.memset(vts32[:, :, 3 * DV:3 * DV + 1], 1.0).then_inc(preset, 1)
                pool.memset(k_rows[:, :, :, SH:SH + 3], 1.0).then_inc(preset, 1)
                pool.memset(V[:, :, :, 3 * DV:3 * DV + 1], 1.0).then_inc(preset, 1)
                sem.start(pool)

            @block.scalar
            def _(act):
                act.wait_ge(lam_sum, 1)
                act.activation(lam4[:, 2:4], lam4[:, 0:2], ACT.Exp).then_inc(lam_exp, 1)
                act.wait_ge(mv_ready, 1)
                act.activation(rstd[:], var[:], ACT.Sqrt).then_inc(rstd_done, 1)

            @block.vector
            def _(dve):
                ch = Chain(dve, dve_done)
                dve.wait_ge(loaded, 16 * 8)
                ch(dve.tensor_copy(identb[:], ident[:]))
                ch(dve.memset(state[:], 0.0))
                ch(dve.tensor_tensor(lqk[:, 0::2, :], lqk[:, 0::2, :], lqk[:, 1::2, :], ALU.mult))
                dve.tensor_reduce(lam4[:, 0:2], lqk[:, 0::2, :], AX.X, ALU.add).then_inc(lam_sum, 1)
                for tile in tiles(dve):
                    dve.bn_stats(tile(st), tile(xs)).then_inc(dve_done, 1)
                ch.n += NT
                dve.wait_ge(dve_done, ch.n)
                mean_rstd(dve, None, ch, st, mean[:], var[:], vtmp[:])
                dve.tensor_scalar(var[:], var[:], 1e-5, None, ALU.add).then_inc(mv_ready, 1)
                dve.wait_ge(lam_exp, 1)
                ch(dve.tensor_tensor(lam4[:, 4:5], lam4[:, 2:3], lam4[:, 3:4], ALU.subtract))
                ch(dve.tensor_scalar(lam[:], lam4[:, 4:5], LAM_INIT, None, ALU.add))
                dve.wait_ge(rstd_done, 1)
                ch(dve.reciprocal(rstd[:], rstd[:]))
                for tile in tiles(dve):
                    dve.tensor_scalar(tile(xn), tile(xs), tile(mean),
                                      tile(rstd), ALU.subtract, ALU.mult).then_inc(dve_done, 1)
                ch.n += NT
                dve.wait_ge(dve_done, ch.n)

        with nc.Fori(0, B) as b:
            with ExitStack() as pctx, nc.Block() as block:
                def pt(name, shape, dt):
                    return pctx.enter_context(nc.psum_tensor(name, shape, dt))
                ps_x = [pt(f"ps_x{s}", [P, 512], F32) for s in range(2)]
                ps_qkv = [pt(f"ps_qkv{s}", [P, 512], F32) for s in range(2)]
                ps_q = [pt(f"ps_q{s}", [P, 1024], BF16) for s in range(2)]
                ps_k = [pt(f"ps_k{s}", [P, 1024], BF16) for s in range(2)]
                HB = TB // 2

                def row_groups(rows, s, lo, hi, step):
                    return rows[:, s, :, :].rearrange("p n (g d) -> p n g d", d=D)[:, :, lo:hi:step, :]

                def part_groups(s, j, o, n):
                    return parts[:, s, j, o * P:(o + 1) * P].rearrange("p (n a d) -> p n a d", a=1, d=D) \
                        .to_broadcast([P, S2, n, D])

                @block.sync
                def _(sp):
                    with sp.Fori(0, HB) as k:
                        for s in range(2):
                            sp.wait_ge(xT_ready[s], ONE + b * HB + k)
                            sp.dma_start(xslot[:, s, :], xn[:, bass.ds(b * TB + 2 * k + s, 1), :]
                                         .rearrange("p a d -> p (a d)")).then_inc(x_in[s], 16)

                @block.tensor
                def _(pe):
                    def front(t, s, used):
                        pe.wait_ge(x_in[s], 16 * (used + 1))
                        pe.wait_ge(xT_copied[s], ONE + used)
                        pe.transpose(ps_x[s][:, 0:P], xslot[:, s, :], ident[:]).then_inc(xT_ready[s], 1)
                        pe.wait_ge(xT_copied[s], ONE + used + 1)
                        pe.wait_ge(squared[s], ONE + used)
                        pe.matmul(ps_qkv[s][:, 0:3 * P], xnT[:, s, :], wqkv[:], start=True, stop=True) \
                            .then_inc(qkv_ready[s], 1)

                    def back(t, s, used):
                        pe.wait_ge(q_rows_done[s], ONE + used + 1)
                        pe.wait_ge(qT_copied[s], ONE + used)
                        for h in range(H):
                            last = pe.transpose(ps_q[s][:, h * P:(h + 1) * P],
                                                q_rows[:, s, 2 * h:2 * h + 2, :].rearrange("p a r -> p (a r)"),
                                                identb[:])
                        last.then_inc(qT_ready[s], 1)
                        pe.wait_ge(k_rows_done[s], ONE + used + 1)
                        pe.wait_ge(kT_copied[s], ONE + used)
                        for h in range(H):
                            last = pe.transpose(ps_k[s][:, h * P:(h + 1) * P],
                                                k_rows[:, s, 2 * h:2 * h + 2, :].rearrange("p a r -> p (a r)"),
                                                identb[:])
                        last.then_inc(kT_ready[s], 1)

                    pipelined(pe, front, back, TB, b * HB)

                @block.scalar
                def _(act):
                    def front(t, s, used):
                        act.wait_ge(xT_ready[s], ONE + used + 1)
                        act.copy(xnT[:, s, :], ps_x[s][:, 0:P]).then_inc(xT_copied[s], 1)
                        act.wait_ge(qkv_ready[s], used + 1)
                        act.wait_ge(split_done[s], ONE + used)
                        act.wait_ge(norms_done[s], ONE + used)
                        if s == 1:
                            act.wait_ge(v_done[s], ONE + used)
                        act.mul(qkv[:, s, 0:P], ps_qkv[s][:, 0:P], D ** -0.5).then_inc(qkv_copied[s], 1)
                        act.copy(qkv[:, s, P:3 * P], ps_qkv[s][:, P:3 * P]).then_inc(qkv_copied[s], 1)
                        act.wait_ge(qkv_copied[s], 2 * (used + 1))
                        act.activation(sq[:, s, :], qkv[:, s, 0:2 * P], ACT.Square).then_inc(squared[s], 1)

                    def back(t, s, used):
                        act.wait_ge(split_done[s], ONE + used + 1)
                        act.wait_ge(kT_ready[s], ONE + used)
                        for n, (j, lo, hi, step) in enumerate(((0, 0, 4, 3), (0, 5, 6, 1), (1, 1, 5, 3), (2, 2, 3, 1))):
                            last = act.copy(row_groups(k_rows, s, lo, hi, step), part_groups(s, j, 1, (hi - lo + step - 1) // step))
                        last.then_inc(k_rows_done[s], 1)

                    pipelined(act, front, back, TB, b * HB)

                @block.vector
                def _(dve):
                    def front(t, s, used):
                        c = (b * TB + t) * 3
                        dve.wait_ge(qkv_copied[s], 2 * (used + 1))
                        dve.wait_ge(q_rows_done[s], ONE + used)
                        dve.wait_ge(k_rows_done[s], ONE + used)
                        dve.wait_ge(v_done[s], ONE + used)
                        hi, mid, lo = (parts[:, s, k, :] for k in range(3))
                        dve.tensor_copy(hi, qkv[:, s, :]).then_inc(build_chain, 1)
                        dve.wait_ge(build_chain, c + 1)
                        dve.tensor_tensor(rest[:, s, :], qkv[:, s, :], hi, ALU.subtract).then_inc(build_chain, 1)
                        dve.wait_ge(build_chain, c + 2)
                        dve.tensor_copy(mid, rest[:, s, :]).then_inc(build_chain, 1)
                        dve.wait_ge(build_chain, c + 3)
                        dve.tensor_tensor(lo, rest[:, s, :], mid, ALU.subtract).then_inc(split_done[s], 1)
                        dve.wait_ge(squared[s], ONE + used + 1)
                        dve.tensor_reduce(norms[:, bass.ds(t, 1), :].rearrange("p a n -> p (a n)"),
                                          sq[:, s, :].rearrange("p (n d) -> p n d", d=D), AX.X, ALU.add) \
                            .then_inc(norms_done[s], 1)

                    def back(t, s, used):
                        dve.wait_ge(qT_ready[s], ONE + used + 1)
                        dve.tensor_copy(QT[:, :, bass.ds(t * P, P)],
                                        ps_q[s][:].rearrange("p (h t) -> p h t", h=H)).then_inc(qT_copied[s], 1)
                        dve.wait_ge(kT_ready[s], ONE + used + 1)
                        dve.tensor_copy(KTa[:, :, bass.ds(t * P, P)],
                                        ps_k[s][:].rearrange("p (h t) -> p h t", h=H)).then_inc(kT_copied[s], 1)

                    pipelined(dve, front, back, TB, b * HB)
                    dve.wait_ge(norms_done[0], ONE + (b + 1) * HB)
                    dve.wait_ge(norms_done[1], ONE + (b + 1) * HB)
                    dve.tensor_reduce(nmax[:], norms[:].rearrange("p t n -> p n t"), AX.X, ALU.max) \
                        .then_inc(nmax_ready, 1)
                    dve.wait_ge(nall_ready, b + 1)
                    c = b * 8
                    dve.tensor_tensor(nall[:, 0:S2], nall[:, 0:S2], nall[:, S2:2 * S2], ALU.mult) \
                        .then_inc(bound_chain, 1)
                    dve.wait_ge(bound_chain, c + 1)
                    dve.tensor_reduce(bound[:, 0:1], nall[:, 0:S2], AX.X, ALU.max).then_inc(bound_chain, 1)
                    dve.wait_ge(bound_chain, c + 2)
                    dve.tensor_tensor(state[:, 0:1], state[:, 0:1], state[:, 1:2], ALU.add).then_inc(bound_chain, 1)
                    dve.wait_ge(bound_chain, c + 3)
                    dve.tensor_scalar(bound[:, 1:2], bound[:, 0:1], SAFE * SAFE, None, ALU.is_le) \
                        .then_inc(bound_chain, 1)
                    dve.wait_ge(bound_chain, c + 4)
                    dve.tensor_scalar(state[:, 1:2], bound[:, 1:2], -1.0, 1.0, ALU.mult, ALU.add) \
                        .then_inc(bound_chain, 1)
                    dve.wait_ge(bound_chain, c + 5)
                    dve.tensor_copy(state_i[:], state[:]).then_inc(bound_chain, 3)

                @block.gpsimd
                def _(pool):
                    with pool.Fori(0, HB) as k:
                        for s in range(2):
                            used = b * HB + k
                            t = 2 * k + s
                            pool.wait_ge(split_done[s], ONE + used + 1)
                            pool.wait_ge(qT_ready[s], ONE + used)
                            pool.sem_inc(carried, 1)
                            for j, lo, hi in ((0, 0, 3), (1, 3, 5), (2, 5, 6)):
                                last = pool.tensor_copy(row_groups(q_rows, s, lo, hi, 1), part_groups(s, j, 0, hi - lo))
                            last.then_inc(q_rows_done[s], 1)
                            if s == 1:
                                pool.tensor_copy(V32[:, bass.ds(k, 1), :].rearrange("p a n -> p (a n)"),
                                                 qkv[:, s, 2 * P:3 * P])
                            pool.tensor_copy(
                                V[:, bass.ds(t, 1), :, 0:3 * DV].rearrange("p a h (j d) -> p (a h) j d", j=3),
                                parts[:, s, :, 2 * P:3 * P].rearrange("p j (h d) -> p h j d", d=DV)) \
                                .then_inc(v_done[s], 1)
                    pool.wait_ge(nmax_ready, b + 1)
                    pool.sem_inc(carried, 1)
                    pool.partition_all_reduce(nall[:], nmax[:], P, RMAX).then_inc(nall_ready, 1)

            with ExitStack() as pctx, nc.Block() as block:
                ps_m = [pctx.enter_context(nc.psum_tensor(f"ps_m{s}", [P, N], F32)) for s in range(2)]
                HEADS = 2 * H
                PAIRS = TB // 2

                @block.tensor
                def _(pe):
                    m = pe.value_load(state_i[0:1, 0:1], min_val=0, max_val=1)
                    with pe.If(pe.value_load(state_i[0:1, 1:2], min_val=0, max_val=1) > 0):
                        for i in range(2):
                            with pe.Fori(0, H) as h:
                                head = m * HEADS + i * H + h
                                pe.wait_ge(keys_masked, head + 1)
                                pe.sem_inc(carried, 1)
                                with pe.Fori(0, PAIRS) as k:
                                    for s in range(2):
                                        pe.wait_ge(max_taken[s], ONE + head * PAIRS + k)
                                        for c in range(4):
                                            last = pe.matmul(ps_m[s][:, 512 * c:512 * (c + 1)],
                                                             QT[:, bass.ds(h, 1), bass.ds((2 * k + s) * P, P)]
                                                             .rearrange("p a n -> p (a n)"),
                                                             kts[:, 512 * c:512 * (c + 1)], start=True, stop=True)
                                        last.then_inc(all_scores[s], 1)
                        pe.wait_ge(shift_split, m + 1)
                        pe.sem_inc(carried, 1)
                        for t in range(TB):
                            last = pe.transpose(ps_m[0][0:3 * S2, t * P // 2:(t + 1) * P // 2].bitcast(BF16),
                                                shparts[:, t, :, :].rearrange("p j n -> p (j n)"), identb[:])
                        last.then_inc(shift_T, 1)

                @block.vector
                def _(dve):
                    m = dve.value_load(state_i[0:1, 0:1], min_val=0, max_val=1)
                    with dve.If(dve.value_load(state_i[0:1, 1:2], min_val=0, max_val=1) > 0):
                        for i in range(2):
                            dve.memset(kts[:], 0.0).then_inc(shift_chain, 1)
                            dve.wait_ge(shift_chain, m * 6 + i + 1)
                            dve.sem_inc(carried, 1)
                            with dve.Fori(0, H) as h:
                                head = m * HEADS + i * H + h
                                rows = slice(ROW * i, ROW * (i + 1))
                                dve.tensor_copy(kts[rows, :], KTa[rows, bass.ds(h, 1), :]
                                                .rearrange("p a n -> p (a n)")).then_inc(keys_masked, 1)
                                with dve.Fori(0, PAIRS) as k:
                                    for s in range(2):
                                        dve.wait_ge(all_scores[s], head * PAIRS + k + 1)
                                        dve.tensor_reduce(shift[:, bass.ds(2 * k + s, 1), bass.ds(i * H + h, 1)]
                                                          .rearrange("p a n -> p (a n)"),
                                                          ps_m[s][:], AX.X, ALU.max, negate=True) \
                                            .then_inc(max_taken[s], 1)
                            for s in range(2):
                                dve.wait_ge(max_taken[s], ONE + (m * HEADS + (i + 1) * H) * PAIRS)
                        dve.tensor_copy(shparts[:, :, 0, :], shift[:]).then_inc(shift_chain, 1)
                        dve.wait_ge(shift_chain, m * 6 + 3)
                        dve.tensor_tensor(shift[:], shift[:], shparts[:, :, 0, :], ALU.subtract) \
                            .then_inc(shift_chain, 1)
                        dve.wait_ge(shift_chain, m * 6 + 4)
                        dve.tensor_copy(shparts[:, :, 1, :], shift[:]).then_inc(shift_chain, 1)
                        dve.wait_ge(shift_chain, m * 6 + 5)
                        dve.tensor_tensor(shift[:], shift[:], shparts[:, :, 1, :], ALU.subtract) \
                            .then_inc(shift_chain, 1)
                        dve.wait_ge(shift_chain, m * 6 + 6)
                        dve.tensor_copy(shparts[:, :, 2, :], shift[:]).then_inc(shift_split, 1)

                @block.scalar
                def _(act):
                    m = act.value_load(state_i[0:1, 0:1], min_val=0, max_val=1)
                    with act.If(act.value_load(state_i[0:1, 1:2], min_val=0, max_val=1) > 0):
                        act.wait_ge(shift_T, m + 1)
                        act.copy(low[0:3 * S2, 0:2, :].rearrange("p r n -> p (r n)"),
                                 ps_m[0][0:3 * S2, 0:N // 2].bitcast(BF16)).then_inc(shift_copied, 1)

                @block.sync
                def _(sp):
                    m = sp.value_load(state_i[0:1, 0:1], min_val=0, max_val=1)
                    with sp.If(sp.value_load(state_i[0:1, 1:2], min_val=0, max_val=1) > 0):
                        sp.wait_ge(shift_copied, m + 1)
                        for j in range(3):
                            for i in range(2):
                                row = j * S2 + i * H
                                sp.dma_start(QT[ROW * i + SH + j:ROW * i + SH + j + 1, :, :],
                                             low[row:row + H, 0:2, :]).then_inc(shift_rows, 16)
                        sp.wait_ge(shift_rows, (m + 1) * 6 * 16)
                        sp.sem_inc(carried, 1)

            with ExitStack() as pctx, nc.Block() as block:
                def pt(name, shape, dt):
                    return pctx.enter_context(nc.psum_tensor(name, shape, dt))
                ps_s = pt("ps_s", [P, 4, 512], F32)
                ps_o = pt("ps_o", [P, 2, 512], F32)
                ps_t = pt("ps_t", [P, 512], F32)
                NU = 2 * H
                G = 32

                @block.sync
                def _(sp):
                    with sp.Fori(0, H) as h:
                        with sp.Fori(0, 2) as qp:
                            U = b * NU + h * 2 + qp

                            def load_q(r):
                                sp.wait_ge(q_free[r], ONE + U)
                                for i in range(2):
                                    rows = slice(ROW * i, ROW * (i + 1))
                                    sp.dma_start(qts[rows, r, i, :],
                                                 QT[rows, bass.ds(h, 1), bass.ds(qp * 1024 + r * 512, 512)]
                                                 .rearrange("p a n -> p (a n)")).then_inc(q_in[r], 16)
                            load_q(0)
                            for c in range(4):
                                sp.wait_ge(k_free[c], ONE + U)
                                sp.dma_start(kts[:, c * 512:(c + 1) * 512],
                                             KTa[:, bass.ds(h, 1), c * 512:(c + 1) * 512]
                                             .rearrange("p a n -> p (a n)")).then_inc(k_in[c], 16)
                                sp.wait_ge(v_free[c], ONE + U)
                                sp.dma_start(vts[:, 4 * c:4 * c + 4, :],
                                             V[:, 4 * c:4 * c + 4, bass.ds(h, 1), :]
                                             .rearrange("p t a n -> p t (a n)")).then_inc(v_in[c], 16)
                                sp.dma_start(vts32[:, c, 0:DV],
                                             V32[:, 2 * c + 1, bass.ds(h * DV, DV)]).then_inc(v_in[c], 16)
                            load_q(1)

                @block.tensor
                def _(pe):
                    def scores(u, x):
                        U, x = b * NU + u + x // G, x % G
                        r, kt = x // KT, x % KT
                        if kt == 0:
                            pe.wait_ge(q_in[r], 32 * (U + 1))
                        if r == 0 and kt % 4 == 0:
                            pe.wait_ge(k_in[kt // 4], 16 * (U + 1))
                        y = x - 2
                        pe.wait_ge(exp_done[y % RING], ONE + U * (G // RING) + y // RING + 1)
                        for i in range(2):
                            last = pe.matmul(ps_s[:, 2 * (x % 2) + i, :], kts[:, kt * P:(kt + 1) * P], qts[:, r, i, :],
                                             start=True, stop=True)
                        last.then_inc(scores_ready[x % 2], 1)

                    def values(u, x):
                        U, x = b * NU + u + x // G, x % G
                        r, kt, slot = x // KT, x % KT, x % RING
                        if r == 0 and kt % 4 == 0:
                            pe.wait_ge(v_in[kt // 4], 32 * (U + 1))
                        if kt == 0:
                            pe.wait_ge(evac0, ONE + U * 2 + r)
                            pe.wait_ge(evac1, ONE + U * 2 + r)
                        pe.wait_ge(exp_done[slot], ONE + U * (G // RING) + x // RING + 1)
                        if slot == RING - 1:
                            for i in range(2):
                                last = pe.matmul(ps_o[64 * i:64 * (i + 1), i, :], vts32[:, kt // RING, :],
                                                 prob[:, slot, 512 * i:512 * (i + 1)], start=False,
                                                 stop=(kt == KT - 1))
                                if i == 0 and r == 1:
                                    last.then_inc(k_free[kt // 4], 1)
                            last.then_inc(pv_done[slot], 1)
                            return
                        pe.wait_ge(low_done[slot], U * (G // RING) + x // RING + 1)
                        for i in range(2):
                            high = prob[:, slot, 512 * i:512 * (i + 1)].bitcast(BF16)[:, 1::2]
                            mm = pe.matmul(ps_o[0:64, i, :], vts[:, kt, :], high, start=(kt == 0),
                                           stop=(kt == KT - 2 and i == 1))
                            if i == 0 and r == 1 and kt % 4 == 0 and kt:
                                mm.then_inc(v_free[kt // 4 - 1], 1)
                            if i == 1 and kt == KT - 2:
                                mm.then_inc(q_free[r], 1)
                            last = pe.matmul(ps_o[64:128, i, :], vts[:, kt, :], low[:, slot, 512 * i:512 * (i + 1)],
                                             start=(kt == 0), stop=(kt == KT - 2 and i == 0))
                        last.then_inc(pv_done[slot], 1)

                    def totals(u, r):
                        n = (b * NU + u) * 2 + r
                        pe.wait_ge(evac0, ONE + n + 1)
                        pe.wait_ge(evac1, ONE + n + 1)
                        pe.wait_ge(norm_chain, ONE + 4 * n)
                        for i in range(8):
                            last = pe.matmul(ps_t[:, i * (DV + 1):(i + 1) * (DV + 1)], stack[:, i * P:(i + 1) * P],
                                             sel[:], start=True, stop=True)
                            if r == 1 and i == 0:
                                last.then_inc(v_free[3], 1)
                        last.then_inc(t_ready, 1)

                    AHEAD, T = 4, 4

                    def step(u, x, more=True):
                        values(u, x)
                        if more or x + AHEAD < G:
                            scores(u, x + AHEAD)
                        if x == KT + T - 1:
                            totals(u, 0)
                        if x == G + T - 1:
                            totals(u, 1)

                    for x in range(AHEAD):
                        scores(0, x)
                    for x in range(T):
                        step(0, x)
                    with pe.Fori(0, NU - 1) as u:
                        for x in range(T, G + T):
                            step(u, x)
                    for x in range(T, G):
                        step(NU - 1, x, more=False)
                    totals(NU - 1, 1)

                @block.scalar
                def _(act):
                    def exps(u, x):
                        U, x = b * NU + u + x // G, x % G
                        slot = x % RING
                        act.wait_ge(scores_ready[x % 2], U * (G // 2) + x // 2 + 1)
                        act.wait_ge(pv_done[slot], ONE + U * (G // RING) + x // RING)
                        act.activation(prob[:, slot, :],
                                       ps_s[:, 2 * (x % 2):2 * (x % 2) + 2, :].rearrange("p a n -> p (a n)"),
                                       ACT.Exp).then_inc(exp_done[slot], 1)

                    def evacuate(u, r):
                        U = b * NU + u
                        x = KT * r + KT - 1
                        act.wait_ge(pv_done[x % RING], ONE + U * (G // RING) + x // RING + 1)
                        act.wait_ge(t_ready, ONE + U * 2 + r)
                        act.copy(stack[:, 0:512], ps_o[:, 0, :]).then_inc(evac0, 1)

                    def step(u, x):
                        exps(u, x)
                        if x == KT + 1:
                            evacuate(u, 0)
                        if x == G + 1:
                            evacuate(u, 1)

                    for x in range(2):
                        exps(0, x)
                    with act.Fori(0, NU - 1) as u:
                        for x in range(2, G + 2):
                            step(u, x)
                    for x in range(2, G):
                        step(NU - 1, x)
                    evacuate(NU - 1, 1)

                @block.vector
                def _(dve):
                    def lows(u, x):
                        U, x = b * NU + u + x // G, x % G
                        slot = x % RING
                        if slot == RING - 1:
                            return
                        dve.wait_ge(exp_done[slot], ONE + U * (G // RING) + x // RING + 1)
                        dve.tensor_tensor(low[:, slot, :], prob[:, slot, :], prob[:, slot, :].bitcast(BF16)[:, 1::2],
                                          ALU.subtract).then_inc(low_done[slot], 1)

                    def evacuate(u, r):
                        U = b * NU + u
                        x = KT * r + KT - 1
                        dve.wait_ge(pv_done[x % RING], ONE + U * (G // RING) + x // RING + 1)
                        dve.wait_ge(t_ready, ONE + U * 2 + r)
                        dve.tensor_copy(stack[:, 512:1024], ps_o[:, 1, :]).then_inc(evac1, 1)

                    def normalise(u, r):
                        U = b * NU + u
                        c = (U * 2 + r) * 4
                        tot = ps_t[:, 0:8 * (DV + 1)].rearrange("p (i n) -> p i n", n=DV + 1)
                        dve.wait_ge(t_ready, ONE + U * 2 + r + 1)
                        dve.reciprocal(rec[:], tot[:, :, DV]).then_inc(norm_chain, 1)
                        dve.wait_ge(norm_chain, ONE + c + 1)
                        dve.tensor_tensor(onrm[:], tot[:, :, 0:DV],
                                          rec[:].rearrange("p (i a) -> p i a", a=1).to_broadcast([P, 8, DV]),
                                          ALU.mult).then_inc(norm_chain, 1)
                        dve.wait_ge(norm_chain, ONE + c + 2)
                        dve.tensor_scalar(ot[:], onrm[:, 4:8, :], lam[:], None, ALU.mult).then_inc(norm_chain, 1)
                        dve.wait_ge(norm_chain, ONE + c + 3)
                        dve.tensor_tensor(o_all[:, bass.ds(U * 8 + r * 4, 4), :], onrm[:, 0:4, :], ot[:],
                                          ALU.subtract).then_inc(norm_chain, 1)

                    E, NRM = KT, 22

                    def step(u, x):
                        lows(u, x)
                        if x == KT:
                            evacuate(u, 0)
                        if x == NRM:
                            normalise(u, 0)
                        if x == KT + KT:
                            evacuate(u, 1)
                        if x == KT + NRM:
                            normalise(u, 1)

                    for x in range(7):
                        lows(0, x)
                    with dve.Fori(0, NU - 1) as u:
                        for x in range(7, G + 7):
                            step(u, x)
                    for x in range(7, G):
                        step(NU - 1, x)
                    evacuate(NU - 1, 1)
                    normalise(NU - 1, 1)



FF = 512
NK3 = 512
KF = FF // P
CH = 512
CT = CH // P
NC = B * N // CH
E = 32
EP = E // 2
EALL = EP + 1
TWO_OVER_PI = 0.6366197723675814


def add_normalised(nc, sem, name, xs, y, st, scalars, last=False):
    mean, var, tmp, rstd = scalars
    chain = sem(name + "_dve")
    var_ready = sem(name + "_var_ready")
    rstd_done = sem(name + "_rstd_done")
    with nc.Block() as block:
        @block.vector
        def _(dve):
            ch = Chain(dve, chain)
            mean_rstd(dve, None, ch, st, mean, var, tmp)
            dve.tensor_scalar(var, var, 1e-5, None, ALU.add).then_inc(var_ready, 1)
            dve.wait_ge(rstd_done, 1)
            ch(dve.reciprocal(rstd, rstd))
            for tile in tiles(dve):
                dve.tensor_scalar(tile(y), tile(y), tile(mean),
                                  tile(rstd), ALU.subtract, ALU.mult).then_inc(chain, 1)
            ch.n += NT
            dve.wait_ge(chain, ch.n)
            ch(dve.tensor_tensor(xs[:], xs[:], y[:], ALU.add))
            if not last:
                for tile in tiles(dve):
                    dve.bn_stats(tile(st), tile(xs)).then_inc(chain, 1)
                ch.n += NT
                dve.wait_ge(chain, ch.n)

        @block.scalar
        def _(act):
            act.wait_ge(var_ready, 1)
            act.activation(rstd, var, ACT.Sqrt).then_inc(rstd_done, 1)


def later_layers(nc, a, sem, xs, o_all, ident, identb, out):
    with ExitStack() as ctx:
        def sbt(name, shape, dt=F32, c=ctx):
            return c.enter_context(nc.sbuf_tensor(name, shape, dt))

        y = sbt("y", [P, NT, P])
        st = sbt("stats", [P, NT, 6])
        mean = sbt("mean2", [P, NT])[:]
        var = sbt("var2", [P, NT])[:]
        tmp = sbt("tmp2", [P, NT])[:]
        rstd = sbt("rstd2", [P, NT])[:]
        scale = sbt("scale2", [P, NT])[:]
        scalars = (mean, var, tmp, rstd)
        slot = sbt("slot", [P, 2, CT, P])
        xT = sbt("xT", [P, 2, CH])
        wo = sbt("wo_sb", [P, P])
        lng = sbt("lng", [P, 1])
        lnb = sbt("lnb", [P, 1])
        wg = sbt("wg", [P, EALL * P])
        wu = sbt("wu", [P, EALL * P])
        wd = sbt("wd", [P, EALL, P])
        gw = sbt("gw", [P, E])
        gbias = sbt("gbias", [P, E])
        esel = sbt("esel", [3 * E, EP * P], BF16)
        w_in = sem("wo_in")
        moe_in = sem("moe_in")
        esel_in = sem("esel_in")
        carried = sem("carried_later")

        n_g = NT * H
        grstd = sbt("grstd", [P, n_g])
        group = ExitStack()
        esel_f = sbt("esel_f", [3 * E, EP * P], F32, group)
        gsum = sbt("gsum", [P, n_g], F32, group)
        gvar = sbt("gvar", [P, n_g], F32, group)
        gsq = sbt("gsq", [P, n_g, DV], F32, group)
        g_chain, g_sq, g_var, g_rstd = sem("g_chain"), sem("g_sq"), sem("g_var"), sem("g_rstd")
        

        def bc(v, n, d):
            return v.rearrange("p (n a) -> p n a", a=1).to_broadcast([P, n, d])

        with nc.Block() as block:
            @block.sync
            def _(sp):
                sp.dma_start(wo[:], a["wo"]).then_inc(w_in, 16)
                sp.dma_start(lng[:], a["lng"]).then_inc(w_in, 16)
                sp.dma_start(lnb[:], a["lnb"]).then_inc(w_in, 16)
                sp.dma_start(wg[:], a["wg"]).then_inc(moe_in, 16)
                sp.dma_start(wu[:], a["wu"]).then_inc(moe_in, 16)
                sp.dma_start(wd[:], a["wd"]).then_inc(moe_in, 16)
                sp.dma_start(gw[:], a["gw"]).then_inc(moe_in, 16)
                sp.dma_start(gbias[:], a["gb"].partition_broadcast(P)).then_inc(moe_in, 16)
                sp.dma_start(esel_f[:], a["esel"]).then_inc(esel_in, 16)

            @block.vector
            def _(dve):
                ch = Chain(dve, g_chain)
                ch(dve.tensor_reduce(gsum[:], o_all[:], AX.X, ALU.add))
                ch(dve.tensor_scalar(gsum[:], gsum[:], 1.0 / DV, None, ALU.mult))
                ch(dve.tensor_tensor(o_all[:], o_all[:], bc(gsum[:], n_g, DV), ALU.subtract))
                dve.wait_ge(g_sq, 1)
                ch(dve.tensor_reduce(gvar[:], gsq[:], AX.X, ALU.add))
                dve.tensor_scalar(gvar[:], gvar[:], 1.0 / DV, 1e-5, ALU.mult, ALU.add).then_inc(g_var, 1)
                dve.wait_ge(esel_in, 16)
                ch(dve.tensor_copy(esel[:], esel_f[:]))
                dve.wait_ge(g_rstd, 1)
                ch(dve.reciprocal(grstd[:], grstd[:]))

            @block.scalar
            def _(act):
                act.wait_ge(g_chain, 3)
                act.activation(gsq[:], o_all[:], ACT.Square).then_inc(g_sq, 1)
                act.wait_ge(g_var, 1)
                act.activation(grstd[:], gvar[:], ACT.Sqrt).then_inc(g_rstd, 1)

        group.close()

        def slots(name, from_one=False):
            return [sem(f"{name}{s}", ONE if from_one else 0) for s in range(2)]

        with ExitStack() as pctx, nc.Block() as block:
            ps_t = [pctx.enter_context(nc.psum_tensor(f"p1_t{s}", [P, CH], F32)) for s in range(2)]
            ps_y = [pctx.enter_context(nc.psum_tensor(f"p1_y{s}", [P, CH], F32)) for s in range(2)]
            on_ready, t_ready, t_copied = slots("p1_on"), slots("p1_t", True), slots("p1_tc", True)
            y_ready, y_copied, stat = slots("p1_y", True), slots("p1_yc", True), sem("p1_stat")
            o_v = o_all[:].rearrange("p (b h q t) d -> p b h q t d", b=B, h=H, q=NQC)
            r_v = grstd[:].rearrange("p (b h q t a) -> p b h q t a", b=B, h=H, q=NQC, a=1)

            @block.sync
            def _(sp):
                sem.start(sp)

            @block.vector
            def _(dve):
                def front(c, s, used):
                    b, q = c // NQC, c % NQC
                    dve.wait_ge(t_ready[s], ONE + used)
                    for t in range(CT):
                        last = dve.tensor_tensor(
                            slot[:, s, t, :].rearrange("p (h d) -> p h d", h=H),
                            o_v[:, b, :, q, t, :], r_v[:, b, :, q, t, :].to_broadcast([P, H, DV]), ALU.mult)
                    last.then_inc(on_ready[s], 1)

                def back(c, s, used):
                    dve.wait_ge(y_copied[s], ONE + used + 1)
                    for t in range(CT):
                        dve.bn_stats(st[:, CT * c + t:CT * c + t + 1, :], y[:, CT * c + t:CT * c + t + 1, :]) \
                            .then_inc(stat, 1)

                for c in range(NC):
                    front(c, c % 2, c // 2)
                    if c:
                        back(c - 1, (c - 1) % 2, (c - 1) // 2)
                back(NC - 1, 1, (NC - 1) // 2)
                dve.wait_ge(stat, NT)

            @block.tensor
            def _(pe):
                pe.wait_ge(w_in, 48)

                def front(c, s, used):
                    pe.wait_ge(on_ready[s], used + 1)
                    pe.wait_ge(t_copied[s], ONE + used)
                    for t in range(CT):
                        last = pe.transpose(ps_t[s][:, t * P:(t + 1) * P], slot[:, s, t, :], ident[:])
                    last.then_inc(t_ready[s], 1)

                def back(c, s, used):
                    pe.wait_ge(t_copied[s], ONE + used + 1)
                    pe.wait_ge(y_copied[s], ONE + used)
                    for t in range(CT):
                        last = pe.matmul(ps_y[s][:, t * P:(t + 1) * P], xT[:, s, t * P:(t + 1) * P], wo[:],
                                         start=True, stop=True)
                    last.then_inc(y_ready[s], 1)

                pipelined(pe, front, back, NC, 0)

            @block.scalar
            def _(act):
                act.wait_ge(w_in, 48)

                def front(c, s, used):
                    act.wait_ge(t_ready[s], ONE + used + 1)
                    act.wait_ge(y_ready[s], ONE + used)
                    act.activation(xT[:, s, :], ps_t[s][:], ACT.Identity, bias=lnb[:], scale=lng[:]) \
                        .then_inc(t_copied[s], 1)

                def back(c, s, used):
                    act.wait_ge(y_ready[s], ONE + used + 1)
                    act.sem_inc(carried, 1)
                    act.copy(y[:, bass.ds(CT * c, CT), :].rearrange("p t d -> p (t d)"), ps_y[s][:]) \
                        .then_inc(y_copied[s], 1)

                pipelined(act, front, back, NC, 0)

        add_normalised(nc, sem, "res1", xs, y, st, scalars)

        small = sem("l2_small")
        with ExitStack() as l2:
            def sb2(name, shape, dt=F32):
                return l2.enter_context(nc.sbuf_tensor(name, shape, dt))
            up = sb2("up", [P, FF])
            down = sb2("down", [P, KF, P])
            tern = sb2("tern", [P, FF])
            sgn = sb2("sgn", [P, FF])
            asum = sb2("asum", [P, 2])
            aall = sb2("aall", [P, 2])
            ones = sb2("ones", [P, 1])
            hid = sb2("hid", [P, 2, KF, CH])
            hsq = sb2("hsq", [P, KF, CH])
            hsum = sb2("hsum", [P, 2, CH])
            rms = sb2("rms", [P, NT])
            loaded, chain, asum_ready, aall_ready, sqrt_in, sqrt_out = (sem("l2_" + n) for n in (
                "loaded", "chain", "asum", "aall", "sqrt_in", "sqrt_out"))
            with nc.Block() as block:
                @block.sync
                def _(sp):
                    sp.dma_start(up[:], a["up"]).then_inc(loaded, 16)
                    sp.dma_start(down[:], a["down"]).then_inc(loaded, 16)

                @block.gpsimd
                def _(pool):
                    pool.memset(ones[:], 1.0)
                    pool.wait_ge(asum_ready, 1)
                    pool.partition_all_reduce(aall[:], asum[:], P, RADD).then_inc(aall_ready, 1)

                @block.scalar
                def _(act):
                    act.wait_ge(sqrt_in, 1)
                    act.activation(rstd, scale, ACT.Sqrt).then_inc(sqrt_out, 1)
                    act.wait_ge(small, 1)
                    act.activation(scale, tmp, ACT.Sqrt).then_inc(small, 1)

                @block.vector
                def _(dve):
                    ch = Chain(dve, chain)
                    mean_rstd(dve, None, ch, st, mean, var, tmp)
                    dve.tensor_scalar(scale, var, 1e-5, None, ALU.add).then_inc(sqrt_in, 1)
                    dve.wait_ge(loaded, 32)
                    flat_down = down[:].rearrange("p k n -> p (k n)")
                    for i, w in enumerate((up[:], flat_down)):
                        ch(dve.tensor_reduce(asum[:, i:i + 1], w, AX.X, ALU.add, apply_absolute_value=True))
                    dve.tensor_scalar(asum[:], asum[:], 0.5 / (P * FF), None, ALU.mult).then_inc(asum_ready, 1)
                    dve.wait_ge(aall_ready, 1)
                    ch(dve.tensor_scalar(asum[:], aall[:], -1.0, None, ALU.mult))
                    for i, w in enumerate((up[:], flat_down)):
                        ch(dve.tensor_scalar(tern[:], w, aall[:, i:i + 1], None, ALU.is_gt))
                        ch(dve.tensor_scalar(sgn[:], w, asum[:, i:i + 1], None, ALU.is_lt))
                        ch(dve.tensor_tensor(tern[:], tern[:], sgn[:], ALU.subtract))
                        ch(dve.tensor_tensor(tern[:], tern[:], w, ALU.subtract))
                        ch(dve.tensor_tensor(w, w, tern[:], ALU.add))
                    dve.wait_ge(sqrt_out, 1)
                    ch(dve.reciprocal(rstd, rstd))
                    ch(dve.tensor_tensor(tmp, rstd, rstd, ALU.mult))
                    dve.tensor_tensor(tmp, tmp, var, ALU.mult).then_inc(small, 1)
                    dve.wait_ge(small, 2)
                    ch(dve.tensor_scalar(scale, scale, 1e-8, None, ALU.add))
                    ch(dve.reciprocal(scale, scale))
                    ch(dve.tensor_tensor(scale, scale, rstd, ALU.mult))

            with ExitStack() as pctx, nc.Block() as block:
                ps_t = pctx.enter_context(nc.psum_tensor("p2_t", [P, CH], F32))
                ps_h = pctx.enter_context(nc.psum_tensor("p2_h", [P, KF, CH], F32))
                ps_y = pctx.enter_context(nc.psum_tensor("p2_y", [P, CH], F32))
                ps_r = pctx.enter_context(nc.psum_tensor("p2_r", [P, CH], F32))
                xn_ready, h_ready, sq_done = (slots("p2_" + n) for n in ("xn", "h", "sq"))
                t_ready, t_copied, h_done, sum_done, y_ready = (
                    slots("p2_" + n, True) for n in ("t", "tc", "hd", "sum", "y"))
                y_copied, stat, r_copied = sem("p2_yc", ONE), sem("p2_stat"), sem("p2_rc", ONE)

                @block.sync
                def _(sp):
                    sem.start(sp)

                @block.vector
                def _(dve):
                    def front(c, s, used):
                        dve.wait_ge(t_ready[s], ONE + used)
                        for t in range(CT):
                            i = CT * c + t
                            last = dve.tensor_scalar(slot[:, s, t, :], xs[:, bass.ds(i, 1), :].rearrange("p a d -> p (a d)"),
                                                     mean[:, bass.ds(i, 1)], scale[:, bass.ds(i, 1)],
                                                     ALU.subtract, ALU.mult)
                        last.then_inc(xn_ready[s], 1)

                    def back(c, s, used):
                        dve.wait_ge(sq_done[s], used + 1)
                        dve.wait_ge(y_ready[s], ONE + used)
                        dve.tensor_reduce(hsum[:, s, :], hsq[:].rearrange("p k n -> p n k"), AX.X, ALU.add) \
                            .then_inc(sum_done[s], 1)
                        dve.wait_ge(y_copied, ONE + c + 1)
                        dve.tensor_copy(rms[:, bass.ds(CT * c, CT)], ps_r[:, 0:CT]).then_inc(r_copied, 1)
                        for t in range(CT):
                            dve.bn_stats(st[:, bass.ds(CT * c + t, 1), :], y[:, bass.ds(CT * c + t, 1), :]) \
                                .then_inc(stat, 1)

                    pipelined(dve, front, back, NC, 0)
                    dve.wait_ge(stat, NT)

                @block.tensor
                def _(pe):
                    def front(c, s, used):
                        pe.wait_ge(xn_ready[s], used + 1)
                        pe.wait_ge(t_copied[1 - s], ONE + used + s)
                        for t in range(CT):
                            last = pe.transpose(ps_t[:, t * P:(t + 1) * P], slot[:, s, t, :], ident[:])
                        last.then_inc(t_ready[s], 1)
                        pe.wait_ge(t_copied[s], ONE + used + 1)
                        for k in range(KF):
                            pe.wait_ge(h_done[1 - s], ONE + (used + s) * KF)
                            pe.matmul(ps_h[:, k, :], up[:, k * P:(k + 1) * P], xT[:, s, :], start=True, stop=True) \
                                .then_inc(h_ready[s], 1)

                    def back(c, s, used):
                        pe.wait_ge(h_done[s], ONE + (used + 1) * KF)
                        pe.wait_ge(y_copied, ONE + c)
                        pe.wait_ge(r_copied, ONE + c)
                        for t in range(CT):
                            for k in range(KF):
                                pe.matmul(ps_y[:, t * P:(t + 1) * P], hid[:, s, k, t * P:(t + 1) * P], down[:, k, :],
                                          start=(k == 0), stop=(k == KF - 1))
                        pe.wait_ge(sum_done[s], ONE + used + 1)
                        for t in range(CT):
                            last = pe.matmul(ps_r[:, t:t + 1], hsum[:, s, t * P:(t + 1) * P], ones[:],
                                             start=True, stop=True)
                        last.then_inc(y_ready[s], 1)

                    pipelined(pe, front, back, NC, 0)

                @block.scalar
                def _(act):
                    def front(c, s, used):
                        act.wait_ge(t_ready[s], ONE + used + 1)
                        act.copy(xT[:, s, :], ps_t[:]).then_inc(t_copied[s], 1)
                        act.wait_ge(y_ready[s], ONE + used)
                        for k in range(KF):
                            act.wait_ge(h_ready[s], used * KF + k + 1)
                            act.activation(hid[:, s, k, :], ps_h[:, k, :], ACT.Gelu).then_inc(h_done[s], 1)
                        act.wait_ge(h_done[s], ONE + (used + 1) * KF)
                        act.wait_ge(sum_done[1 - s], ONE + used + s)
                        act.activation(hsq[:], hid[:, s, :, :], ACT.Square).then_inc(sq_done[s], 1)

                    def back(c, s, used):
                        act.wait_ge(y_ready[s], ONE + used + 1)
                        act.sem_inc(carried, 1)
                        act.copy(y[:, bass.ds(CT * c, CT), :].rearrange("p t d -> p (t d)"), ps_y[:]) \
                            .then_inc(y_copied, 1)

                    pipelined(act, front, back, NC, 0)

            q = sem("l2_q")
            with nc.Block() as block:
                @block.scalar
                def _(act):
                    act.wait_ge(q, 1)
                    act.activation(rms[:], rms[:], ACT.Sqrt).then_inc(q, 1)

                @block.vector
                def _(dve):
                    dve.tensor_scalar(rms[:], rms[:], 1.0 / FF, None, ALU.mult).then_inc(q, 1)
                    dve.wait_ge(q, 2)
                    ch = Chain(dve, q, 2)
                    ch(dve.tensor_scalar(rms[:], rms[:], 1e-8, None, ALU.add))
                    ch(dve.reciprocal(rms[:], rms[:]))
                    for tile in tiles(dve):
                        dve.tensor_scalar(tile(y), tile(y), tile(rms),
                                          None, ALU.mult).then_inc(q, 1)
                    ch.n += NT
                    dve.wait_ge(q, 2 + ch.n)
                    for tile in tiles(dve):
                        dve.bn_stats(tile(st), tile(y)).then_inc(q, 1)
                    ch.n += NT
                    dve.wait_ge(q, 2 + ch.n)
        add_normalised(nc, sem, "res2", xs, y, st, scalars)
        third_layer(nc, a, sem, xs, y, o_all, st, scalars, scale, slot, xT, ident, slots, carried)
        add_normalised(nc, sem, "res3", xs, y, st, scalars)
        experts(nc, a, sem, xs, y, st, scalars, scale, slot, xT, ident, identb, slots,
                wg, wu, wd, gw, gbias, esel, moe_in, carried)
        add_normalised(nc, sem, "res4", xs, y, st, scalars, last=True)
        stored = sem("stored")
        with nc.Block() as block:
            @block.sync
            def _(sp):
                for c in range(4):
                    sp.dma_start(out[:, 8 * c:8 * c + 8, :], xs[:, 8 * c:8 * c + 8, :]).then_inc(stored, 16)
                sp.wait_ge(stored, 64)


def third_layer(nc, a, sem, xs, y, o_all, st, scalars, scale, slot, xT, ident, slots, carried):
    mean, var, tmp, rstd = scalars
    with ExitStack() as l3:
        def sb3(name, shape, dt=F32):
            return l3.enter_context(nc.sbuf_tensor(name, shape, dt))
        kw = sb3("kw", [P, KF, P])
        kT = sb3("kT", [P, NK3])
        qw = sb3("qw", [P, KF, P])
        bias3 = sb3("bias3", [P, P])
        w3 = sb3("w3", [P, P])
        b3 = sb3("b3", [P, P])
        kn = sb3("kn", [P, KF])
        ksq = sb3("ksq", [P, KF, P])
        zsq = o_all[:].rearrange("p g d -> p (g d)").rearrange("p (t n) -> p t n", n=P)
        zn = sb3("zn", [P, NT])
        loaded, kc, pc, kt_ready, zs = (sem("l3_" + n) for n in ("loaded", "kc", "pc", "kt", "zs"))

        def rows(v):
            return v[:].rearrange("p (a d) -> p a d", a=1).to_broadcast([P, NT, P])

        with ExitStack() as pctx, nc.Block() as block:
            ps_k = pctx.enter_context(nc.psum_tensor("p3_k", [P, NK3], F32))

            @block.sync
            def _(sp):
                sp.dma_start(kw[:], a["kw"]).then_inc(loaded, 16)
                sp.dma_start(qw[:], a["qw"]).then_inc(loaded, 16)
                for dst, n in ((bias3, "bias3"), (w3, "w3"), (b3, "b3")):
                    sp.dma_start(dst[:], a[n].partition_broadcast(P)).then_inc(loaded, 16)

            @block.vector
            def _(dve):
                ch = Chain(dve, kc)
                dve.wait_ge(loaded, 80)
                ch(dve.tensor_tensor(ksq[:], kw[:], kw[:], ALU.mult))
                ch(dve.tensor_reduce(kn[:], ksq[:], AX.X, ALU.add))
                dve.tensor_scalar(kn[:], kn[:], 1e-24, None, ALU.max).then_inc(pc, 1)
                dve.wait_ge(pc, 2)
                ch(dve.reciprocal(kn[:], kn[:]))
                ch(dve.tensor_tensor(kw[:], kw[:], kn[:].rearrange("p (k a) -> p k a", a=1).to_broadcast([P, KF, P]),
                                     ALU.mult))
                mean_rstd(dve, None, ch, st, mean, var, tmp)
                dve.tensor_scalar(scale, var, 1e-5, None, ALU.add).then_inc(pc, 1)
                dve.wait_ge(pc, 4)
                ch(dve.reciprocal(rstd, rstd))
                ch(dve.tensor_tensor(tmp, rstd, rstd, ALU.mult))
                ch(dve.tensor_tensor(tmp, tmp, var, ALU.mult))
                dve.tensor_scalar(tmp, tmp, 1e-12, None, ALU.add).then_inc(pc, 1)
                dve.wait_ge(pc, 6)
                ch(dve.reciprocal(tmp, tmp))
                ch(dve.tensor_tensor(scale, rstd, tmp, ALU.mult))
                for tile in tiles(dve):
                    dve.tensor_scalar(tile(y), tile(xs), tile(mean),
                                      tile(scale), ALU.subtract, ALU.mult).then_inc(kc, 1)
                ch.n += NT
                dve.wait_ge(kc, ch.n)
                ch(dve.tensor_tensor(y[:], y[:], rows(w3), ALU.mult))
                dve.tensor_tensor(y[:], y[:], rows(b3), ALU.add).then_inc(zs, 1)
                dve.wait_ge(zs, 2)
                ch(dve.tensor_reduce(zn[:], zsq, AX.X, ALU.add))
                dve.tensor_scalar(zn[:], zn[:], 1e-24, None, ALU.max).then_inc(pc, 1)
                dve.wait_ge(pc, 8)
                ch(dve.reciprocal(zn[:], zn[:]))

            @block.scalar
            def _(act):
                for i, (n, root) in enumerate(((kn[:], kn[:]), (scale, rstd), (tmp, tmp))):
                    act.wait_ge(pc, 2 * i + 1)
                    act.activation(root, n, ACT.Sqrt).then_inc(pc, 1)
                act.wait_ge(kt_ready, 1)
                act.copy(kT[:], ps_k[:]).then_inc(kt_ready, 1)
                act.wait_ge(zs, 1)
                act.activation(zsq, y[:], ACT.Square).then_inc(zs, 1)
                act.wait_ge(pc, 7)
                act.activation(zn[:], zn[:], ACT.Sqrt).then_inc(pc, 1)

            @block.tensor
            def _(pe):
                pe.wait_ge(kc, 4)
                for k in range(KF):
                    last = pe.transpose(ps_k[:, k * P:(k + 1) * P], kw[:, k, :], ident[:])
                last.then_inc(kt_ready, 1)

        d_all = sb3("d_all", [P, NC, KF * CH])
        s_sb = sb3("s_sb", [P, 2, KF * CH])
        ln_p = sb3("ln_p", [P, 2, KF * CH])
        pw = sb3("pw", [P, KF, CH])
        with ExitStack() as pctx, nc.Block() as block:
            ps_t = pctx.enter_context(nc.psum_tensor("p3_t", [P, CH], F32))
            ps_s = pctx.enter_context(nc.psum_tensor("p3_s", [P, KF, CH], F32))
            q_ready, t_ready, t_copied = slots("p3_q"), slots("p3_t", True), slots("p3_tc", True)
            s_ready, d_done = slots("p3_s"), slots("p3_d", True)
            clipped = [sem(f"p3_clip{k}", ONE) for k in range(KF)]
            lns = sem("p3_ln")
            ln_m_done = slots("p3_lnm")

            @block.sync
            def _(sp):
                sem.start(sp)

            @block.vector
            def _(dve):
                def first(c, s, used):
                    dve.wait_ge(t_ready[s], ONE + used)
                    for t in range(CT):
                        i = CT * c + t
                        last = dve.tensor_scalar(slot[:, s, t, :], y[:, bass.ds(i, 1), :].rearrange("p a d -> p (a d)"),
                                                 zn[:, bass.ds(i, 1)], None, ALU.mult)
                    last.then_inc(q_ready[s], 1)

                def second(c, s, used):
                    dve.wait_ge(d_done[s], ONE + used)
                    for k in range(KF):
                        dve.wait_ge(s_ready[s], KF * used + k + 1)
                        dve.tensor_scalar(s_sb[:, s, k * CH:(k + 1) * CH], ps_s[:, k, :], 1.0 - 1e-6, -1.0 + 1e-6,
                                          ALU.min, ALU.max).then_inc(clipped[k], 1)

                def third(c, s, used):
                    dve.wait_ge(ln_m_done[s], used + 1)
                    dve.tensor_tensor(d_all[:, bass.ds(c, 1), :].rearrange("p a n -> p (a n)"), ln_p[:, s, :],
                                      s_sb[:, s, :], ALU.subtract).then_inc(d_done[s], 1)

                pipelined3(dve, first, second, third, NC)

            @block.tensor
            def _(pe):
                def front(c, s, used):
                    pe.wait_ge(q_ready[s], used + 1)
                    pe.wait_ge(t_copied[1 - s], ONE + used + s)
                    for t in range(CT):
                        last = pe.transpose(ps_t[:, t * P:(t + 1) * P], slot[:, s, t, :], ident[:])
                    last.then_inc(t_ready[s], 1)

                def back(c, s, used):
                    pe.wait_ge(t_copied[s], ONE + used + 1)
                    for k in range(KF):
                        pe.wait_ge(clipped[k], ONE + c)
                        pe.matmul(ps_s[:, k, :], kT[:, k * P:(k + 1) * P], xT[:, s, :], start=True, stop=True) \
                            .then_inc(s_ready[s], 1)

                pipelined(pe, front, back, NC, 0)

            @block.scalar
            def _(act):
                def front(c, s, used):
                    act.wait_ge(t_ready[s], ONE + used + 1)
                    act.copy(xT[:, s, :], ps_t[:]).then_inc(t_copied[s], 1)

                def back(c, s, used):
                    for k in range(KF):
                        act.wait_ge(clipped[k], ONE + c + 1)
                    act.wait_ge(d_done[s], ONE + used)
                    act.activation(ln_p[:, s, :], s_sb[:, s, :], ACT.Ln, bias=1.0, scale=1.0).then_inc(lns, 1)
                    act.wait_ge(lns, c + 1)
                    act.activation(s_sb[:, s, :], s_sb[:, s, :], ACT.Ln, bias=1.0, scale=-1.0) \
                        .then_inc(ln_m_done[s], 1)

                pipelined(act, front, back, NC, 0)

        at, w_2 = s_sb, ln_p
        with ExitStack() as pctx, nc.Block() as block:
            ps_x = [pctx.enter_context(nc.psum_tensor(f"p3_x{s}", [P, CH], F32)) for s in range(2)]
            w2_done, w4_done, w8_done = (slots("p3c_" + n) for n in ("w2", "w4", "w8"))
            pw_done, x_ready, x_copied = (slots("p3c_" + n, True) for n in ("pw", "x", "xc"))
            ac = sem("p3c_ac")
            half_b = sb3("half_b", [P, 1])
            hb = sem("p3_half")

            @block.sync
            def _(sp):
                sem.start(sp)

            @block.gpsimd
            def _(pool):
                pool.memset(half_b[:], 0.5).then_inc(hb, 1)

            @block.scalar
            def _(act):
                act.wait_ge(hb, 1)

                def first(c, s, used):
                    act.wait_ge(pw_done[s], ONE + used)
                    act.sem_inc(carried, 1)
                    act.activation(at[:, s, :], d_all[:, bass.ds(c, 1), :].rearrange("p a n -> p (a n)"), ACT.Tanh,
                                   scale=0.25).then_inc(ac, 1)
                    act.wait_ge(ac, 2 * c + 1)
                    act.activation(at[:, s, :], at[:, s, :], ACT.Arctan).then_inc(ac, 1)
                    act.wait_ge(ac, 2 * c + 2)
                    act.activation(w_2[:, s, :], at[:, s, :], ACT.Square, bias=half_b[:], scale=TWO_OVER_PI) \
                        .then_inc(w2_done[s], 1)

                def second(c, s, used):
                    act.wait_ge(w4_done[s], used + 1)
                    act.activation(w_2[:, s, :], w_2[:, s, :], ACT.Square, scale=TWO_OVER_PI ** 0.5) \
                        .then_inc(w8_done[s], 1)

                def third(c, s, used):
                    act.wait_ge(x_ready[s], ONE + used + 1)
                    act.sem_inc(carried, 1)
                    act.copy(y[:, bass.ds(CT * c, CT), :].rearrange("p t d -> p (t d)"), ps_x[s][:]) \
                        .then_inc(x_copied[s], 1)

                pipelined3(act, first, second, third, NC)

            @block.vector
            def _(dve):
                def front(c, s, used):
                    dve.wait_ge(w2_done[s], used + 1)
                    dve.tensor_tensor(w_2[:, s, :], w_2[:, s, :], w_2[:, s, :], ALU.mult).then_inc(w4_done[s], 1)

                def back(c, s, used):
                    dve.wait_ge(w8_done[s], used + 1)
                    dve.wait_ge(x_ready[1 - s], ONE + used + s)
                    dve.scalar_tensor_tensor(pw[:].rearrange("p k n -> p (k n)"), at[:, s, :], 0.7853981633974483,
                                             w_2[:, s, :], ALU.add, ALU.mult).then_inc(pw_done[s], 1)

                pipelined(dve, front, back, NC, 0)

            @block.tensor
            def _(pe):
                with pe.Fori(0, NC // 2) as k:
                    for s in range(2):
                        pe.wait_ge(pw_done[s], ONE + k + 1)
                        pe.wait_ge(x_copied[s], ONE + k)
                        for t in range(CT):
                            for j in range(KF):
                                last = pe.matmul(ps_x[s][:, t * P:(t + 1) * P], pw[:, j, t * P:(t + 1) * P],
                                                 qw[:, j, :], start=(j == 0), stop=(j == KF - 1))
                        last.then_inc(x_ready[s], 1)

        xc, xp = sem("l3_xc"), sem("l3_xp")
        with nc.Block() as block:
            @block.scalar
            def _(act):
                act.activation(zsq, y[:], ACT.Square).then_inc(xp, 1)
                act.wait_ge(xp, 2)
                act.activation(zn[:], zn[:], ACT.Sqrt).then_inc(xp, 1)

            @block.vector
            def _(dve):
                ch = Chain(dve, xc)
                dve.wait_ge(xp, 1)
                ch(dve.tensor_reduce(zn[:], zsq, AX.X, ALU.add))
                dve.tensor_scalar(zn[:], zn[:], 1e-24, None, ALU.max).then_inc(xp, 1)
                dve.wait_ge(xp, 3)
                ch(dve.reciprocal(zn[:], zn[:]))
                for tile in tiles(dve):
                    dve.tensor_scalar(tile(y), tile(y), tile(zn),
                                      None, ALU.mult).then_inc(xc, 1)
                ch.n += NT
                dve.wait_ge(xc, ch.n)
                ch(dve.tensor_tensor(y[:], y[:], rows(bias3), ALU.add))
                for tile in tiles(dve):
                    dve.bn_stats(tile(st), tile(y)).then_inc(xc, 1)
                ch.n += NT
                dve.wait_ge(xc, ch.n)


def experts(nc, a, sem, xs, y, st, scalars, scale, slot, xT, ident, identb, slots,
            wg, wu, wd, gw, gbias, esel, moe_in, carried):
    mean, var, tmp, rstd = scalars
    NG, TOPK, BIG = 4, 8, 3.0e38
    EG = E // NG
    with ExitStack() as l4:
        def sb4(name, shape, dt=F32):
            return l4.enter_context(nc.sbuf_tensor(name, shape, dt))
        xnT = sb4("xnT_all", [P, B * N])
        sc = sb4("sc", [P, NT, E])
        cho = sb4("cho", [P, NT, E])
        work = sb4("work", [P, NT, E])
        eq = sb4("eq", [P, NT, E])
        m1 = sb4("m1", [P, NT * NG])
        m2 = sb4("m2", [P, NT * NG])
        cnt = sb4("cnt", [P, NT * NG])
        rank = sb4("rank", [P, NT, NG])
        cmp = sb4("cmp", [P, NT, NG])
        top8 = sb4("top8", [P, NT, TOPK])
        wsum = sb4("wsum", [P, NT])
        wparts = sb4("wparts", [P, NT, 3, E], BF16)
        wT = sb4("wT", [3 * E, B * N], BF16)
        silu = sb4("silu", [P, 2, CH])
        prod = sb4("prod", [P, 2, CH])
        hT = sb4("hT", [P, 2, CH])
        fT = sb4("fT", [P, CH])
        pc, chain = sem("l4_pc"), sem("l4_chain")
        with nc.Block() as block:
            @block.scalar
            def _(act):
                act.wait_ge(pc, 1)
                act.activation(rstd, scale, ACT.Sqrt).then_inc(pc, 1)

            @block.vector
            def _(dve):
                ch = Chain(dve, chain)
                mean_rstd(dve, None, ch, st, mean, var, tmp)
                dve.tensor_scalar(scale, var, 1e-5, None, ALU.add).then_inc(pc, 1)
                dve.wait_ge(moe_in, 16 * 5)
                dve.wait_ge(pc, 2)
                ch(dve.reciprocal(rstd, rstd))

        with ExitStack() as pctx, nc.Block() as block:
            ps_t = [pctx.enter_context(nc.psum_tensor(f"p4_t{s}", [P, CH], F32)) for s in range(2)]
            ps_l = [pctx.enter_context(nc.psum_tensor(f"p4_l{s}", [P, CH], F32)) for s in range(2)]
            xn_ready = slots("p4_xn")
            t_ready, t_copied, l_ready, all_copied = (slots("p4_" + n, True) for n in ("t", "tc", "l", "all"))
            sig_done = sem("p4_sig")

            @block.sync
            def _(sp):
                sem.start(sp)

            @block.vector
            def _(dve):
                with dve.Fori(0, NC // 2) as k:
                    for s in range(2):
                        dve.wait_ge(t_ready[s], ONE + k)
                        for t in range(CT):
                            i = CT * (2 * k + s) + t
                            last = dve.tensor_scalar(slot[:, s, t, :], xs[:, bass.ds(i, 1), :].rearrange("p a d -> p (a d)"),
                                                     mean[:, bass.ds(i, 1)], rstd[:, bass.ds(i, 1)],
                                                     ALU.subtract, ALU.mult)
                        last.then_inc(xn_ready[s], 1)

            @block.tensor
            def _(pe):
                def front(c, s, used):
                    pe.wait_ge(xn_ready[s], used + 1)
                    pe.wait_ge(t_copied[s], ONE + used)
                    for t in range(CT):
                        last = pe.transpose(ps_t[s][:, t * P:(t + 1) * P], slot[:, s, t, :], ident[:])
                    last.then_inc(t_ready[s], 1)

                def back(c, s, used):
                    pe.wait_ge(t_copied[s], ONE + used + 1)
                    for t in range(CT):
                        last = pe.matmul(ps_l[s][:, t * E:(t + 1) * E], xT[:, s, t * P:(t + 1) * P], gw[:],
                                         start=True, stop=True)
                    last.then_inc(l_ready[s], 1)

                pipelined(pe, front, back, NC, 0)

            @block.scalar
            def _(act):
                def front(c, s, used):
                    act.wait_ge(t_ready[s], ONE + used + 1)
                    act.wait_ge(l_ready[s], ONE + used)
                    act.wait_ge(all_copied[s], ONE + used)
                    act.copy(xT[:, s, :], ps_t[s][:]).then_inc(t_copied[s], 1)

                def back(c, s, used):
                    act.wait_ge(l_ready[s], ONE + used + 1)
                    act.sem_inc(carried, 1)
                    act.activation(sc[:, bass.ds(CT * c, CT), :].rearrange("p t e -> p (t e)"),
                                   ps_l[s][:, 0:CT * E], ACT.Sigmoid).then_inc(sig_done, 1)

                pipelined(act, front, back, NC, 0)

            @block.gpsimd
            def _(pool):
                with pool.Fori(0, NC // 2) as k:
                    for s in range(2):
                        pool.wait_ge(t_copied[s], ONE + k + 1)
                        pool.sem_inc(carried, 1)
                        pool.tensor_copy(xnT[:, bass.ds((2 * k + s) * CH, CH)], xT[:, s, :]).then_inc(all_copied[s], 1)

        with ExitStack() as pctx, nc.Block() as block:
            ps_w = [pctx.enter_context(nc.psum_tensor(f"p4_w{s}", [P, 1024], BF16)) for s in range(2)]
            wp_ready, w_ready, w_copied = sem("p4_wp"), sem("p4_w"), sem("p4_wc")
            rc = sem("p4_rc")

            @block.vector
            def _(dve):
                ch = Chain(dve, rc)

                def g3(v):
                    return v[:].rearrange("p t (g e) -> p (t g) e", g=NG)

                def gb3(v):
                    return v[:].rearrange("p (n a) -> p n a", a=1).to_broadcast([P, NT * NG, EG])

                ch(dve.tensor_tensor(cho[:], sc[:],
                                     gbias[:].rearrange("p (a e) -> p a e", a=1).to_broadcast([P, NT, E]), ALU.add))
                ch(dve.tensor_reduce(m1[:], g3(cho), AX.X, ALU.max))
                ch(dve.tensor_tensor(g3(eq), g3(cho), gb3(m1), ALU.is_equal))
                ch(dve.tensor_reduce(cnt[:], g3(eq), AX.X, ALU.add))
                ch(dve.scalar_tensor_tensor(work[:], eq[:], -BIG, cho[:], ALU.mult, ALU.add))
                ch(dve.tensor_reduce(m2[:], g3(work), AX.X, ALU.max))
                ch(dve.tensor_scalar(cnt[:], cnt[:], 1.5, None, ALU.is_gt))
                ch(dve.copy_predicated(m2[:], cnt[:].bitcast(I32), m1[:]))
                ch(dve.tensor_tensor(m1[:], m1[:], m2[:], ALU.add))
                gs = m1[:].rearrange("p (t g) -> p t g", g=NG)
                ch(dve.memset(rank[:], 0.0))
                for j in range(NG):
                    other = gs[:, :, j:j + 1]
                    if j + 1 < NG:
                        ch(dve.tensor_tensor(cmp[:, :, j + 1:NG], other.to_broadcast([P, NT, NG - j - 1]),
                                             gs[:, :, j + 1:NG], ALU.is_ge))
                    if j:
                        ch(dve.tensor_tensor(cmp[:, :, 0:j], other.to_broadcast([P, NT, j]), gs[:, :, 0:j], ALU.is_gt))
                    ch(dve.memset(cmp[:, :, j:j + 1], 0.0))
                    ch(dve.tensor_tensor(rank[:], rank[:], cmp[:], ALU.add))
                ch(dve.tensor_scalar(rank[:], rank[:], 1.5, None, ALU.is_lt))
                ch(dve.tensor_tensor(g3(work), g3(cho),
                                     rank[:].rearrange("p t (g a) -> p (t g) a", a=1).to_broadcast([P, NT * NG, EG]),
                                     ALU.mult))
                for t in range(NT):
                    dve.max(top8[:, t, :], work[:, t, :]).then_inc(rc, 1)
                ch.n += NT
                dve.wait_ge(rc, ch.n)
                for t in range(NT):
                    dve.match_replace(eq[:, t, :], top8[:, t, :], work[:, t, :], BIG).then_inc(rc, 1)
                ch.n += NT
                dve.wait_ge(rc, ch.n)
                ch(dve.tensor_scalar(eq[:], eq[:], BIG, None, ALU.is_ge))
                ch(dve.tensor_tensor(sc[:], sc[:], eq[:], ALU.mult))
                ch(dve.tensor_reduce(wsum[:], sc[:], AX.X, ALU.add))
                ch(dve.tensor_scalar(wsum[:], wsum[:], 1e-20, None, ALU.add))
                ch(dve.reciprocal(wsum[:], wsum[:]))
                ch(dve.tensor_scalar(wsum[:], wsum[:], 2.5, None, ALU.mult))
                ch(dve.tensor_tensor(sc[:], sc[:], wsum[:].rearrange("p (t a) -> p t a", a=1)
                                     .to_broadcast([P, NT, E]), ALU.mult))
                ch(dve.tensor_copy(wparts[:, :, 0, :], sc[:]))
                ch(dve.tensor_tensor(sc[:], sc[:], wparts[:, :, 0, :], ALU.subtract))
                ch(dve.tensor_copy(wparts[:, :, 1, :], sc[:]))
                dve.tensor_tensor(wparts[:, :, 2, :], sc[:], wparts[:, :, 1, :], ALU.subtract).then_inc(wp_ready, 1)

            @block.tensor
            def _(pe):
                pe.wait_ge(wp_ready, 1)
                for t in range(NT):
                    g = t // 8
                    if t % 8 == 0 and g >= 2:
                        pe.wait_ge(w_copied, g - 1)
                    pe.transpose(ps_w[g % 2][0:3 * E, (t % 8) * P:(t % 8 + 1) * P],
                                 wparts[:, t, :, :].rearrange("p j e -> p (j e)"), identb[:]).then_inc(w_ready, 1)

            @block.scalar
            def _(act):
                for g in range(NT // 8):
                    act.wait_ge(w_ready, 8 * (g + 1))
                    act.copy(wT[:, g * 1024:(g + 1) * 1024], ps_w[g % 2][0:3 * E, :]).then_inc(w_copied, 1)

        with ExitStack() as pctx, nc.Block() as block:
            def pt(name):
                return [pctx.enter_context(nc.psum_tensor(f"{name}{s}", [P, CH], F32)) for s in range(2)]
            ps_g, ps_u, ps_w = pt("p5_g"), pt("p5_u"), pt("p5_w")
            ps_f = pctx.enter_context(nc.psum_tensor("p5_f", [P, CH], F32))
            ps_t = pctx.enter_context(nc.psum_tensor("p5_t", [P, CH], F32))
            g_ready, u_ready, w_ready = (slots("p5_" + n) for n in ("g", "u", "w"))
            silu_done, prod_done, h_done, down_done = (
                slots("p5_" + n, True) for n in ("silu", "prod", "h", "down"))
            f_copied, ft_ready, ft_copied = (sem("p5_" + n, ONE) for n in ("fc", "ft", "ftc"))
            stat = sem("p5_stat")
            USES = (EALL - EALL // 2, EALL // 2)

            def uses(c, e):
                return e % 2, c * USES[e % 2] + e // 2

            def w_uses(c, e):
                return c * (EP // 2) + e // 2

            @block.sync
            def _(sp):
                sem.start(sp)

            @block.tensor
            def _(pe):
                def down(c, e):
                    s, n = uses(c, e)
                    pe.wait_ge(h_done[s], ONE + n + 1)
                    pe.matmul(ps_f[:], wd[:, e, :], hT[:, s, :], start=(e == 0), stop=(e == EP)) \
                        .then_inc(down_done[s], 1)

                with pe.Fori(0, NC) as c:
                    x_c = xnT[:, bass.ds(c * CH, CH)]
                    for e in range(EALL):
                        s, n = uses(c, e)
                        pe.wait_ge(silu_done[s], ONE + n)
                        pe.matmul(ps_g[s][:], wg[:, e * P:(e + 1) * P], x_c, start=True, stop=True) \
                            .then_inc(g_ready[s], 1)
                        pe.wait_ge(prod_done[s], ONE + n)
                        pe.matmul(ps_u[s][:], wu[:, e * P:(e + 1) * P], x_c, start=True, stop=True) \
                            .then_inc(u_ready[s], 1)
                        if e < EP:
                            pe.wait_ge(h_done[s], ONE + n)
                            pe.matmul(ps_w[s][:], esel[:, e * P:(e + 1) * P], wT[:, bass.ds(c * CH, CH)],
                                      start=True, stop=True).then_inc(w_ready[s], 1)
                        if e == 1:
                            pe.wait_ge(f_copied, ONE + c)
                        if e >= 1:
                            down(c, e - 1)
                    down(c, EP)
                    pe.wait_ge(f_copied, ONE + c + 1)
                    pe.wait_ge(ft_copied, ONE + c)
                    for t in range(CT):
                        last = pe.transpose(ps_t[:, t * P:(t + 1) * P], fT[:, t * P:(t + 1) * P], ident[:])
                    last.then_inc(ft_ready, 1)

            @block.scalar
            def _(act):
                with act.Fori(0, NC) as c:
                    for e in range(EALL):
                        s, n = uses(c, e)
                        act.wait_ge(g_ready[s], n + 1)
                        act.wait_ge(prod_done[s], ONE + n)
                        act.activation(silu[:, s, :], ps_g[s][:], ACT.Silu).then_inc(silu_done[s], 1)
                    s, n = uses(c, EP)
                    act.wait_ge(down_done[s], ONE + n + 1)
                    act.wait_ge(ft_ready, ONE + c)
                    act.copy(fT[:], ps_f[:]).then_inc(f_copied, 1)
                    act.wait_ge(ft_ready, ONE + c + 1)
                    act.sem_inc(carried, 1)
                    act.copy(y[:, bass.ds(CT * c, CT), :].rearrange("p t d -> p (t d)"), ps_t[:]) \
                        .then_inc(ft_copied, 1)

            @block.vector
            def _(dve):
                with dve.Fori(0, NC) as c:
                    for e in range(EALL):
                        s, n = uses(c, e)
                        dve.wait_ge(silu_done[s], ONE + n + 1)
                        dve.wait_ge(u_ready[s], n + 1)
                        if e < EP:
                            dve.tensor_tensor(prod[:, s, :], ps_u[s][:], silu[:, s, :], ALU.mult) \
                                .then_inc(prod_done[s], 1)
                            dve.wait_ge(prod_done[s], ONE + n + 1)
                            dve.wait_ge(w_ready[s], w_uses(c, e) + 1)
                            dve.wait_ge(down_done[s], ONE + n)
                            dve.tensor_tensor(hT[:, s, :], ps_w[s][:], prod[:, s, :], ALU.mult) \
                                .then_inc(h_done[s], 1)
                        else:
                            dve.wait_ge(down_done[s], ONE + n)
                            dve.tensor_tensor(prod[:, s, :], ps_u[s][:], silu[:, s, :], ALU.mult) \
                                .then_inc(prod_done[s], 1)
                            dve.wait_ge(prod_done[s], ONE + n + 1)
                            dve.tensor_copy(hT[:, s, :], prod[:, s, :]).then_inc(h_done[s], 1)
                    dve.wait_ge(ft_copied, ONE + c + 1)
                    for t in range(CT):
                        dve.bn_stats(st[:, bass.ds(CT * c + t, 1), :], y[:, bass.ds(CT * c + t, 1), :]) \
                            .then_inc(stat, 1)
                dve.wait_ge(stat, NT)


def program(nc, a, out):
    with ExitStack() as ctx:
        def sb(name, shape, dt):
            return ctx.enter_context(nc.sbuf_tensor(name, shape, dt))

        xs = sb("xs", [P, NT, P], F32)
        o_all = sb("o_all", [P, B * H * NQC * CT, DV], F32)
        ident = sb("ident_sb", [P, P], F32)
        identb = sb("identb", [P, P], BF16)
        with Semaphores(nc) as sem:
            attention_layer(nc, a, sb, None, sem, xs, o_all, ident, identb)
        with Semaphores(nc) as sem:
            later_layers(nc, a, sem, xs, o_all, ident, identb, out)


def kernel(**inputs):
    import numpy as np
    import concourse.bacc as bacc
    from concourse.bass_utils import run_bass_kernel_spmd

    f = {k: np.asarray(v) for k, v in inputs.items()}
    sel = np.zeros((P, DV + 1), np.float32)
    for base in (0, VC):
        for r in range(3 * DV):
            sel[base + r, r % DV] = 1
        sel[base + 3 * DV, DV] = 1
    esel = np.zeros((3 * E, EP * P), np.float32)
    for r in range(3 * E):
        esel[r, (r % E) * (P // 2):(r % E + 1) * (P // 2)] = 1
    tiles = lambda w: np.ascontiguousarray(w.reshape(-1, P, w.shape[-1]).transpose(1, 0, 2))
    arrays = {
        "x": f["L0_attn_x"].reshape(B * N, P),
        "wqkv": np.concatenate([f["L0_attn_Wq"], f["L0_attn_Wk"], f["L0_attn_Wv"]], 1),
        "sel": sel, "ident": np.eye(P, dtype=np.float32),
        "lqk": np.stack([f["L0_attn_" + k] for k in ("lq1", "lk1", "lq2", "lk2")]),
        "wo": f["L0_attn_Wo"],
        "lng": np.tile(f["L0_attn_ln_g"], H)[:, None], "lnb": np.tile(f["L0_attn_ln_b"], H)[:, None],
        "up": f["L0_ffn_w_up"].T, "down": tiles(f["L0_ffn_w_down"].T),
        "kw": tiles(f["L1_attn_k_weight"]), "qw": tiles(f["L1_attn_q_weight"]),
        "bias3": f["L1_attn_bias"], "w3": f["L1_attn_ln_weight"], "b3": f["L1_attn_ln_bias"],
        "gw": f["L1_ffn_gate_w"].T, "gb": f["L1_ffn_gate_bias"], "esel": esel,
        "wg": np.concatenate([f["L1_ffn_expert_gate"].reshape(-1, P), f["L1_ffn_shared_gate"]]).T,
        "wu": np.concatenate([f["L1_ffn_expert_up"].reshape(-1, P), f["L1_ffn_shared_up"]]).T,
        "wd": tiles(np.concatenate([f["L1_ffn_expert_down"].transpose(0, 2, 1).reshape(-1, P),
                                    f["L1_ffn_shared_down"].T])),
    }
    arrays = {k: np.ascontiguousarray(v) for k, v in arrays.items()}
    nc = bacc.Bacc("TRN2", target_bir_lowering=False, num_devices=1)
    a = {k: nc.dram_tensor("in_" + k, v.shape, F32, kind="ExternalInput").ap() for k, v in arrays.items()}
    a["x"] = a["x"].rearrange("(t p) d -> p t d", p=P)
    out = nc.dram_tensor("out", (B * N, P), F32, kind="ExternalOutput").ap()
    program(nc, a, out.rearrange("(t p) d -> p t d", p=P))
    r = run_bass_kernel_spmd(nc, [{"in_" + k: v for k, v in arrays.items()}], core_ids=[0])
    return r.results[0]["out"].reshape(B, N, P)
```

```python
import concourse.bass as bass
from concourse import mybir
from contextlib import ExitStack

F32 = mybir.dt.float32
BF16 = mybir.dt.bfloat16
F16 = mybir.dt.float16
I32 = mybir.dt.int32
ALU = mybir.AluOpType
ACT = mybir.ActivationFunctionType
AX = mybir.AxisListType
RMAX = bass.bass_isa.ReduceOp.max
RADD = bass.bass_isa.ReduceOp.add

P = 128
B = 2
N = 2048
NT = B * N // P
TB = NT // B
H = 8
S2 = 16
D = 8
DV = 16
ROW = 64
NSPLIT = 6
SH = NSPLIT * D
VC = 64
NQC = 4
KT = 16
RING = 4
SAFE = 40.0
ONE = 1
LAM_INIT = 0.8 - 0.6 * 2.718281828459045 ** (-0.3 * 12)


class Chain:

    def __init__(self, eng, sem, base=0):
        self.eng, self.sem, self.base, self.n = eng, sem, base, 0

    def __call__(self, ins):
        self.n += 1
        ins.then_inc(self.sem, 1)
        self.eng.wait_ge(self.sem, self.base + self.n)


class Semaphores:

    def __init__(self, nc):
        self.nc = nc

    def __enter__(self):
        self.handles, self.from_one = [], []
        return self

    def __call__(self, name, start=0):
        self.handles.append(self.nc.alloc_semaphore(name=name))
        if start == ONE:
            self.from_one.append(self.handles[-1])
        return self.handles[-1]

    def start(self, eng):
        for handle in self.from_one:
            eng.sem_inc(handle, ONE)
        self.from_one = []

    def __exit__(self, *_):
        with self.nc.Block() as block:
            @block.gpsimd
            def _(pool):
                for handle in self.handles:
                    pool.sem_clear(handle)
        for handle in self.handles:
            self.nc.release_semaphore(handle)


def pipelined(eng, front, back, n, base):
    half = n // 2
    front(0, 0, base)
    with eng.Fori(0, half - 1) as k:
        front(2 * k + 1, 1, base + k)
        back(2 * k, 0, base + k)
        front(2 * k + 2, 0, base + k + 1)
        back(2 * k + 1, 1, base + k)
    front(n - 1, 1, base + half - 1)
    back(n - 2, 0, base + half - 1)
    back(n - 1, 1, base + half - 1)


def pipelined_far(eng, front, back, n, base):
    half = n // 2
    front(0, 0, base)
    front(1, 1, base)
    with eng.Fori(0, half - 1) as k:
        front(2 * k + 2, 0, base + k + 1)
        back(2 * k, 0, base + k)
        front(2 * k + 3, 1, base + k + 1)
        back(2 * k + 1, 1, base + k)
    back(n - 2, 0, base + half - 1)
    back(n - 1, 1, base + half - 1)


def pipelined3(eng, first, second, third, n):
    half = n // 2
    first(0, 0, 0)
    first(1, 1, 0)
    second(0, 0, 0)
    with eng.Fori(0, half - 1) as k:
        first(2 * k + 2, 0, k + 1)
        second(2 * k + 1, 1, k)
        third(2 * k, 0, k)
        first(2 * k + 3, 1, k + 1)
        second(2 * k + 2, 0, k + 1)
        third(2 * k + 1, 1, k)
    second(n - 1, 1, half - 1)
    third(n - 2, 0, half - 1)
    third(n - 1, 1, half - 1)


def two_ahead(eng, first, second, n, third=None):
    def step(t, s, used):
        second(t, s, used)
        first(t + 2, s, used + 1)
        if third:
            third(t - 1, 1 - s, used - 1 + s)

    half = n // 2
    first(0, 0, 0)
    first(1, 1, 0)
    second(0, 0, 0)
    first(2, 0, 1)
    with eng.Fori(0, half - 2) as k:
        step(2 * k + 1, 1, k)
        step(2 * k + 2, 0, k + 1)
    step(n - 3, 1, half - 2)
    second(n - 2, 0, half - 1)
    if third:
        third(n - 3, 1, half - 2)
    second(n - 1, 1, half - 1)
    if third:
        third(n - 2, 0, half - 1)
        third(n - 1, 1, half - 1)


def mean_rstd(dve, ch, st, mean, var, tmp):
    ch(dve.tensor_tensor(mean, st[:, :, 1], st[:, :, 4], ALU.add))
    ch(dve.tensor_scalar(mean, mean, 0.5, None, ALU.mult))
    ch(dve.tensor_tensor(tmp, st[:, :, 1], mean, ALU.subtract))
    ch(dve.tensor_tensor(tmp, tmp, tmp, ALU.mult))
    ch(dve.tensor_tensor(var, st[:, :, 2], st[:, :, 5], ALU.add))
    ch(dve.tensor_scalar(var, var, 1.0 / P, None, ALU.mult))
    ch(dve.tensor_tensor(var, var, tmp, ALU.add))


def attention_layer(nc, a, sem, xs, o_all, ident, identb):
    with ExitStack() as ctx:
        def sbt(name, shape, dt):
            return ctx.enter_context(nc.sbuf_tensor(name, shape, dt))

        xn = sbt("xn", [P, NT, P], F32)
        wqkv = sbt("wqkv_sb", [P, 3 * P], F32)
        sel = sbt("sel_sb", [P, DV + 1], F32)
        lqk = sbt("lqk_sb", [P, 4, D], F32)
        lam = sbt("lam", [P, 1], F32)
        lam4 = sbt("lam4", [P, 6], F32)
        st = sbt("st", [P, NT, 6], F32)
        mean = sbt("mean", [P, NT], F32)
        var = sbt("var", [P, NT], F32)
        vtmp = sbt("vtmp", [P, NT], F32)
        rstd = sbt("rstd", [P, NT], F32)
        xslot = sbt("xslot", [P, 2, P], F32)
        xnT = sbt("xnT", [P, 2, P], F32)
        qkv = sbt("qkv", [P, 2, 3 * P], F32)
        rest = sbt("rest", [P, 2, 3 * P], F32)
        parts = sbt("parts", [P, 2, 3, 3 * P], BF16)
        q_rows = sbt("q_rows", [P, 2, S2, ROW], BF16)
        k_rows = sbt("k_rows", [P, 2, S2, ROW], BF16)
        sq = sbt("sq", [P, 2, 2 * P], F32)
        norms = sbt("norms", [P, TB, 2 * S2], F32)
        nmax = sbt("nmax", [P, 2 * S2], F32)
        nall = sbt("nall", [P, 2 * S2], F32)
        bound = sbt("bound", [P, 2], F32)
        state = sbt("state", [P, 2], F32)
        state_i = sbt("state_i", [P, 2], I32)
        QT = sbt("QT", [P, H, N], BF16)
        KTa = sbt("KTa", [P, H, N], BF16)
        V = sbt("V", [P, TB, H, VC], BF16)
        kts = sbt("kts", [P, N], BF16)
        qts = sbt("qts", [P, 2, 2, 512], BF16)
        vts = sbt("vts", [P, KT, VC], BF16)
        V32 = sbt("V32", [P, TB, P], F32)
        vts32 = sbt("vts32", [P, KT // RING, VC], F32)
        prob = sbt("prob", [P, RING, 1024], F32)
        low = sbt("low", [P, RING - 1, 1024], BF16)
        stack = sbt("stack", [P, 1024], F32)
        rec = sbt("rec", [P, 8], F32)
        onrm = sbt("onrm", [P, 8, DV], F32)
        ot = sbt("ot", [P, 4, DV], F32)
        shift = sbt("shift", [P, TB, S2], F32)
        shparts = sbt("shparts", [P, TB, 3, S2], BF16)

        loaded = sem("attn_loaded")
        x_loaded = [sem(f"x_loaded{c}") for c in range(4)]
        negated = sem("a_negated")
        normalised = sem("a_normalised")
        dve_done = sem("a_dve")
        preset = sem("a_preset")
        mv_ready = sem("a_mv_ready")
        lam_sum = sem("lam_sum")
        lam_exp = sem("lam_exp")
        rstd_done = sem("a_rstd")

        x_in = [sem(f"x_in{s}") for s in range(2)]
        xT_ready = [sem(f"xT_ready{s}", ONE) for s in range(2)]
        xT_copied = [sem(f"xT_copied{s}", ONE) for s in range(2)]
        qkv_ready = [sem(f"qkv_ready{s}") for s in range(2)]
        qkv_copied = [sem(f"qkv_copied{s}") for s in range(2)]
        squared = [sem(f"squared{s}", ONE) for s in range(2)]
        split_done = [sem(f"split_done{s}", ONE) for s in range(2)]
        build_chain = sem("build_chain")
        norms_done = [sem(f"norms_done{s}", ONE) for s in range(2)]
        q_rows_done = [sem(f"q_rows_done{s}", ONE) for s in range(2)]
        k_rows_done = [sem(f"k_rows_done{s}", ONE) for s in range(2)]
        v_done = [sem(f"v_done{s}", ONE) for s in range(2)]
        qT_ready = [sem(f"qT_ready{s}", ONE) for s in range(2)]
        kT_ready = [sem(f"kT_ready{s}", ONE) for s in range(2)]
        qT_copied = [sem(f"qT_copied{s}", ONE) for s in range(2)]
        kT_copied = [sem(f"kT_copied{s}", ONE) for s in range(2)]
        nmax_ready = sem("nmax_ready")
        carried = sem("carried")
        nall_ready = sem("nall_ready")
        bound_chain = sem("bound_chain")

        keys_masked = sem("keys_masked")
        all_scores = [sem(f"all_scores{s}") for s in range(2)]
        max_taken = [sem(f"max_taken{s}", ONE) for s in range(2)]
        shift_chain = sem("shift_chain")
        shift_split = sem("shift_split")
        shift_T = sem("shift_T")
        shift_copied = sem("shift_copied")
        shift_rows = sem("shift_rows")

        q_in = [sem(f"q_in{r}") for r in range(2)]
        k_in = [sem(f"k_in{c}") for c in range(4)]
        v_in = [sem(f"v_in{c}") for c in range(4)]
        q_free = [sem(f"q_free{r}", ONE) for r in range(2)]
        k_free = [sem(f"k_free{c}", ONE) for c in range(4)]
        v_free = [sem(f"v_free{c}", ONE) for c in range(4)]
        scores_ready = [sem(f"scores_ready{s}") for s in range(2)]
        exp_done = [sem(f"exp_done{s}", ONE) for s in range(RING)]
        low_done = [sem(f"low_done{s}") for s in range(RING - 1)]
        pv_done = [sem(f"pv_done{s}", ONE) for s in range(RING)]
        evac0 = sem("evac0", ONE)
        evac1 = sem("evac1", ONE)
        t_ready = sem("t_ready", ONE)
        norm_chain = sem("norm_chain", ONE)

        HALF = NT // 2

        with nc.Block() as block:
            @block.sync
            def _(sp):
                for c in range(4):
                    sp.dma_start(xs[:, 8 * c:8 * c + 8, :], a["x"][:, 8 * c:8 * c + 8, :]).then_inc(x_loaded[c], 16)
                sp.dma_start(wqkv[:], a["wqkv"]).then_inc(loaded, 16)
                sp.dma_start(sel[:], a["sel"]).then_inc(loaded, 16)
                sp.dma_start(ident[:], a["ident"]).then_inc(loaded, 16)
                sp.dma_start(lqk[:], a["lqk"].partition_broadcast(P)).then_inc(loaded, 16)

            @block.gpsimd
            def _(pool):
                pool.memset(q_rows[:], 0.0).then_inc(preset, 1)
                pool.memset(k_rows[:], 0.0).then_inc(preset, 1)
                pool.memset(V[:], 0.0).then_inc(preset, 1)
                pool.memset(qts[:], 0.0).then_inc(preset, 1)
                pool.memset(vts32[:], 0.0).then_inc(preset, 1)
                pool.wait_ge(preset, 5)
                pool.memset(vts32[:, :, 3 * DV:3 * DV + 1], 1.0).then_inc(preset, 1)
                pool.memset(k_rows[:, :, :, SH:SH + 3], 1.0).then_inc(preset, 1)
                pool.memset(V[:, :, :, 3 * DV:3 * DV + 1], 1.0).then_inc(preset, 1)
                sem.start(pool)

            @block.scalar
            def _(act):
                act.wait_ge(lam_sum, 1)
                act.activation(lam4[:, 2:4], lam4[:, 0:2], ACT.Exp).then_inc(lam_exp, 1)
                act.wait_ge(mv_ready, 1)
                act.activation(rstd[:], var[:], ACT.Sqrt).then_inc(rstd_done, 1)
                act.wait_ge(negated, 1)
                act.wait_ge(x_loaded[3], 16)
                for t in range(HALF, NT):
                    act.activation(xn[:, t, :], xs[:, t, :], ACT.Identity, bias=vtmp[:, t:t + 1],
                                   scale=rstd[:, t:t + 1]).then_inc(normalised, 1)
                act.wait_ge(normalised, NT - HALF)

            @block.vector
            def _(dve):
                ch = Chain(dve, dve_done)
                dve.wait_ge(loaded, 16 * 4)
                ch(dve.tensor_copy(identb[:], ident[:]))
                ch(dve.memset(state[:], 0.0))
                ch(dve.tensor_tensor(lqk[:, 0::2, :], lqk[:, 0::2, :], lqk[:, 1::2, :], ALU.mult))
                dve.tensor_reduce(lam4[:, 0:2], lqk[:, 0::2, :], AX.X, ALU.add).then_inc(lam_sum, 1)
                for t in range(NT):
                    if t % 8 == 0:
                        dve.wait_ge(x_loaded[t // 8], 16)
                    dve.bn_stats(st[:, t, :], xs[:, t, :]).then_inc(dve_done, 1)
                ch.n += NT
                dve.wait_ge(dve_done, ch.n)
                mean_rstd(dve, ch, st, mean[:], var[:], vtmp[:])
                dve.tensor_scalar(var[:], var[:], 1e-5, None, ALU.add).then_inc(mv_ready, 1)
                dve.wait_ge(lam_exp, 1)
                ch(dve.tensor_tensor(lam4[:, 4:5], lam4[:, 2:3], lam4[:, 3:4], ALU.subtract))
                ch(dve.tensor_scalar(lam[:], lam4[:, 4:5], LAM_INIT, None, ALU.add))
                dve.wait_ge(rstd_done, 1)
                ch(dve.reciprocal(rstd[:], rstd[:]))
                dve.scalar_tensor_tensor(vtmp[:], mean[:], -1.0, rstd[:], ALU.mult, ALU.mult).then_inc(negated, 1)
                for t in range(HALF):
                    dve.tensor_scalar(xn[:, t, :], xs[:, t, :], mean[:, t:t + 1], rstd[:, t:t + 1],
                                      ALU.subtract, ALU.mult).then_inc(dve_done, 1)
                ch.n += HALF
                dve.wait_ge(dve_done, ch.n)

        with nc.Fori(0, B) as b:
            with ExitStack() as pctx, nc.Block() as block:
                def pt(name, shape, dt):
                    return pctx.enter_context(nc.psum_tensor(name, shape, dt))
                ps_x = [pt(f"ps_x{s}", [P, 512], F32) for s in range(2)]
                ps_qkv = [pt(f"ps_qkv{s}", [P, 512], F32) for s in range(2)]
                ps_q = [pt(f"ps_q{s}", [P, 1024], BF16) for s in range(2)]
                ps_k = [pt(f"ps_k{s}", [P, 1024], BF16) for s in range(2)]
                HB = TB // 2

                def row_groups(rows, s, lo, hi, step):
                    return rows[:, s, :, :].rearrange("p n (g d) -> p n g d", d=D)[:, :, lo:hi:step, :]

                def part_groups(s, j, o, n):
                    return parts[:, s, j, o * P:(o + 1) * P].rearrange("p (n a d) -> p n a d", a=1, d=D) \
                        .to_broadcast([P, S2, n, D])

                @block.sync
                def _(sp):
                    with sp.Fori(0, HB) as k:
                        for s in range(2):
                            sp.wait_ge(xT_ready[s], ONE + b * HB + k)
                            sp.dma_start(xslot[:, s, :], xn[:, bass.ds(b * TB + 2 * k + s, 1), :]
                                         .rearrange("p a d -> p (a d)")).then_inc(x_in[s], 16)

                @block.tensor
                def _(pe):
                    def front(t, s, used):
                        pe.wait_ge(x_in[s], 16 * (used + 1))
                        pe.wait_ge(xT_copied[s], ONE + used)
                        pe.transpose(ps_x[s][:, 0:P], xslot[:, s, :], ident[:]).then_inc(xT_ready[s], 1)
                        pe.wait_ge(xT_copied[s], ONE + used + 1)
                        pe.wait_ge(squared[s], ONE + used)
                        pe.matmul(ps_qkv[s][:, 0:3 * P], xnT[:, s, :], wqkv[:], start=True, stop=True) \
                            .then_inc(qkv_ready[s], 1)

                    def back(t, s, used):
                        pe.wait_ge(q_rows_done[s], ONE + used + 1)
                        pe.wait_ge(qT_copied[s], ONE + used)
                        for h in range(H):
                            last = pe.transpose(ps_q[s][:, h * P:(h + 1) * P],
                                                q_rows[:, s, 2 * h:2 * h + 2, :].rearrange("p a r -> p (a r)"),
                                                identb[:])
                        last.then_inc(qT_ready[s], 1)
                        pe.wait_ge(k_rows_done[s], ONE + used + 1)
                        pe.wait_ge(kT_copied[s], ONE + used)
                        for h in range(H):
                            last = pe.transpose(ps_k[s][:, h * P:(h + 1) * P],
                                                k_rows[:, s, 2 * h:2 * h + 2, :].rearrange("p a r -> p (a r)"),
                                                identb[:])
                        last.then_inc(kT_ready[s], 1)

                    pipelined_far(pe, front, back, TB, b * HB)

                @block.scalar
                def _(act):
                    def front(t, s, used):
                        act.wait_ge(xT_ready[s], ONE + used + 1)
                        act.copy(xnT[:, s, :], ps_x[s][:, 0:P]).then_inc(xT_copied[s], 1)
                        act.wait_ge(qkv_ready[s], used + 1)
                        act.wait_ge(split_done[s], ONE + used)
                        act.wait_ge(norms_done[s], ONE + used)
                        act.mul(qkv[:, s, 0:P], ps_qkv[s][:, 0:P], D ** -0.5).then_inc(qkv_copied[s], 1)
                        act.copy(qkv[:, s, P:3 * P], ps_qkv[s][:, P:3 * P]).then_inc(qkv_copied[s], 1)
                        if s == 1:
                            act.copy(V32[:, bass.ds(t, 1), :].rearrange("p a n -> p (a n)"),
                                     ps_qkv[s][:, 2 * P:3 * P])
                        act.wait_ge(qkv_copied[s], 2 * (used + 1))
                        act.activation(sq[:, s, :], qkv[:, s, 0:2 * P], ACT.Square).then_inc(squared[s], 1)

                    def back(t, s, used):
                        act.wait_ge(split_done[s], ONE + used + 1)
                        act.sem_inc(carried, 1)
                        act.copy(V[:, bass.ds(t, 1), :, 0:3 * DV].rearrange("p a h (j d) -> p (a h) j d", j=3),
                                 parts[:, s, :, 2 * P:3 * P].rearrange("p j (h d) -> p h j d", d=DV)) \
                            .then_inc(v_done[s], 1)
                        act.wait_ge(kT_ready[s], ONE + used)
                        for n, (j, lo, hi, step) in enumerate(((0, 0, 4, 3), (0, 5, 6, 1), (1, 1, 5, 3), (2, 2, 3, 1))):
                            last = act.copy(row_groups(k_rows, s, lo, hi, step), part_groups(s, j, 1, (hi - lo + step - 1) // step))
                        last.then_inc(k_rows_done[s], 1)

                    pipelined(act, front, back, TB, b * HB)

                @block.vector
                def _(dve):
                    def front(t, s, used):
                        c = (b * TB + t) * 3
                        dve.wait_ge(qkv_copied[s], 2 * (used + 1))
                        dve.wait_ge(q_rows_done[s], ONE + used)
                        dve.wait_ge(k_rows_done[s], ONE + used)
                        dve.wait_ge(v_done[s], ONE + used)
                        hi, mid, lo = (parts[:, s, k, :] for k in range(3))
                        dve.tensor_copy(hi, qkv[:, s, :]).then_inc(build_chain, 1)
                        dve.wait_ge(build_chain, c + 1)
                        dve.tensor_tensor(rest[:, s, :], qkv[:, s, :], hi, ALU.subtract).then_inc(build_chain, 1)
                        dve.wait_ge(build_chain, c + 2)
                        dve.tensor_copy(mid, rest[:, s, :]).then_inc(build_chain, 1)
                        dve.wait_ge(build_chain, c + 3)
                        dve.tensor_tensor(lo, rest[:, s, :], mid, ALU.subtract).then_inc(split_done[s], 1)
                        dve.wait_ge(squared[s], ONE + used + 1)
                        dve.tensor_reduce(norms[:, bass.ds(t, 1), :].rearrange("p a n -> p (a n)"),
                                          sq[:, s, :].rearrange("p (n d) -> p n d", d=D), AX.X, ALU.add) \
                            .then_inc(norms_done[s], 1)

                    def back(t, s, used):
                        dve.wait_ge(qT_ready[s], ONE + used + 1)
                        dve.tensor_copy(QT[:, :, bass.ds(t * P, P)],
                                        ps_q[s][:].rearrange("p (h t) -> p h t", h=H)).then_inc(qT_copied[s], 1)
                        dve.wait_ge(kT_ready[s], ONE + used + 1)
                        dve.tensor_copy(KTa[:, :, bass.ds(t * P, P)],
                                        ps_k[s][:].rearrange("p (h t) -> p h t", h=H)).then_inc(kT_copied[s], 1)

                    pipelined_far(dve, front, back, TB, b * HB)
                    dve.wait_ge(norms_done[0], ONE + (b + 1) * HB)
                    dve.wait_ge(norms_done[1], ONE + (b + 1) * HB)
                    dve.tensor_reduce(nmax[:], norms[:].rearrange("p t n -> p n t"), AX.X, ALU.max) \
                        .then_inc(nmax_ready, 1)
                    dve.wait_ge(nall_ready, b + 1)
                    c = b * 8
                    dve.tensor_tensor(nall[:, 0:S2], nall[:, 0:S2], nall[:, S2:2 * S2], ALU.mult) \
                        .then_inc(bound_chain, 1)
                    dve.wait_ge(bound_chain, c + 1)
                    dve.tensor_reduce(bound[:, 0:1], nall[:, 0:S2], AX.X, ALU.max).then_inc(bound_chain, 1)
                    dve.wait_ge(bound_chain, c + 2)
                    dve.tensor_tensor(state[:, 0:1], state[:, 0:1], state[:, 1:2], ALU.add).then_inc(bound_chain, 1)
                    dve.wait_ge(bound_chain, c + 3)
                    dve.tensor_scalar(bound[:, 1:2], bound[:, 0:1], SAFE * SAFE, None, ALU.is_le) \
                        .then_inc(bound_chain, 1)
                    dve.wait_ge(bound_chain, c + 4)
                    dve.tensor_scalar(state[:, 1:2], bound[:, 1:2], -1.0, 1.0, ALU.mult, ALU.add) \
                        .then_inc(bound_chain, 1)
                    dve.wait_ge(bound_chain, c + 5)
                    dve.tensor_copy(state_i[:], state[:]).then_inc(bound_chain, 3)

                @block.gpsimd
                def _(pool):
                    with pool.Fori(0, HB) as k:
                        for s in range(2):
                            used = b * HB + k
                            t = 2 * k + s
                            pool.wait_ge(split_done[s], ONE + used + 1)
                            pool.wait_ge(qT_ready[s], ONE + used)
                            pool.sem_inc(carried, 1)
                            for j, lo, hi in ((0, 0, 3), (1, 3, 5), (2, 5, 6)):
                                last = pool.tensor_copy(row_groups(q_rows, s, lo, hi, 1), part_groups(s, j, 0, hi - lo))
                            last.then_inc(q_rows_done[s], 1)
                    pool.wait_ge(nmax_ready, b + 1)
                    pool.sem_inc(carried, 1)
                    pool.partition_all_reduce(nall[:], nmax[:], P, RMAX).then_inc(nall_ready, 1)

            with ExitStack() as pctx, nc.Block() as block:
                ps_m = [pctx.enter_context(nc.psum_tensor(f"ps_m{s}", [P, N], F32)) for s in range(2)]
                HEADS = 2 * H
                PAIRS = TB // 2

                @block.tensor
                def _(pe):
                    m = pe.value_load(state_i[0:1, 0:1], min_val=0, max_val=1)
                    with pe.If(pe.value_load(state_i[0:1, 1:2], min_val=0, max_val=1) > 0):
                        for i in range(2):
                            with pe.Fori(0, H) as h:
                                head = m * HEADS + i * H + h
                                pe.wait_ge(keys_masked, head + 1)
                                pe.sem_inc(carried, 1)
                                with pe.Fori(0, PAIRS) as k:
                                    for s in range(2):
                                        pe.wait_ge(max_taken[s], ONE + head * PAIRS + k)
                                        for c in range(4):
                                            last = pe.matmul(ps_m[s][:, 512 * c:512 * (c + 1)],
                                                             QT[:, bass.ds(h, 1), bass.ds((2 * k + s) * P, P)]
                                                             .rearrange("p a n -> p (a n)"),
                                                             kts[:, 512 * c:512 * (c + 1)], start=True, stop=True)
                                        last.then_inc(all_scores[s], 1)
                        pe.wait_ge(shift_split, m + 1)
                        pe.sem_inc(carried, 1)
                        for t in range(TB):
                            last = pe.transpose(ps_m[0][0:3 * S2, t * P // 2:(t + 1) * P // 2].bitcast(BF16),
                                                shparts[:, t, :, :].rearrange("p j n -> p (j n)"), identb[:])
                        last.then_inc(shift_T, 1)

                @block.vector
                def _(dve):
                    m = dve.value_load(state_i[0:1, 0:1], min_val=0, max_val=1)
                    with dve.If(dve.value_load(state_i[0:1, 1:2], min_val=0, max_val=1) > 0):
                        for i in range(2):
                            dve.memset(kts[:], 0.0).then_inc(shift_chain, 1)
                            dve.wait_ge(shift_chain, m * 6 + i + 1)
                            dve.sem_inc(carried, 1)
                            with dve.Fori(0, H) as h:
                                head = m * HEADS + i * H + h
                                rows = slice(ROW * i, ROW * (i + 1))
                                dve.tensor_copy(kts[rows, :], KTa[rows, bass.ds(h, 1), :]
                                                .rearrange("p a n -> p (a n)")).then_inc(keys_masked, 1)
                                with dve.Fori(0, PAIRS) as k:
                                    for s in range(2):
                                        dve.wait_ge(all_scores[s], head * PAIRS + k + 1)
                                        dve.tensor_reduce(shift[:, bass.ds(2 * k + s, 1), bass.ds(i * H + h, 1)]
                                                          .rearrange("p a n -> p (a n)"),
                                                          ps_m[s][:], AX.X, ALU.max, negate=True) \
                                            .then_inc(max_taken[s], 1)
                            for s in range(2):
                                dve.wait_ge(max_taken[s], ONE + (m * HEADS + (i + 1) * H) * PAIRS)
                        dve.tensor_copy(shparts[:, :, 0, :], shift[:]).then_inc(shift_chain, 1)
                        dve.wait_ge(shift_chain, m * 6 + 3)
                        dve.tensor_tensor(shift[:], shift[:], shparts[:, :, 0, :], ALU.subtract) \
                            .then_inc(shift_chain, 1)
                        dve.wait_ge(shift_chain, m * 6 + 4)
                        dve.tensor_copy(shparts[:, :, 1, :], shift[:]).then_inc(shift_chain, 1)
                        dve.wait_ge(shift_chain, m * 6 + 5)
                        dve.tensor_tensor(shift[:], shift[:], shparts[:, :, 1, :], ALU.subtract) \
                            .then_inc(shift_chain, 1)
                        dve.wait_ge(shift_chain, m * 6 + 6)
                        dve.tensor_copy(shparts[:, :, 2, :], shift[:]).then_inc(shift_split, 1)

                @block.scalar
                def _(act):
                    m = act.value_load(state_i[0:1, 0:1], min_val=0, max_val=1)
                    with act.If(act.value_load(state_i[0:1, 1:2], min_val=0, max_val=1) > 0):
                        act.wait_ge(shift_T, m + 1)
                        act.copy(low[0:3 * S2, 0:2, :].rearrange("p r n -> p (r n)"),
                                 ps_m[0][0:3 * S2, 0:N // 2].bitcast(BF16)).then_inc(shift_copied, 1)

                @block.sync
                def _(sp):
                    m = sp.value_load(state_i[0:1, 0:1], min_val=0, max_val=1)
                    with sp.If(sp.value_load(state_i[0:1, 1:2], min_val=0, max_val=1) > 0):
                        sp.wait_ge(shift_copied, m + 1)
                        for j in range(3):
                            for i in range(2):
                                row = j * S2 + i * H
                                sp.dma_start(QT[ROW * i + SH + j:ROW * i + SH + j + 1, :, :],
                                             low[row:row + H, 0:2, :]).then_inc(shift_rows, 16)
                        sp.wait_ge(shift_rows, (m + 1) * 6 * 16)
                        sp.sem_inc(carried, 1)

            with ExitStack() as pctx, nc.Block() as block:
                def pt(name, shape, dt):
                    return pctx.enter_context(nc.psum_tensor(name, shape, dt))
                ps_s = pt("ps_s", [P, 4, 512], F32)
                ps_o = pt("ps_o", [P, 2, 512], F32)
                ps_t = pt("ps_t", [P, 512], F32)
                NU = 2 * H
                G = 32

                @block.sync
                def _(sp):
                    with sp.Fori(0, H) as h:
                        with sp.Fori(0, 2) as qp:
                            U = b * NU + h * 2 + qp

                            def load_q(r):
                                sp.wait_ge(q_free[r], ONE + U)
                                for i in range(2):
                                    rows = slice(ROW * i, ROW * (i + 1))
                                    sp.dma_start(qts[rows, r, i, :],
                                                 QT[rows, bass.ds(h, 1), bass.ds(qp * 1024 + r * 512, 512)]
                                                 .rearrange("p a n -> p (a n)")).then_inc(q_in[r], 16)
                            load_q(0)
                            for c in range(4):
                                sp.wait_ge(k_free[c], ONE + U)
                                sp.dma_start(kts[:, c * 512:(c + 1) * 512],
                                             KTa[:, bass.ds(h, 1), c * 512:(c + 1) * 512]
                                             .rearrange("p a n -> p (a n)")).then_inc(k_in[c], 16)
                                sp.wait_ge(v_free[c], ONE + U)
                                sp.dma_start(vts[:, 4 * c:4 * c + 4, :],
                                             V[:, 4 * c:4 * c + 4, bass.ds(h, 1), :]
                                             .rearrange("p t a n -> p t (a n)")).then_inc(v_in[c], 16)
                                sp.dma_start(vts32[:, c, 0:DV],
                                             V32[:, RING * c + RING - 1, bass.ds(h * DV, DV)]).then_inc(v_in[c], 16)
                            load_q(1)

                @block.tensor
                def _(pe):
                    def scores(u, x):
                        U, x = b * NU + u + x // G, x % G
                        r, kt = x // KT, x % KT
                        if kt == 0:
                            pe.wait_ge(q_in[r], 32 * (U + 1))
                        if r == 0 and kt % 4 == 0:
                            pe.wait_ge(k_in[kt // 4], 16 * (U + 1))
                        y = x - 2
                        pe.wait_ge(exp_done[y % RING], ONE + U * (G // RING) + y // RING + 1)
                        for i in range(2):
                            last = pe.matmul(ps_s[:, 2 * (x % 2) + i, :], kts[:, kt * P:(kt + 1) * P], qts[:, r, i, :],
                                             start=True, stop=True)
                        last.then_inc(scores_ready[x % 2], 1)

                    def values(u, x):
                        U, x = b * NU + u + x // G, x % G
                        r, kt, slot = x // KT, x % KT, x % RING
                        if r == 0 and kt % 4 == 0:
                            pe.wait_ge(v_in[kt // 4], 32 * (U + 1))
                        if kt == 0:
                            pe.wait_ge(evac0, ONE + U * 2 + r)
                            pe.wait_ge(evac1, ONE + U * 2 + r)
                        pe.wait_ge(exp_done[slot], ONE + U * (G // RING) + x // RING + 1)
                        if slot == RING - 1:
                            for i in range(2):
                                last = pe.matmul(ps_o[64 * i:64 * (i + 1), i, :], vts32[:, kt // RING, :],
                                                 prob[:, slot, 512 * i:512 * (i + 1)], start=False,
                                                 stop=(kt == KT - 1))
                                if i == 0 and r == 1:
                                    last.then_inc(k_free[kt // 4], 1)
                            last.then_inc(pv_done[slot], 1)
                            return
                        pe.wait_ge(low_done[slot], U * (G // RING) + x // RING + 1)
                        for i in range(2):
                            high = prob[:, slot, 512 * i:512 * (i + 1)].bitcast(BF16)[:, 1::2]
                            mm = pe.matmul(ps_o[0:64, i, :], vts[:, kt, :], high, start=(kt == 0),
                                           stop=(kt == KT - 2 and i == 1))
                            if i == 0 and r == 1 and kt % 4 == 0 and kt:
                                mm.then_inc(v_free[kt // 4 - 1], 1)
                            if i == 1 and kt == KT - 2:
                                mm.then_inc(q_free[r], 1)
                            last = pe.matmul(ps_o[64:128, i, :], vts[:, kt, :], low[:, slot, 512 * i:512 * (i + 1)],
                                             start=(kt == 0), stop=(kt == KT - 2 and i == 0))
                        last.then_inc(pv_done[slot], 1)

                    def totals(u, r, part):
                        n = (b * NU + u) * 2 + r
                        if part == 0:
                            pe.wait_ge(evac0, ONE + n + 1)
                            pe.wait_ge(evac1, ONE + n + 1)
                            pe.wait_ge(norm_chain, ONE + 4 * n)
                        for i in range(2 * part, 2 * part + 2):
                            last = pe.matmul(ps_t[:, i * (DV + 1):(i + 1) * (DV + 1)], stack[:, i * P:(i + 1) * P],
                                             sel[:], start=True, stop=True)
                            if r == 1 and i == 0:
                                last.then_inc(v_free[3], 1)
                        if part == 3:
                            last.then_inc(t_ready, 1)

                    AHEAD, T = 4, 4

                    def step(u, x, more=True):
                        values(u, x)
                        if more or x + AHEAD < G:
                            scores(u, x + AHEAD)
                        if KT <= x < KT + 4:
                            totals(u, 0, x - KT)
                        if x >= G:
                            totals(u, 1, x - G)

                    for x in range(AHEAD):
                        scores(0, x)
                    for x in range(T):
                        step(0, x)
                    with pe.Fori(0, NU - 1) as u:
                        for x in range(T, G + T):
                            step(u, x)
                    for x in range(T, G):
                        step(NU - 1, x, more=False)
                    for part in range(4):
                        totals(NU - 1, 1, part)

                @block.scalar
                def _(act):
                    def exps(u, x):
                        U, x = b * NU + u + x // G, x % G
                        slot = x % RING
                        act.wait_ge(scores_ready[x % 2], U * (G // 2) + x // 2 + 1)
                        act.wait_ge(pv_done[slot], ONE + U * (G // RING) + x // RING)
                        act.activation(prob[:, slot, :],
                                       ps_s[:, 2 * (x % 2):2 * (x % 2) + 2, :].rearrange("p a n -> p (a n)"),
                                       ACT.Exp).then_inc(exp_done[slot], 1)

                    def evacuate(u, r):
                        U = b * NU + u
                        x = KT * r + KT - 1
                        act.wait_ge(pv_done[x % RING], ONE + U * (G // RING) + x // RING + 1)
                        act.wait_ge(t_ready, ONE + U * 2 + r)
                        act.copy(stack[:, 0:512], ps_o[:, 0, :]).then_inc(evac0, 1)

                    def step(u, x):
                        exps(u, x)
                        if x == KT + 2:
                            evacuate(u, 0)
                        if x == G + 2:
                            evacuate(u, 1)

                    for x in range(3):
                        exps(0, x)
                    with act.Fori(0, NU - 1) as u:
                        for x in range(3, G + 3):
                            step(u, x)
                    for x in range(3, G):
                        step(NU - 1, x)
                    evacuate(NU - 1, 1)

                @block.vector
                def _(dve):
                    def lows(u, x):
                        U, x = b * NU + u + x // G, x % G
                        slot = x % RING
                        if slot == RING - 1:
                            return
                        dve.wait_ge(exp_done[slot], ONE + U * (G // RING) + x // RING + 1)
                        dve.tensor_tensor(low[:, slot, :], prob[:, slot, :], prob[:, slot, :].bitcast(BF16)[:, 1::2],
                                          ALU.subtract).then_inc(low_done[slot], 1)

                    def evacuate(u, r):
                        U = b * NU + u
                        x = KT * r + KT - 1
                        dve.wait_ge(pv_done[x % RING], ONE + U * (G // RING) + x // RING + 1)
                        dve.wait_ge(t_ready, ONE + U * 2 + r)
                        dve.tensor_copy(stack[:, 512:1024], ps_o[:, 1, :]).then_inc(evac1, 1)

                    def normalise(u, r):
                        U = b * NU + u
                        c = (U * 2 + r) * 4
                        tot = ps_t[:, 0:8 * (DV + 1)].rearrange("p (i n) -> p i n", n=DV + 1)
                        dve.wait_ge(t_ready, ONE + U * 2 + r + 1)
                        dve.reciprocal(rec[:], tot[:, :, DV]).then_inc(norm_chain, 1)
                        dve.wait_ge(norm_chain, ONE + c + 1)
                        dve.tensor_tensor(onrm[:], tot[:, :, 0:DV],
                                          rec[:].rearrange("p (i a) -> p i a", a=1).to_broadcast([P, 8, DV]),
                                          ALU.mult).then_inc(norm_chain, 1)
                        dve.wait_ge(norm_chain, ONE + c + 2)
                        dve.tensor_scalar(ot[:], onrm[:, 4:8, :], lam[:], None, ALU.mult).then_inc(norm_chain, 1)
                        dve.wait_ge(norm_chain, ONE + c + 3)
                        dve.tensor_tensor(o_all[:, bass.ds(U * 8 + r * 4, 4), :], onrm[:, 0:4, :], ot[:],
                                          ALU.subtract).then_inc(norm_chain, 1)

                    E, NRM = KT, 22

                    def step(u, x):
                        lows(u, x)
                        if x == KT:
                            evacuate(u, 0)
                        if x == NRM:
                            normalise(u, 0)
                        if x == KT + KT:
                            evacuate(u, 1)
                        if x == KT + NRM:
                            normalise(u, 1)

                    for x in range(7):
                        lows(0, x)
                    with dve.Fori(0, NU - 1) as u:
                        for x in range(7, G + 7):
                            step(u, x)
                    for x in range(7, G):
                        step(NU - 1, x)
                    evacuate(NU - 1, 1)
                    normalise(NU - 1, 1)



FF = 512
NK3 = 512
KF = FF // P
CH = 512
CT = CH // P
NC = B * N // CH
E = 32
EP = E // 2
EALL = EP + 1
X_SCALE = 256.0
W_SCALE = 1024.0
TWO_OVER_PI = 0.6366197723675814


def add_normalised(nc, sem, name, xs, y, st, scalars, factor=None, out=None):
    mean, var, tmp, rstd = scalars
    chain = sem(name + "_dve")
    var_ready = sem(name + "_var_ready")
    rstd_done = sem(name + "_rstd_done")
    shifted = sem(name + "_shifted")
    stored = sem(name + "_stored")
    group_end = []
    with nc.Block() as block:
        @block.vector
        def _(dve):
            ch = Chain(dve, chain)
            mean_rstd(dve, ch, st, mean, var, tmp)
            if factor is not None:
                ch(dve.tensor_tensor(var, var, factor, ALU.mult))
                ch(dve.tensor_tensor(var, var, factor, ALU.mult))
            dve.tensor_scalar(var, var, 1e-5, None, ALU.add).then_inc(var_ready, 1)
            dve.wait_ge(rstd_done, 1)
            ch(dve.reciprocal(rstd, rstd))
            if factor is not None:
                ch(dve.tensor_tensor(rstd, rstd, factor, ALU.mult))
            dve.scalar_tensor_tensor(tmp, mean, -1.0, rstd, ALU.mult, ALU.mult).then_inc(var_ready, 1)
            for g in range(NT // 8):
                dve.wait_ge(shifted, 8 * (g + 1))
                for t in range(8 * g, 8 * g + 8):
                    dve.scalar_tensor_tensor(xs[:, t, :], y[:, t, :], rstd[:, t:t + 1], xs[:, t, :],
                                             ALU.mult, ALU.add).then_inc(chain, 1)
                ch.n += 8
                group_end.append(ch.n)
                if out is None:
                    dve.wait_ge(chain, ch.n)
                    for t in range(8 * g, 8 * g + 8):
                        dve.bn_stats(st[:, t, :], xs[:, t, :]).then_inc(chain, 1)
                    ch.n += 8
            dve.wait_ge(chain, ch.n)

        @block.scalar
        def _(act):
            act.wait_ge(var_ready, 1)
            act.activation(rstd, var, ACT.Sqrt).then_inc(rstd_done, 1)
            act.wait_ge(var_ready, 2)
            for t in range(NT):
                act.activation(xs[:, t, :], xs[:, t, :], ACT.Identity, bias=tmp[:, t:t + 1], scale=1.0) \
                    .then_inc(shifted, 1)

        if out is not None:
            @block.sync
            def _(sp):
                for g, end in enumerate(group_end):
                    sp.wait_ge(chain, end)
                    sp.dma_start(out[:, 8 * g:8 * g + 8, :], xs[:, 8 * g:8 * g + 8, :]).then_inc(stored, 16)
                sp.wait_ge(stored, 16 * len(group_end))


def later_layers(nc, a, sem, xs, o_all, ident, identb, out):
    with ExitStack() as ctx:
        def sbt(name, shape, dt=F32, c=ctx):
            return c.enter_context(nc.sbuf_tensor(name, shape, dt))

        y = sbt("y", [P, NT, P])
        st = sbt("stats", [P, NT, 6])
        mean = sbt("mean2", [P, NT])[:]
        var = sbt("var2", [P, NT])[:]
        tmp = sbt("tmp2", [P, NT])[:]
        rstd = sbt("rstd2", [P, NT])[:]
        scale = sbt("scale2", [P, NT])[:]
        scalars = (mean, var, tmp, rstd)
        slot = sbt("slot", [P, 2, CT, P])
        xT = sbt("xT", [P, 2, CH])
        wo = sbt("wo_sb", [P, P])
        lng = sbt("lng", [P, 1])
        lnb = sbt("lnb", [P, 1])
        wg = sbt("wg", [P, EALL * P])
        wu = sbt("wu", [P, EALL * P])
        wd = sbt("wd", [P, EALL, P])
        gw = sbt("gw", [P, E])
        gbias = sbt("gbias", [P, E])
        esel = sbt("esel", [3 * E, EP * P], BF16)
        w_in = sem("wo_in")
        moe_in = sem("moe_in")
        esel_in = sem("esel_in")
        carried = sem("carried_later")

        n_g = NT * H
        grstd = sbt("grstd", [P, n_g])
        group = ExitStack()
        esel_f = sbt("esel_f", [3 * E, EP * P], F32, group)
        gsum = sbt("gsum", [P, n_g], F32, group)
        gvar = sbt("gvar", [P, n_g], F32, group)
        gsq = sbt("gsq", [P, n_g, DV], F32, group)
        g_chain, g_sq, g_var, g_rstd = sem("g_chain"), sem("g_sq"), sem("g_var"), sem("g_rstd")
        

        def bc(v, n, d):
            return v.rearrange("p (n a) -> p n a", a=1).to_broadcast([P, n, d])

        with nc.Block() as block:
            @block.sync
            def _(sp):
                sp.dma_start(wo[:], a["wo"]).then_inc(w_in, 16)
                sp.dma_start(lng[:], a["lng"]).then_inc(w_in, 16)
                sp.dma_start(lnb[:], a["lnb"]).then_inc(w_in, 16)
                sp.dma_start(wg[:], a["wg"]).then_inc(moe_in, 16)
                sp.dma_start(wu[:], a["wu"]).then_inc(moe_in, 16)
                sp.dma_start(wd[:], a["wd"]).then_inc(moe_in, 16)
                sp.dma_start(gw[:], a["gw"]).then_inc(moe_in, 16)
                sp.dma_start(gbias[:], a["gb"].partition_broadcast(P)).then_inc(moe_in, 16)
                sp.dma_start(esel_f[:], a["esel"]).then_inc(esel_in, 16)

            @block.vector
            def _(dve):
                ch = Chain(dve, g_chain)
                ch(dve.tensor_reduce(gsum[:], o_all[:], AX.X, ALU.add))
                ch(dve.tensor_scalar(gsum[:], gsum[:], 1.0 / DV, None, ALU.mult))
                ch(dve.tensor_tensor(o_all[:], o_all[:], bc(gsum[:], n_g, DV), ALU.subtract))
                dve.wait_ge(g_sq, 1)
                ch(dve.tensor_reduce(gvar[:], gsq[:], AX.X, ALU.add))
                dve.tensor_scalar(gvar[:], gvar[:], 1.0 / DV, 1e-5, ALU.mult, ALU.add).then_inc(g_var, 1)
                dve.wait_ge(esel_in, 16)
                ch(dve.tensor_copy(esel[:], esel_f[:]))
                dve.wait_ge(g_rstd, 1)
                ch(dve.reciprocal(grstd[:], grstd[:]))

            @block.scalar
            def _(act):
                act.wait_ge(g_chain, 3)
                act.activation(gsq[:], o_all[:], ACT.Square).then_inc(g_sq, 1)
                act.wait_ge(g_var, 1)
                act.activation(grstd[:], gvar[:], ACT.Sqrt).then_inc(g_rstd, 1)

        group.close()

        def slots(name, from_one=False):
            return [sem(f"{name}{s}", ONE if from_one else 0) for s in range(2)]

        with ExitStack() as pctx, nc.Block() as block:
            ps_t = [pctx.enter_context(nc.psum_tensor(f"p1_t{s}", [P, CH], F32)) for s in range(2)]
            ps_y = [pctx.enter_context(nc.psum_tensor(f"p1_y{s}", [P, CH], F32)) for s in range(2)]
            on_ready, t_ready, t_copied = slots("p1_on"), slots("p1_t", True), slots("p1_tc", True)
            y_ready, y_copied, stat = slots("p1_y", True), slots("p1_yc", True), sem("p1_stat")
            o_v = o_all[:].rearrange("p (b h q t) d -> p b h q t d", b=B, h=H, q=NQC)
            r_v = grstd[:].rearrange("p (b h q t a) -> p b h q t a", b=B, h=H, q=NQC, a=1)

            @block.sync
            def _(sp):
                sem.start(sp)

            @block.vector
            def _(dve):
                def front(c, s, used):
                    b, q = c // NQC, c % NQC
                    dve.wait_ge(t_ready[s], ONE + used)
                    for t in range(CT):
                        last = dve.tensor_tensor(
                            slot[:, s, t, :].rearrange("p (h d) -> p h d", h=H),
                            o_v[:, b, :, q, t, :], r_v[:, b, :, q, t, :].to_broadcast([P, H, DV]), ALU.mult)
                    last.then_inc(on_ready[s], 1)

                def back(c, s, used):
                    dve.wait_ge(y_copied[s], ONE + used + 1)
                    for t in range(CT):
                        dve.bn_stats(st[:, CT * c + t:CT * c + t + 1, :], y[:, CT * c + t:CT * c + t + 1, :]) \
                            .then_inc(stat, 1)

                for c in range(NC + 2):
                    if c < NC:
                        front(c, c % 2, c // 2)
                    if c >= 2:
                        back(c - 2, c % 2, (c - 2) // 2)
                dve.wait_ge(stat, NT)

            @block.tensor
            def _(pe):
                pe.wait_ge(w_in, 48)

                def front(c, s, used):
                    pe.wait_ge(on_ready[s], used + 1)
                    pe.wait_ge(t_copied[s], ONE + used)
                    for t in range(CT):
                        last = pe.transpose(ps_t[s][:, t * P:(t + 1) * P], slot[:, s, t, :], ident[:])
                    last.then_inc(t_ready[s], 1)

                def back(c, s, used):
                    pe.wait_ge(t_copied[s], ONE + used + 1)
                    pe.wait_ge(y_copied[s], ONE + used)
                    for t in range(CT):
                        last = pe.matmul(ps_y[s][:, t * P:(t + 1) * P], xT[:, s, t * P:(t + 1) * P], wo[:],
                                         start=True, stop=True)
                    last.then_inc(y_ready[s], 1)

                two_ahead(pe, front, back, NC)

            @block.scalar
            def _(act):
                act.wait_ge(w_in, 48)

                def front(c, s, used):
                    act.wait_ge(t_ready[s], ONE + used + 1)
                    act.wait_ge(y_ready[s], ONE + used)
                    act.activation(xT[:, s, :], ps_t[s][:], ACT.Identity, bias=lnb[:], scale=lng[:]) \
                        .then_inc(t_copied[s], 1)

                def back(c, s, used):
                    act.wait_ge(y_ready[s], ONE + used + 1)
                    act.sem_inc(carried, 1)
                    act.copy(y[:, bass.ds(CT * c, CT), :].rearrange("p t d -> p (t d)"), ps_y[s][:]) \
                        .then_inc(y_copied[s], 1)

                two_ahead(act, front, back, NC)

        add_normalised(nc, sem, "res1", xs, y, st, scalars)

        small = sem("l2_small")
        with ExitStack() as l2:
            def sb2(name, shape, dt=F32):
                return l2.enter_context(nc.sbuf_tensor(name, shape, dt))
            up = sb2("up", [P, FF])
            down = sb2("down", [P, KF, P])
            tern = sb2("tern", [P, FF])
            sgn = sb2("sgn", [P, FF])
            asum = sb2("asum", [P, 2])
            aall = sb2("aall", [P, 2])
            ones = sb2("ones", [P, 1])
            hid = sb2("hid", [P, 2, KF, CH])
            hsq = sb2("hsq", [P, KF, CH])
            hsum = sb2("hsum", [P, 2, CH])
            rms = sb2("rms", [P, NT])
            loaded, chain, asum_ready, aall_ready, sqrt_in, sqrt_out = (sem("l2_" + n) for n in (
                "loaded", "chain", "asum", "aall", "sqrt_in", "sqrt_out"))
            with nc.Block() as block:
                @block.sync
                def _(sp):
                    sp.dma_start(up[:], a["up"]).then_inc(loaded, 16)
                    sp.dma_start(down[:], a["down"]).then_inc(loaded, 16)

                @block.gpsimd
                def _(pool):
                    pool.memset(ones[:], 1.0)
                    pool.wait_ge(asum_ready, 1)
                    pool.partition_all_reduce(aall[:], asum[:], P, RADD).then_inc(aall_ready, 1)

                @block.scalar
                def _(act):
                    act.wait_ge(sqrt_in, 1)
                    act.activation(rstd, scale, ACT.Sqrt).then_inc(sqrt_out, 1)
                    act.wait_ge(small, 1)
                    act.activation(scale, tmp, ACT.Sqrt).then_inc(small, 1)

                @block.vector
                def _(dve):
                    ch = Chain(dve, chain)
                    mean_rstd(dve, ch, st, mean, var, tmp)
                    dve.tensor_scalar(scale, var, 1e-5, None, ALU.add).then_inc(sqrt_in, 1)
                    dve.wait_ge(loaded, 32)
                    flat_down = down[:].rearrange("p k n -> p (k n)")
                    for i, w in enumerate((up[:], flat_down)):
                        ch(dve.tensor_reduce(asum[:, i:i + 1], w, AX.X, ALU.add, apply_absolute_value=True))
                    dve.tensor_scalar(asum[:], asum[:], 0.5 / (P * FF), None, ALU.mult).then_inc(asum_ready, 1)
                    dve.wait_ge(aall_ready, 1)
                    ch(dve.tensor_scalar(asum[:], aall[:], -1.0, None, ALU.mult))
                    for i, w in enumerate((up[:], flat_down)):
                        ch(dve.tensor_scalar(tern[:], w, aall[:, i:i + 1], None, ALU.is_gt))
                        ch(dve.tensor_scalar(sgn[:], w, asum[:, i:i + 1], None, ALU.is_lt))
                        ch(dve.tensor_tensor(tern[:], tern[:], sgn[:], ALU.subtract))
                        ch(dve.tensor_tensor(tern[:], tern[:], w, ALU.subtract))
                        ch(dve.tensor_tensor(w, w, tern[:], ALU.add))
                    dve.wait_ge(sqrt_out, 1)
                    ch(dve.reciprocal(rstd, rstd))
                    ch(dve.tensor_tensor(tmp, rstd, rstd, ALU.mult))
                    dve.tensor_tensor(tmp, tmp, var, ALU.mult).then_inc(small, 1)
                    dve.wait_ge(small, 2)
                    ch(dve.tensor_scalar(scale, scale, 1e-8, None, ALU.add))
                    ch(dve.reciprocal(scale, scale))
                    ch(dve.tensor_tensor(scale, scale, rstd, ALU.mult))

            with ExitStack() as pctx, nc.Block() as block:
                ps_t = pctx.enter_context(nc.psum_tensor("p2_t", [P, CH], F32))
                ps_h = pctx.enter_context(nc.psum_tensor("p2_h", [P, KF, CH], F32))
                ps_y = pctx.enter_context(nc.psum_tensor("p2_y", [P, CH], F32))
                ps_r = pctx.enter_context(nc.psum_tensor("p2_r", [P, CH], F32))
                xn_ready, h_ready, sq_done = (slots("p2_" + n) for n in ("xn", "h", "sq"))
                t_ready, t_copied, h_done, sum_done, y_ready = (
                    slots("p2_" + n, True) for n in ("t", "tc", "hd", "sum", "y"))
                y_copied, stat, r_copied = sem("p2_yc", ONE), sem("p2_stat"), sem("p2_rc", ONE)

                @block.sync
                def _(sp):
                    sem.start(sp)

                @block.vector
                def _(dve):
                    def front(c, s, used):
                        dve.wait_ge(t_ready[s], ONE + used)
                        for t in range(CT):
                            i = CT * c + t
                            last = dve.tensor_scalar(slot[:, s, t, :], xs[:, bass.ds(i, 1), :].rearrange("p a d -> p (a d)"),
                                                     mean[:, bass.ds(i, 1)], scale[:, bass.ds(i, 1)],
                                                     ALU.subtract, ALU.mult)
                        last.then_inc(xn_ready[s], 1)

                    def back(c, s, used):
                        dve.wait_ge(sq_done[s], used + 1)
                        dve.wait_ge(y_ready[s], ONE + used)
                        dve.tensor_reduce(hsum[:, s, :], hsq[:].rearrange("p k n -> p n k"), AX.X, ALU.add) \
                            .then_inc(sum_done[s], 1)

                    def statistics(c, s, used):
                        dve.wait_ge(y_copied, ONE + c + 1)
                        dve.tensor_copy(rms[:, bass.ds(CT * c, CT)], ps_r[:, 0:CT]).then_inc(r_copied, 1)
                        for t in range(CT):
                            dve.bn_stats(st[:, bass.ds(CT * c + t, 1), :], y[:, bass.ds(CT * c + t, 1), :]) \
                                .then_inc(stat, 1)

                    two_ahead(dve, front, back, NC, statistics)
                    dve.wait_ge(stat, NT)

                @block.tensor
                def _(pe):
                    def front(c, s, used):
                        pe.wait_ge(xn_ready[s], used + 1)
                        pe.wait_ge(t_copied[1 - s], ONE + used + s)
                        for t in range(CT):
                            last = pe.transpose(ps_t[:, t * P:(t + 1) * P], slot[:, s, t, :], ident[:])
                        last.then_inc(t_ready[s], 1)
                        pe.wait_ge(t_copied[s], ONE + used + 1)
                        for k in range(KF):
                            pe.wait_ge(h_done[1 - s], ONE + (used + s) * KF)
                            pe.matmul(ps_h[:, k, :], up[:, k * P:(k + 1) * P], xT[:, s, :], start=True, stop=True) \
                                .then_inc(h_ready[s], 1)

                    def back(c, s, used):
                        pe.wait_ge(h_done[s], ONE + (used + 1) * KF)
                        pe.wait_ge(y_copied, ONE + c)
                        for t in range(CT):
                            for k in range(KF):
                                pe.matmul(ps_y[:, t * P:(t + 1) * P], hid[:, s, k, t * P:(t + 1) * P], down[:, k, :],
                                          start=(k == 0), stop=(k == KF - 1))
                        pe.wait_ge(sum_done[s], ONE + used + 1)
                        pe.wait_ge(r_copied, ONE + c)
                        for t in range(CT):
                            last = pe.matmul(ps_r[:, t:t + 1], hsum[:, s, t * P:(t + 1) * P], ones[:],
                                             start=True, stop=True)
                        last.then_inc(y_ready[s], 1)

                    two_ahead(pe, front, back, NC)

                @block.scalar
                def _(act):
                    def front(c, s, used):
                        act.wait_ge(t_ready[s], ONE + used + 1)
                        act.copy(xT[:, s, :], ps_t[:]).then_inc(t_copied[s], 1)
                        act.wait_ge(y_ready[s], ONE + used)
                        for k in range(KF):
                            act.wait_ge(h_ready[s], used * KF + k + 1)
                            act.activation(hid[:, s, k, :], ps_h[:, k, :], ACT.Gelu).then_inc(h_done[s], 1)
                        act.wait_ge(h_done[s], ONE + (used + 1) * KF)
                        act.wait_ge(sum_done[1 - s], ONE + used + s)
                        act.activation(hsq[:], hid[:, s, :, :], ACT.Square).then_inc(sq_done[s], 1)

                    def back(c, s, used):
                        act.wait_ge(y_ready[s], ONE + used + 1)
                        act.sem_inc(carried, 1)
                        act.copy(y[:, bass.ds(CT * c, CT), :].rearrange("p t d -> p (t d)"), ps_y[:]) \
                            .then_inc(y_copied, 1)

                    two_ahead(act, front, back, NC)

            q = sem("l2_q")
            with nc.Block() as block:
                @block.scalar
                def _(act):
                    act.wait_ge(q, 1)
                    act.activation(rms[:], rms[:], ACT.Sqrt).then_inc(q, 1)

                @block.vector
                def _(dve):
                    dve.tensor_scalar(rms[:], rms[:], 1.0 / FF, None, ALU.mult).then_inc(q, 1)
                    dve.wait_ge(q, 2)
                    ch = Chain(dve, q, 2)
                    ch(dve.tensor_scalar(rms[:], rms[:], 1e-8, None, ALU.add))
                    ch(dve.reciprocal(rms[:], rms[:]))
            add_normalised(nc, sem, "res2", xs, y, st, scalars, rms[:])
        third_layer(nc, a, sem, xs, y, o_all, st, scalars, scale, slot, xT, ident, slots, carried)
        add_normalised(nc, sem, "res3", xs, y, st, scalars)
        experts(nc, a, sem, xs, y, st, scalars, scale, slot, xT, ident, identb, slots,
                wg, wu, wd, gw, gbias, esel, moe_in, carried)
        add_normalised(nc, sem, "res4", xs, y, st, scalars, out=out)


def third_layer(nc, a, sem, xs, y, o_all, st, scalars, scale, slot, xT, ident, slots, carried):
    mean, var, tmp, rstd = scalars
    with ExitStack() as l3:
        def sb3(name, shape, dt=F32):
            return l3.enter_context(nc.sbuf_tensor(name, shape, dt))
        kw = sb3("kw", [P, KF, P])
        kT = sb3("kT", [P, NK3])
        qw = sb3("qw", [P, KF, P])
        bias3 = sb3("bias3", [P, P])
        w3 = sb3("w3", [P, P])
        b3 = sb3("b3", [P, P])
        kn = sb3("kn", [P, KF])
        ksq = sb3("ksq", [P, KF, P])
        zsq = o_all[:].rearrange("p g d -> p (g d)").rearrange("p (t n) -> p t n", n=P)
        zn = sb3("zn", [P, NT])
        loaded, kc, pc, kt_ready, zs, shift_ready, xn_ready, squares = (sem("l3_" + n) for n in (
            "loaded", "kc", "pc", "kt", "zs", "shift_ready", "xn", "squares"))

        def rows(v):
            return v[:].rearrange("p (a d) -> p a d", a=1).to_broadcast([P, 8, P])

        with ExitStack() as pctx, nc.Block() as block:
            ps_k = pctx.enter_context(nc.psum_tensor("p3_k", [P, NK3], F32))

            @block.sync
            def _(sp):
                sp.dma_start(kw[:], a["kw"]).then_inc(loaded, 16)
                sp.dma_start(qw[:], a["qw"]).then_inc(loaded, 16)
                for dst, n in ((bias3, "bias3"), (w3, "w3"), (b3, "b3")):
                    sp.dma_start(dst[:], a[n].partition_broadcast(P)).then_inc(loaded, 16)

            @block.vector
            def _(dve):
                ch = Chain(dve, kc)
                dve.wait_ge(loaded, 80)
                ch(dve.tensor_tensor(ksq[:], kw[:], kw[:], ALU.mult))
                ch(dve.tensor_reduce(kn[:], ksq[:], AX.X, ALU.add))
                dve.tensor_scalar(kn[:], kn[:], 1e-24, None, ALU.max).then_inc(pc, 1)
                dve.wait_ge(pc, 2)
                ch(dve.reciprocal(kn[:], kn[:]))
                ch(dve.tensor_tensor(kw[:], kw[:], kn[:].rearrange("p (k a) -> p k a", a=1).to_broadcast([P, KF, P]),
                                     ALU.mult))
                mean_rstd(dve, ch, st, mean, var, tmp)
                dve.tensor_scalar(scale, var, 1e-5, None, ALU.add).then_inc(pc, 1)
                dve.wait_ge(pc, 4)
                ch(dve.reciprocal(rstd, rstd))
                ch(dve.tensor_tensor(tmp, rstd, rstd, ALU.mult))
                ch(dve.tensor_tensor(tmp, tmp, var, ALU.mult))
                dve.tensor_scalar(tmp, tmp, 1e-12, None, ALU.add).then_inc(pc, 1)
                dve.wait_ge(pc, 6)
                ch(dve.reciprocal(tmp, tmp))
                ch(dve.tensor_tensor(scale, rstd, tmp, ALU.mult))
                dve.scalar_tensor_tensor(tmp, mean, -1.0, scale, ALU.mult, ALU.mult).then_inc(shift_ready, 1)
                for g in range(NT // 8):
                    part = y[:, 8 * g:8 * g + 8, :]
                    dve.wait_ge(xn_ready, 8 * (g + 1))
                    ch(dve.tensor_tensor(part, part, rows(w3), ALU.mult))
                    dve.tensor_tensor(part, part, rows(b3), ALU.add).then_inc(zs, 1)
                    if g:
                        dve.wait_ge(squares, g)
                        ch(dve.tensor_reduce(zn[:, 8 * g - 8:8 * g], zsq[:, 8 * g - 8:8 * g, :], AX.X, ALU.add))
                dve.wait_ge(squares, NT // 8)
                ch(dve.tensor_reduce(zn[:, NT - 8:NT], zsq[:, NT - 8:NT, :], AX.X, ALU.add))
                dve.tensor_scalar(zn[:], zn[:], 1e-24, None, ALU.max).then_inc(pc, 1)
                dve.wait_ge(pc, 8)
                ch(dve.reciprocal(zn[:], zn[:]))

            @block.scalar
            def _(act):
                def squared(g):
                    act.wait_ge(zs, g + 1)
                    act.activation(zsq[:, 8 * g:8 * g + 8, :], y[:, 8 * g:8 * g + 8, :], ACT.Square) \
                        .then_inc(squares, 1)

                for i, (n, root) in enumerate(((kn[:], kn[:]), (scale, rstd), (tmp, tmp))):
                    act.wait_ge(pc, 2 * i + 1)
                    act.activation(root, n, ACT.Sqrt).then_inc(pc, 1)
                act.wait_ge(kt_ready, 1)
                act.copy(kT[:], ps_k[:]).then_inc(kt_ready, 1)
                act.wait_ge(shift_ready, 1)
                for t in range(NT):
                    act.activation(y[:, t, :], xs[:, t, :], ACT.Identity, bias=tmp[:, t:t + 1],
                                   scale=scale[:, t:t + 1]).then_inc(xn_ready, 1)
                    if t % 8 == 7 and t > 8:
                        squared(t // 8 - 1)
                squared(NT // 8 - 1)
                act.wait_ge(pc, 7)
                act.activation(zn[:], zn[:], ACT.Sqrt).then_inc(pc, 1)

            @block.tensor
            def _(pe):
                pe.wait_ge(kc, 4)
                for k in range(KF):
                    last = pe.transpose(ps_k[:, k * P:(k + 1) * P], kw[:, k, :], ident[:])
                last.then_inc(kt_ready, 1)

        d_all = sb3("d_all", [P, NC, KF * CH])
        s_sb = sb3("s_sb", [P, 2, KF * CH])
        ln_p = sb3("ln_p", [P, 2, KF * CH])
        with ExitStack() as pctx, nc.Block() as block:
            ps_t = pctx.enter_context(nc.psum_tensor("p3_t", [P, CH], F32))
            ps_s = pctx.enter_context(nc.psum_tensor("p3_s", [P, KF, CH], F32))
            q_ready, t_ready, t_copied = slots("p3_q"), slots("p3_t", True), slots("p3_tc", True)
            s_ready, d_done = slots("p3_s"), slots("p3_d", True)
            clipped = [sem(f"p3_clip{k}", ONE) for k in range(KF)]
            lns = sem("p3_ln")
            ln_m_done = slots("p3_lnm")

            @block.sync
            def _(sp):
                sem.start(sp)

            @block.vector
            def _(dve):
                def first(c, s, used):
                    dve.wait_ge(t_ready[s], ONE + used)
                    for t in range(CT):
                        i = CT * c + t
                        last = dve.tensor_scalar(slot[:, s, t, :], y[:, bass.ds(i, 1), :].rearrange("p a d -> p (a d)"),
                                                 zn[:, bass.ds(i, 1)], None, ALU.mult)
                    last.then_inc(q_ready[s], 1)

                def second(c, s, used):
                    dve.wait_ge(d_done[s], ONE + used)
                    for k in range(KF):
                        dve.wait_ge(s_ready[s], KF * used + k + 1)
                        dve.tensor_scalar(s_sb[:, s, k * CH:(k + 1) * CH], ps_s[:, k, :], 1.0 - 1e-6, -1.0 + 1e-6,
                                          ALU.min, ALU.max).then_inc(clipped[k], 1)

                def third(c, s, used):
                    dve.wait_ge(ln_m_done[s], used + 1)
                    dve.tensor_tensor(d_all[:, bass.ds(c, 1), :].rearrange("p a n -> p (a n)"), ln_p[:, s, :],
                                      s_sb[:, s, :], ALU.subtract).then_inc(d_done[s], 1)

                two_ahead(dve, first, second, NC, third)

            @block.tensor
            def _(pe):
                def front(c, s, used):
                    pe.wait_ge(q_ready[s], used + 1)
                    pe.wait_ge(t_copied[1 - s], ONE + used + s)
                    for t in range(CT):
                        last = pe.transpose(ps_t[:, t * P:(t + 1) * P], slot[:, s, t, :], ident[:])
                    last.then_inc(t_ready[s], 1)

                def back(c, s, used):
                    pe.wait_ge(t_copied[s], ONE + used + 1)
                    for k in range(KF):
                        pe.wait_ge(clipped[k], ONE + c)
                        pe.matmul(ps_s[:, k, :], kT[:, k * P:(k + 1) * P], xT[:, s, :], start=True, stop=True) \
                            .then_inc(s_ready[s], 1)

                two_ahead(pe, front, back, NC)

            @block.scalar
            def _(act):
                def front(c, s, used):
                    act.wait_ge(t_ready[s], ONE + used + 1)
                    act.copy(xT[:, s, :], ps_t[:]).then_inc(t_copied[s], 1)

                def back(c, s, used):
                    for k in range(KF):
                        act.wait_ge(clipped[k], ONE + c + 1)
                    act.wait_ge(d_done[s], ONE + used)
                    act.activation(ln_p[:, s, :], s_sb[:, s, :], ACT.Ln, bias=1.0, scale=1.0).then_inc(lns, 1)
                    act.wait_ge(lns, c + 1)
                    act.activation(s_sb[:, s, :], s_sb[:, s, :], ACT.Ln, bias=1.0, scale=-1.0) \
                        .then_inc(ln_m_done[s], 1)

                two_ahead(act, front, back, NC)

        w_2, pw = ln_p, s_sb
        with ExitStack() as pctx, nc.Block() as block:
            ps_x = [pctx.enter_context(nc.psum_tensor(f"p3_x{s}", [P, CH], F32)) for s in range(2)]
            w2_done, w4_done, w8_done = (slots("p3c_" + n) for n in ("w2", "w4", "w8"))
            pw_done, x_ready, x_copied = (slots("p3c_" + n, True) for n in ("pw", "x", "xc"))
            ac = sem("p3c_ac")
            stat = sem("p3c_stat")
            half_b = sb3("half_b", [P, 1])
            hb = sem("p3_half")

            @block.sync
            def _(sp):
                sem.start(sp)

            @block.gpsimd
            def _(pool):
                pool.memset(half_b[:], 0.5).then_inc(hb, 1)

            @block.scalar
            def _(act):
                act.wait_ge(hb, 1)
                for c in range(NC):
                    act.activation(d_all[:, c, :], d_all[:, c, :], ACT.Tanh, scale=0.25).then_inc(ac, 1)
                act.wait_ge(ac, NC)

                def first(c, s, used):
                    at = d_all[:, bass.ds(c, 1), :].rearrange("p a n -> p (a n)")
                    act.activation(at, at, ACT.Arctan).then_inc(ac, 1)
                    act.wait_ge(ac, NC + c + 1)
                    act.sem_inc(carried, 1)
                    act.activation(w_2[:, s, :], at, ACT.Square, bias=half_b[:], scale=TWO_OVER_PI) \
                        .then_inc(w2_done[s], 1)

                def second(c, s, used):
                    act.wait_ge(w4_done[s], used + 1)
                    act.wait_ge(x_ready[s], ONE + used)
                    act.activation(pw[:, s, :], w_2[:, s, :], ACT.Square, scale=TWO_OVER_PI ** 0.5) \
                        .then_inc(w8_done[s], 1)

                pipelined(act, first, second, NC, 0)

            @block.vector
            def _(dve):
                def first(c, s, used):
                    dve.wait_ge(w2_done[s], used + 1)
                    dve.tensor_tensor(w_2[:, s, :], w_2[:, s, :], w_2[:, s, :], ALU.mult).then_inc(w4_done[s], 1)

                def second(c, s, used):
                    dve.wait_ge(w8_done[s], used + 1)
                    dve.scalar_tensor_tensor(pw[:, s, :], d_all[:, bass.ds(c, 1), :].rearrange("p a n -> p (a n)"),
                                             0.7853981633974483, pw[:, s, :], ALU.add, ALU.mult) \
                        .then_inc(pw_done[s], 1)

                def third(c, s, used):
                    dve.wait_ge(x_ready[s], ONE + used + 1)
                    dve.sem_inc(carried, 1)
                    dve.tensor_copy(y[:, bass.ds(CT * c, CT), :].rearrange("p t d -> p (t d)"), ps_x[s][:]) \
                        .then_inc(x_copied[s], 1)
                    dve.wait_ge(x_copied[s], ONE + used + 1)
                    for t in range(CT):
                        dve.bn_stats(st[:, bass.ds(CT * c, CT), :][:, t:t + 1, :],
                                     y[:, bass.ds(CT * c, CT), :][:, t:t + 1, :]).then_inc(stat, 1)

                pipelined3(dve, first, second, third, NC)
                dve.wait_ge(stat, NT)

            @block.tensor
            def _(pe):
                with pe.Fori(0, NC // 2) as k:
                    for s in range(2):
                        pe.wait_ge(pw_done[s], ONE + k + 1)
                        pe.wait_ge(x_copied[s], ONE + k)
                        for t in range(CT):
                            for j in range(KF):
                                last = pe.matmul(ps_x[s][:, t * P:(t + 1) * P], pw[:, s, j * CH + t * P:j * CH + (t + 1) * P],
                                                 qw[:, j, :], start=(j == 0), stop=(j == KF - 1))
                        last.then_inc(x_ready[s], 1)

        xc, xp = sem("l3_xc"), sem("l3_xp")
        with nc.Block() as block:
            @block.scalar
            def _(act):
                act.wait_ge(xp, 1)
                act.activation(zn[:], zn[:], ACT.Sqrt).then_inc(xp, 1)

            @block.vector
            def _(dve):
                ch = Chain(dve, xc)
                mean_rstd(dve, ch, st, mean, var, tmp)
                ch(dve.tensor_tensor(tmp, mean, mean, ALU.mult))
                ch(dve.tensor_tensor(zn[:], var, tmp, ALU.add))
                dve.tensor_scalar(zn[:], zn[:], float(P), 1e-24, ALU.mult, ALU.max).then_inc(xp, 1)
                dve.wait_ge(xp, 2)
                ch(dve.reciprocal(zn[:], zn[:]))
                for t in range(NT):
                    dve.scalar_tensor_tensor(y[:, t, :], y[:, t, :], zn[:, t:t + 1], bias3[:], ALU.mult, ALU.add) \
                        .then_inc(xc, 1)
                ch.n += NT
                dve.wait_ge(xc, ch.n)
                for t in range(NT):
                    dve.bn_stats(st[:, t, :], y[:, t, :]).then_inc(xc, 1)
                ch.n += NT
                dve.wait_ge(xc, ch.n)


def experts(nc, a, sem, xs, y, st, scalars, scale, slot, xT, ident, identb, slots,
            wg, wu, wd, gw, gbias, esel, moe_in, carried):
    mean, var, tmp, rstd = scalars
    NG, TOPK, BIG = 4, 8, 3.0e38
    EG = E // NG
    with ExitStack() as l4:
        def sb4(name, shape, dt=F32):
            return l4.enter_context(nc.sbuf_tensor(name, shape, dt))
        x_h = sb4("x_h", [P, 2, B * N], F16)
        wg_h = sb4("wg_h", [P, 2, EALL * P], F16)
        wu_h = sb4("wu_h", [P, 2, EALL * P], F16)
        wd_h = sb4("wd_h", [P, 2, EALL * P], F16)
        wmax = sb4("wmax", [P, 3])
        wmax_all = sb4("wmax_all", [P, 3])
        w_scale = sb4("w_scale", [P, 3])
        g_scale = sb4("g_scale", [P, 1])
        h_scale = sb4("h_scale", [P, 1])
        f_scale = sb4("f_scale", [P, 1])
        sc = sb4("sc", [P, NT, E])
        cho = sb4("cho", [P, NT, E])
        work = sb4("work", [P, NT, E])
        eq = sb4("eq", [P, NT, E])
        m1 = sb4("m1", [P, NT * NG])
        m2 = sb4("m2", [P, NT * NG])
        cnt = sb4("cnt", [P, NT * NG])
        rank = sb4("rank", [P, NT, NG])
        cmp = sb4("cmp", [P, NT, NG])
        top8 = sb4("top8", [P, NT, TOPK])
        wsum = sb4("wsum", [P, NT])
        wparts = sb4("wparts", [P, NT, 3, E], BF16)
        wT = sb4("wT", [3 * E, B * N], BF16)
        silu = sb4("silu", [P, 2, CH])
        prod = sb4("prod", [P, 2, CH])
        hT = sb4("hT", [P, 2, CH])
        hh = sb4("hh", [P, 2, CH], F16)
        hl = sb4("hl", [P, 2, CH], F16)
        fT = sb4("fT", [P, CH])
        pc, chain, max_ready, scale_ready, w_high = (sem("l4_" + n) for n in (
            "pc", "chain", "max", "scale", "w_high"))
        with nc.Block() as block:
            @block.scalar
            def _(act):
                act.wait_ge(pc, 1)
                act.activation(rstd, scale, ACT.Sqrt).then_inc(pc, 1)
                act.wait_ge(scale_ready, 1)
                for i, (w, w_h) in enumerate(((wg[:], wg_h), (wu[:], wu_h),
                                              (wd[:].rearrange("p e d -> p (e d)"), wd_h))):
                    act.activation(w_h[:, 0, :], w, ACT.Copy, scale=w_scale[:, i:i + 1]).then_inc(w_high, 1)

            @block.gpsimd
            def _(pool):
                pool.wait_ge(max_ready, 1)
                pool.partition_all_reduce(wmax_all[:], wmax[:], P, RMAX).then_inc(max_ready, 1)

            @block.vector
            def _(dve):
                ch = Chain(dve, chain)
                mean_rstd(dve, ch, st, mean, var, tmp)
                dve.tensor_scalar(scale, var, 1e-5, None, ALU.add).then_inc(pc, 1)
                dve.wait_ge(moe_in, 16 * 5)
                wd_flat = wd[:].rearrange("p e d -> p (e d)")
                for i, w in enumerate((wg[:], wu[:], wd_flat)):
                    ch(dve.tensor_reduce(wmax[:, i:i + 1], w, AX.X, ALU.max, apply_absolute_value=True))
                dve.tensor_scalar(wmax[:], wmax[:], 1e-12, 1e12, ALU.max, ALU.min).then_inc(max_ready, 1)
                dve.wait_ge(max_ready, 2)
                ch(dve.tensor_scalar(wmax[:].bitcast(I32), wmax_all[:].bitcast(I32), 0x7F800000, None,
                                     ALU.bitwise_and))
                ch(dve.reciprocal(w_scale[:], wmax[:]))
                ch(dve.tensor_scalar(h_scale[:], w_scale[:, 0:1], 0.25 / (X_SCALE * W_SCALE), None, ALU.mult))
                ch(dve.tensor_scalar(g_scale[:], wmax[:, 0:1], 1.0 / (X_SCALE * W_SCALE), None, ALU.mult))
                ch(dve.tensor_tensor(f_scale[:], wmax[:, 0:1], wmax[:, 1:2], ALU.mult))
                ch(dve.tensor_scalar(f_scale[:], f_scale[:], 4.0 / W_SCALE, None, ALU.mult))
                ch(dve.tensor_tensor(f_scale[:], f_scale[:], wmax[:, 2:3], ALU.mult))
                dve.tensor_scalar(w_scale[:], w_scale[:], W_SCALE, None, ALU.mult).then_inc(scale_ready, 1)
                for i, (w, w_h) in enumerate(((wg[:], wg_h), (wu[:], wu_h), (wd_flat, wd_h))):
                    dve.wait_ge(w_high, i + 1)
                    ch(dve.scalar_tensor_tensor(w_h[:, 1, :], w, w_scale[:, i:i + 1], w_h[:, 0, :],
                                                ALU.mult, ALU.subtract))
                dve.wait_ge(pc, 2)
                ch(dve.reciprocal(rstd, rstd))

        with ExitStack() as pctx, nc.Block() as block:
            ps_t = [pctx.enter_context(nc.psum_tensor(f"p4_t{s}", [P, CH], F32)) for s in range(2)]
            ps_l = [pctx.enter_context(nc.psum_tensor(f"p4_l{s}", [P, CH], F32)) for s in range(2)]
            xn_ready, x_high = slots("p4_xn"), slots("p4_high")
            t_ready, t_copied, l_ready, x_split = (slots("p4_" + n, True) for n in ("t", "tc", "l", "split"))
            sig_done = sem("p4_sig")

            @block.sync
            def _(sp):
                sem.start(sp)

            @block.vector
            def _(dve):
                def front(c, s, used):
                    dve.wait_ge(t_ready[s], ONE + used)
                    for t in range(CT):
                        i = CT * c + t
                        last = dve.tensor_scalar(slot[:, s, t, :], xs[:, bass.ds(i, 1), :].rearrange("p a d -> p (a d)"),
                                                 mean[:, bass.ds(i, 1)], rstd[:, bass.ds(i, 1)],
                                                 ALU.subtract, ALU.mult)
                    last.then_inc(xn_ready[s], 1)

                def back(c, s, used):
                    dve.wait_ge(x_high[s], used + 1)
                    dve.scalar_tensor_tensor(x_h[:, 1:2, bass.ds(c * CH, CH)].rearrange("p a n -> p (a n)"),
                                             xT[:, s, :], X_SCALE,
                                             x_h[:, 0:1, bass.ds(c * CH, CH)].rearrange("p a n -> p (a n)"),
                                             ALU.mult, ALU.subtract).then_inc(x_split[s], 1)

                two_ahead(dve, front, back, NC)

            @block.tensor
            def _(pe):
                def front(c, s, used):
                    pe.wait_ge(xn_ready[s], used + 1)
                    pe.wait_ge(t_copied[s], ONE + used)
                    for t in range(CT):
                        last = pe.transpose(ps_t[s][:, t * P:(t + 1) * P], slot[:, s, t, :], ident[:])
                    last.then_inc(t_ready[s], 1)

                def back(c, s, used):
                    pe.wait_ge(t_copied[s], ONE + used + 1)
                    for t in range(CT):
                        last = pe.matmul(ps_l[s][:, t * E:(t + 1) * E], xT[:, s, t * P:(t + 1) * P], gw[:],
                                         start=True, stop=True)
                    last.then_inc(l_ready[s], 1)

                two_ahead(pe, front, back, NC)

            @block.scalar
            def _(act):
                def front(c, s, used):
                    act.wait_ge(t_ready[s], ONE + used + 1)
                    act.wait_ge(l_ready[s], ONE + used)
                    act.wait_ge(x_split[s], ONE + used)
                    act.copy(xT[:, s, :], ps_t[s][:]).then_inc(t_copied[s], 1)
                    act.wait_ge(t_copied[s], ONE + used + 1)
                    act.sem_inc(carried, 1)
                    act.activation(x_h[:, 0:1, bass.ds(c * CH, CH)].rearrange("p a n -> p (a n)"), xT[:, s, :],
                                   ACT.Copy, scale=X_SCALE).then_inc(x_high[s], 1)

                def back(c, s, used):
                    act.wait_ge(l_ready[s], ONE + used + 1)
                    act.sem_inc(carried, 1)
                    act.activation(sc[:, bass.ds(CT * c, CT), :].rearrange("p t e -> p (t e)"),
                                   ps_l[s][:, 0:CT * E], ACT.Sigmoid).then_inc(sig_done, 1)

                two_ahead(act, front, back, NC)

        with ExitStack() as pctx, nc.Block() as block:
            ps_w = [pctx.enter_context(nc.psum_tensor(f"p4_w{s}", [P, 1024], BF16)) for s in range(2)]
            wp_ready, w_ready, w_copied = sem("p4_wp"), sem("p4_w"), sem("p4_wc")
            rc = sem("p4_rc")

            @block.vector
            def _(dve):
                ch = Chain(dve, rc)

                def g3(v):
                    return v[:].rearrange("p t (g e) -> p (t g) e", g=NG)

                def gb3(v):
                    return v[:].rearrange("p (n a) -> p n a", a=1).to_broadcast([P, NT * NG, EG])

                ch(dve.tensor_tensor(cho[:], sc[:],
                                     gbias[:].rearrange("p (a e) -> p a e", a=1).to_broadcast([P, NT, E]), ALU.add))
                ch(dve.tensor_reduce(m1[:], g3(cho), AX.X, ALU.max))
                ch(dve.tensor_tensor(g3(eq), g3(cho), gb3(m1), ALU.is_equal))
                ch(dve.tensor_reduce(cnt[:], g3(eq), AX.X, ALU.add))
                ch(dve.scalar_tensor_tensor(work[:], eq[:], -BIG, cho[:], ALU.mult, ALU.add))
                ch(dve.tensor_reduce(m2[:], g3(work), AX.X, ALU.max))
                ch(dve.tensor_scalar(cnt[:], cnt[:], 1.5, None, ALU.is_gt))
                ch(dve.copy_predicated(m2[:], cnt[:].bitcast(I32), m1[:]))
                ch(dve.tensor_tensor(m1[:], m1[:], m2[:], ALU.add))
                gs = m1[:].rearrange("p (t g) -> p t g", g=NG)
                ch(dve.memset(rank[:], 0.0))
                for j in range(NG):
                    other = gs[:, :, j:j + 1]
                    if j + 1 < NG:
                        ch(dve.tensor_tensor(cmp[:, :, j + 1:NG], other.to_broadcast([P, NT, NG - j - 1]),
                                             gs[:, :, j + 1:NG], ALU.is_ge))
                    if j:
                        ch(dve.tensor_tensor(cmp[:, :, 0:j], other.to_broadcast([P, NT, j]), gs[:, :, 0:j], ALU.is_gt))
                    ch(dve.memset(cmp[:, :, j:j + 1], 0.0))
                    ch(dve.tensor_tensor(rank[:], rank[:], cmp[:], ALU.add))
                ch(dve.tensor_scalar(rank[:], rank[:], 1.5, None, ALU.is_lt))
                ch(dve.tensor_tensor(g3(work), g3(cho),
                                     rank[:].rearrange("p t (g a) -> p (t g) a", a=1).to_broadcast([P, NT * NG, EG]),
                                     ALU.mult))
                for t in range(NT):
                    dve.max(top8[:, t, :], work[:, t, :]).then_inc(rc, 1)
                ch.n += NT
                dve.wait_ge(rc, ch.n)
                for t in range(NT):
                    dve.match_replace(eq[:, t, :], top8[:, t, :], work[:, t, :], BIG).then_inc(rc, 1)
                ch.n += NT
                dve.wait_ge(rc, ch.n)
                ch(dve.tensor_scalar(eq[:], eq[:], BIG, None, ALU.is_ge))
                ch(dve.tensor_tensor(sc[:], sc[:], eq[:], ALU.mult))
                ch(dve.tensor_reduce(wsum[:], sc[:], AX.X, ALU.add))
                ch(dve.tensor_scalar(wsum[:], wsum[:], 1e-20, None, ALU.add))
                ch(dve.reciprocal(wsum[:], wsum[:]))
                ch(dve.tensor_scalar(wsum[:], wsum[:], 2.5, None, ALU.mult))
                ch(dve.tensor_tensor(sc[:], sc[:], wsum[:].rearrange("p (t a) -> p t a", a=1)
                                     .to_broadcast([P, NT, E]), ALU.mult))
                ch(dve.tensor_copy(wparts[:, :, 0, :], sc[:]))
                ch(dve.tensor_tensor(sc[:], sc[:], wparts[:, :, 0, :], ALU.subtract))
                ch(dve.tensor_copy(wparts[:, :, 1, :], sc[:]))
                dve.tensor_tensor(wparts[:, :, 2, :], sc[:], wparts[:, :, 1, :], ALU.subtract).then_inc(wp_ready, 1)

            @block.tensor
            def _(pe):
                pe.wait_ge(wp_ready, 1)
                for t in range(NT):
                    g = t // 8
                    if t % 8 == 0 and g >= 2:
                        pe.wait_ge(w_copied, g - 1)
                    pe.transpose(ps_w[g % 2][0:3 * E, (t % 8) * P:(t % 8 + 1) * P],
                                 wparts[:, t, :, :].rearrange("p j e -> p (j e)"), identb[:]).then_inc(w_ready, 1)

            @block.scalar
            def _(act):
                for g in range(NT // 8):
                    act.wait_ge(w_ready, 8 * (g + 1))
                    act.copy(wT[:, g * 1024:(g + 1) * 1024], ps_w[g % 2][0:3 * E, :]).then_inc(w_copied, 1)

        with ExitStack() as pctx, nc.Block() as block:
            def pt(name):
                return [pctx.enter_context(nc.psum_tensor(f"{name}{s}", [P, CH], F32)) for s in range(2)]
            ps_g, ps_u, ps_w = pt("p5_g"), pt("p5_u"), pt("p5_w")
            ps_f = pctx.enter_context(nc.psum_tensor("p5_f", [P, CH], F32))
            ps_t = pctx.enter_context(nc.psum_tensor("p5_t", [P, CH], F32))
            g_ready, u_ready, w_ready, high_done, low_done = (
                slots("p5_" + n) for n in ("g", "u", "w", "high", "low"))
            silu_done, prod_done, h_done, down_done = (
                slots("p5_" + n, True) for n in ("silu", "prod", "h", "down"))
            f_copied, ft_ready, ft_copied = (sem("p5_" + n, ONE) for n in ("fc", "ft", "ftc"))
            stat = sem("p5_stat")
            USES = (EALL - EALL // 2, EALL // 2)

            def uses(c, e):
                return e % 2, c * USES[e % 2] + e // 2

            def w_uses(c, e):
                return c * (EP // 2) + e // 2

            @block.sync
            def _(sp):
                sem.start(sp)

            @block.tensor
            def _(pe):
                def product(out, w_h, e, high, low, start=True, stop=True):
                    w = slice(e * P, (e + 1) * P)
                    pe.matmul(out, w_h[:, 0, w], high, start=start, stop=False)
                    pe.matmul(out, w_h[:, 0, w], low, start=False, stop=False)
                    return pe.matmul(out, w_h[:, 1, w], high, start=False, stop=stop)

                def down(c, e):
                    s, n = uses(c, e)
                    pe.wait_ge(low_done[s], n + 1)
                    product(ps_f[:], wd_h, e, hh[:, s, :], hl[:, s, :], start=(e == 0), stop=(e == EP)) \
                        .then_inc(down_done[s], 1)

                with pe.Fori(0, NC) as c:
                    high, low = (x_h[:, i:i + 1, bass.ds(c * CH, CH)].rearrange("p a n -> p (a n)")
                                 for i in range(2))
                    for e in range(EALL):
                        s, n = uses(c, e)
                        pe.wait_ge(silu_done[s], ONE + n)
                        product(ps_g[s][:], wg_h, e, high, low).then_inc(g_ready[s], 1)
                        pe.wait_ge(prod_done[s], ONE + n)
                        product(ps_u[s][:], wu_h, e, high, low).then_inc(u_ready[s], 1)
                        if e < EP:
                            pe.wait_ge(h_done[s], ONE + n)
                            pe.matmul(ps_w[s][:], esel[:, e * P:(e + 1) * P], wT[:, bass.ds(c * CH, CH)],
                                      start=True, stop=True).then_inc(w_ready[s], 1)
                        if e == 2:
                            pe.wait_ge(f_copied, ONE + c)
                        if e >= 2:
                            down(c, e - 2)
                    down(c, EP - 1)
                    down(c, EP)
                    pe.wait_ge(f_copied, ONE + c + 1)
                    pe.wait_ge(ft_copied, ONE + c)
                    for t in range(CT):
                        last = pe.transpose(ps_t[:, t * P:(t + 1) * P], fT[:, t * P:(t + 1) * P], ident[:])
                    last.then_inc(ft_ready, 1)

            @block.scalar
            def _(act):
                def high(c, e):
                    s, n = uses(c, e)
                    act.wait_ge(h_done[s], ONE + n + 1)
                    act.wait_ge(down_done[s], ONE + n)
                    act.copy(hh[:, s, :], hT[:, s, :]).then_inc(high_done[s], 1)

                with act.Fori(0, NC) as c:
                    for e in range(EALL):
                        s, n = uses(c, e)
                        act.wait_ge(g_ready[s], n + 1)
                        act.wait_ge(prod_done[s], ONE + n)
                        act.activation(silu[:, s, :], ps_g[s][:], ACT.Silu, scale=g_scale[:]) \
                            .then_inc(silu_done[s], 1)
                        if e >= 1:
                            high(c, e - 1)
                    high(c, EP)
                    s, n = uses(c, EP)
                    act.wait_ge(down_done[s], ONE + n + 1)
                    act.wait_ge(ft_ready, ONE + c)
                    act.activation(fT[:], ps_f[:], ACT.Copy, scale=f_scale[:]).then_inc(f_copied, 1)
                    act.wait_ge(ft_ready, ONE + c + 1)
                    act.sem_inc(carried, 1)
                    act.copy(y[:, bass.ds(CT * c, CT), :].rearrange("p t d -> p (t d)"), ps_t[:]) \
                        .then_inc(ft_copied, 1)

            @block.vector
            def _(dve):
                def low(c, e):
                    s, n = uses(c, e)
                    dve.wait_ge(high_done[s], n + 1)
                    dve.tensor_tensor(hl[:, s, :], hT[:, s, :], hh[:, s, :], ALU.subtract).then_inc(low_done[s], 1)

                with dve.Fori(0, NC) as c:
                    for e in range(EALL):
                        s, n = uses(c, e)
                        dve.wait_ge(silu_done[s], ONE + n + 1)
                        dve.wait_ge(u_ready[s], n + 1)
                        dve.tensor_tensor(prod[:, s, :], ps_u[s][:], silu[:, s, :], ALU.mult) \
                            .then_inc(prod_done[s], 1)
                        if e >= 1:
                            low(c, e - 1)
                        dve.wait_ge(prod_done[s], ONE + n + 1)
                        if e < EP:
                            dve.wait_ge(w_ready[s], w_uses(c, e) + 1)
                            dve.scalar_tensor_tensor(hT[:, s, :], ps_w[s][:], h_scale[:], prod[:, s, :],
                                                     ALU.mult, ALU.mult).then_inc(h_done[s], 1)
                        else:
                            dve.tensor_scalar(hT[:, s, :], prod[:, s, :], h_scale[:], None, ALU.mult) \
                                .then_inc(h_done[s], 1)
                    low(c, EP)
                    dve.wait_ge(ft_copied, ONE + c + 1)
                    for t in range(CT):
                        dve.bn_stats(st[:, bass.ds(CT * c, CT), :][:, t:t + 1, :],
                                     y[:, bass.ds(CT * c, CT), :][:, t:t + 1, :]).then_inc(stat, 1)
                dve.wait_ge(stat, NT)


def program(nc, a, out):
    with ExitStack() as ctx:
        def sb(name, shape, dt):
            return ctx.enter_context(nc.sbuf_tensor(name, shape, dt))

        xs = sb("xs", [P, NT, P], F32)
        o_all = sb("o_all", [P, B * H * NQC * CT, DV], F32)
        ident = sb("ident_sb", [P, P], F32)
        identb = sb("identb", [P, P], BF16)
        with Semaphores(nc) as sem:
            attention_layer(nc, a, sem, xs, o_all, ident, identb)
        with Semaphores(nc) as sem:
            later_layers(nc, a, sem, xs, o_all, ident, identb, out)


def kernel(**inputs):
    import numpy as np
    import concourse.bacc as bacc
    from concourse.bass_utils import run_bass_kernel_spmd

    f = {k: np.asarray(v) for k, v in inputs.items()}
    sel = np.zeros((P, DV + 1), np.float32)
    for base in (0, VC):
        for r in range(3 * DV):
            sel[base + r, r % DV] = 1
        sel[base + 3 * DV, DV] = 1
    esel = np.zeros((3 * E, EP * P), np.float32)
    for r in range(3 * E):
        esel[r, (r % E) * (P // 2):(r % E + 1) * (P // 2)] = 1
    tiles = lambda w: np.ascontiguousarray(w.reshape(-1, P, w.shape[-1]).transpose(1, 0, 2))
    arrays = {
        "x": f["L0_attn_x"].reshape(B * N, P),
        "wqkv": np.concatenate([f["L0_attn_Wq"], f["L0_attn_Wk"], f["L0_attn_Wv"]], 1),
        "sel": sel, "ident": np.eye(P, dtype=np.float32),
        "lqk": np.stack([f["L0_attn_" + k] for k in ("lq1", "lk1", "lq2", "lk2")]),
        "wo": f["L0_attn_Wo"],
        "lng": np.tile(f["L0_attn_ln_g"], H)[:, None], "lnb": np.tile(f["L0_attn_ln_b"], H)[:, None],
        "up": f["L0_ffn_w_up"].T, "down": tiles(f["L0_ffn_w_down"].T),
        "kw": tiles(f["L1_attn_k_weight"]), "qw": tiles(f["L1_attn_q_weight"]),
        "bias3": f["L1_attn_bias"], "w3": f["L1_attn_ln_weight"], "b3": f["L1_attn_ln_bias"],
        "gw": f["L1_ffn_gate_w"].T, "gb": f["L1_ffn_gate_bias"], "esel": esel,
        "wg": np.concatenate([f["L1_ffn_expert_gate"].reshape(-1, P), f["L1_ffn_shared_gate"]]).T,
        "wu": np.concatenate([f["L1_ffn_expert_up"].reshape(-1, P), f["L1_ffn_shared_up"]]).T,
        "wd": tiles(np.concatenate([f["L1_ffn_expert_down"].transpose(0, 2, 1).reshape(-1, P),
                                    f["L1_ffn_shared_down"].T])),
    }
    arrays = {k: np.ascontiguousarray(v) for k, v in arrays.items()}
    nc = bacc.Bacc("TRN2", target_bir_lowering=False, num_devices=1)
    a = {k: nc.dram_tensor("in_" + k, v.shape, F32, kind="ExternalInput").ap() for k, v in arrays.items()}
    a["x"] = a["x"].rearrange("(t p) d -> p t d", p=P)
    out = nc.dram_tensor("out", (B * N, P), F32, kind="ExternalOutput").ap()
    program(nc, a, out.rearrange("(t p) d -> p t d", p=P))
    r = run_bass_kernel_spmd(nc, [{"in_" + k: v for k, v in arrays.items()}], core_ids=[0])
    return r.results[0]["out"].reshape(B, N, P)
```
